# Optimizing a Trainium2 kernel written in Bass

```python
import numpy as np
import jax
import jax.numpy as jnp

def _softmax(x, axis=-1):
    return jax.nn.softmax(x, axis=axis)

def _gelu(x):
    return jax.nn.gelu(x, approximate=True)

def _silu(x):
    return jax.nn.silu(x)

def _sigmoid(x):
    return jax.nn.sigmoid(x)

def _layernorm(x, axis=-1, eps=1e-05):
    m = jnp.mean(x, axis=axis, keepdims=True)
    v = jnp.var(x, axis=axis, keepdims=True)
    return (x - m) / jnp.sqrt(v + eps)

def _scatter_add(tgt, idx, src, axis=0):
    return tgt.at[idx].add(src)

def _segment_sum(src, seg, n):
    return jax.ops.segment_sum(src, seg, n)
kernel_name = 'mk_recurrent_d2_jaxref_r4_eca0f2'

def setup_inputs(seed: int=0):
    np.random.seed(seed)
    _w = jnp.asarray

    def _L0_attn_setup():
        import jax, jax.numpy as jnp
        import numpy as np
        from jax import lax
        B, T, H = (4, 256, 256)
        NH, KD, VD = (4, 128, 256)
        DK, DV = (KD // NH, VD // NH)
        R, R5, G = (32, 160, 64)
        EPS = 1e-05

        def _forward(h, x_proj_mu, xl_w1, xl_w2, xl_b2, x_out_w, x_bias, r_w, w_w1, w_w2, w_b, k_w, v_w, g_w, bonus, gn_weight, gn_bias, o_w):
            B_, T_, H_ = h.shape
            shifted = jnp.pad(h, ((0, 0), (1, 0), (0, 0)))[:, :T_]
            delta = shifted - h
            x_lerp = h + delta * x_proj_mu
            x0 = jnp.tanh(x_lerp @ xl_w1.T) @ xl_w2.T + xl_b2
            x1 = jnp.tanh(x0).reshape(B_, T_, 5, R)
            x2 = jnp.einsum('btnr,hnr->btnh', x1, x_out_w.reshape(H_, 5, R))
            mus = x2 + x_bias
            r_mu, w_mu, k_mu, v_mu, g_mu = (mus[:, :, i] for i in range(5))
            r = (h + delta * r_mu) @ r_w.T
            w_in = h + delta * w_mu
            w = jnp.tanh(w_in @ w_w1.T) @ w_w2.T + w_b
            k = (h + delta * k_mu) @ k_w.T
            v = (h + delta * v_mu) @ v_w.T
            g = (h + delta * g_mu) @ g_w.T
            r = r.reshape(B_, T_, NH, DK)
            k = k.reshape(B_, T_, NH, DK)
            v = v.reshape(B_, T_, NH, DV)
            wd = jnp.exp(-jnp.exp(w.reshape(B_, T_, NH, DK)))

            def step(S, xs):
                r_t, k_t, v_t, w_t = xs
                o_t = jnp.einsum('bhk,bhkv->bhv', r_t, S) + jnp.sum(r_t * bonus * k_t, -1, keepdims=True) * v_t
                S = S * w_t[..., None] + k_t[..., None] * v_t[..., None, :]
                return (S, o_t)
            xs = tuple((jnp.swapaxes(a, 0, 1) for a in (r, k, v, wd)))
            S0 = jnp.zeros((B_, NH, DK, DV), jnp.float32)
            _, oT = lax.scan(step, S0, xs)
            o = jnp.swapaxes(oT, 0, 1)
            mean = o.mean(-1, keepdims=True)
            var = o.var(-1, keepdims=True)
            o = ((o - mean) * lax.rsqrt(var + EPS)).reshape(B_, T_, VD)
            o = (o * gn_weight + gn_bias) * jax.nn.silu(g)
            return o @ o_w.T
        key = jax.random.key(seed)
        ks = jax.random.split(key, 20)
        n = lambda k, s, sc=0.02: jax.random.normal(k, s, dtype=jnp.float32) * sc
        return {'hidden_states': jax.random.normal(ks[0], (B, T, H), dtype=jnp.float32), 'x_proj_mu': n(ks[1], (H,), 0.1), 'xl_w1': n(ks[2], (R, H)), 'xl_w2': n(ks[3], (R5, R)), 'xl_b2': jnp.zeros((R5,), jnp.float32), 'x_out_w': n(ks[4], (H, R5)), 'x_bias': n(ks[5], (5, H), 0.1), 'r_w': n(ks[6], (KD, H)), 'w_w1': n(ks[7], (G, H)), 'w_w2': n(ks[8], (KD, G)), 'w_b': n(ks[9], (KD,), 0.1), 'k_w': n(ks[10], (KD, H)), 'v_w': n(ks[11], (VD, H)), 'g_w': n(ks[12], (VD, H)), 'bonus': n(ks[13], (NH, DK), 0.1), 'gn_weight': jnp.ones((VD,), jnp.float32), 'gn_bias': jnp.zeros((VD,), jnp.float32), 'o_w': n(ks[14], (H, VD))}
    _L0_attn_in = _L0_attn_setup()

    def _L0_ffn_setup():
        import jax, jax.numpy as jnp
        import numpy as np
        DIM = 256
        NUM_EXPERTS = 8
        HIDDEN = 1024
        CAP_FACTOR = 2.0
        B, S = (4, 512)
        key = jax.random.key(seed)
        ks = jax.random.split(key, 6)
        scale_r = 1.0 / np.sqrt(DIM)
        scale_1 = 1.0 / np.sqrt(DIM)
        scale_2 = 1.0 / np.sqrt(HIDDEN)
        return {'x': jax.random.normal(ks[0], (B, S, DIM), dtype=jnp.float32), 'router_w': jax.random.uniform(ks[1], (NUM_EXPERTS, DIM), jnp.float32, -scale_r, scale_r), 'w1': jax.random.uniform(ks[2], (NUM_EXPERTS, DIM, HIDDEN), jnp.float32, -scale_1, scale_1), 'b1': jax.random.uniform(ks[3], (NUM_EXPERTS, HIDDEN), jnp.float32, -scale_1, scale_1), 'w2': jax.random.uniform(ks[4], (NUM_EXPERTS, HIDDEN, DIM), jnp.float32, -scale_2, scale_2), 'b2': jax.random.uniform(ks[5], (NUM_EXPERTS, DIM), jnp.float32, -scale_2, scale_2)}
    _L0_ffn_in = _L0_ffn_setup()

    def _L1_attn_setup():
        import jax, jax.numpy as jnp
        import numpy as np
        import math
        P = 64
        H = 256
        B = 8
        L = 1024
        R_MIN, R_MAX, THETA_MAX = (0.9, 0.999, math.pi)

        def _map_theta_to_A(thetas, G_diag, steps):
            cos_t = jnp.cos(thetas)
            tan_sq = jnp.tan(thetas) ** 2
            sqrt_term = 4.0 * jnp.sqrt(steps ** 4 / cos_t ** 2 + steps ** 5 * G_diag / cos_t ** 2)
            common = steps ** 2 * (-4.0 - 2.0 * steps * G_diag - 4.0 * tan_sq - 2.0 * steps * G_diag * tan_sq)
            denom = 2.0 * steps ** 4 * (1.0 + tan_sq)
            A_plus = (sqrt_term - common) / denom
            A_minus = (-sqrt_term - common) / denom
            return jnp.where(thetas > math.pi / 2, A_plus, A_minus)

        def _binary_operator(q_i, q_j):
            A_i, b_i = q_i
            A_j, b_j = q_j
            iA, iB, iC, iD = jnp.split(A_i, 4, axis=-1)
            jA, jB, jC, jD = jnp.split(A_j, 4, axis=-1)
            A_new = jnp.concatenate([jA * iA + jB * iC, jA * iB + jB * iD, jC * iA + jD * iC, jC * iB + jD * iD], axis=-1)
            b_i1, b_i2 = jnp.split(b_i, 2, axis=-2)
            new_b1 = jA[..., None] * b_i1 + jB[..., None] * b_i2
            new_b2 = jC[..., None] * b_i1 + jD[..., None] * b_i2
            return (A_new, jnp.concatenate([new_b1, new_b2], axis=-2) + b_j)

        def _forward(x, steps_raw, G_raw, A_raw, B_mat, C_mat, D_vec):
            steps = jax.nn.sigmoid(steps_raw)
            G_diag = jax.nn.relu(G_raw)
            A_diag = jax.nn.relu(A_raw)
            Bu = jnp.einsum('blh,pht->blpt', x, B_mat)
            S = 1.0 + steps * G_diag
            alpha = steps ** 2 * A_diag / S
            alpha = 1.99 * jnp.tanh(alpha / 1.99)
            M = jnp.concatenate([1.0 / S, -alpha / steps, steps / S, 1.0 - alpha])
            M_exp = jnp.broadcast_to(M, (x.shape[0], x.shape[1], 4 * steps.shape[0]))
            step_b = steps[None, None, :, None]
            S_b = S[None, None, :, None]
            F1 = step_b * (1.0 / S_b) * Bu
            F2 = step_b ** 2 * (1.0 / S_b) * Bu
            F_mat = jnp.concatenate([F1, F2], axis=-2)
            _, xs = jax.lax.associative_scan(_binary_operator, (M_exp, F_mat), axis=1)
            ys = xs[..., steps.shape[0]:, :]
            Cy = jnp.einsum('blpt,hpt->blht', ys, C_mat)
            return Cy[..., 0] - Cy[..., 1] + x * D_vec
        key = jax.random.key(seed)
        k1, k2, k3, k4, k5, k6, k7 = jax.random.split(key, 7)
        x = jax.random.normal(k1, (B, L, H), dtype=jnp.float32)
        steps_raw = 0.5 * jax.random.normal(k2, (P,), dtype=jnp.float32)
        steps = jax.nn.sigmoid(steps_raw)
        mags = jnp.sqrt(jax.random.uniform(k3, (P,)) * (R_MAX ** 2 - R_MIN ** 2) + R_MIN ** 2)
        G_raw = (1.0 - mags ** 2) / (steps * mags ** 2)
        theta = jax.random.uniform(k4, (P,)) * THETA_MAX
        A_raw = _map_theta_to_A(theta, jax.nn.relu(G_raw), steps)
        std_b = 1.0 / math.sqrt(H)
        B_mat = jax.random.uniform(k5, (P, H, 2), minval=-std_b, maxval=std_b, dtype=jnp.float32)
        std_c = 1.0 / math.sqrt(P)
        C_mat = jax.random.uniform(k6, (H, P, 2), minval=-std_c, maxval=std_c, dtype=jnp.float32)
        D_vec = jax.random.normal(k7, (H,), dtype=jnp.float32)
        return {'input_sequence': x, 'steps_raw': steps_raw, 'G_raw': G_raw, 'A_raw': A_raw, 'B_mat': B_mat, 'C_mat': C_mat, 'D_vec': D_vec}
    _L1_attn_in = _L1_attn_setup()

    def _L1_ffn_setup():
        import jax, jax.numpy as jnp
        import numpy as np
        D_MODEL = 256
        D_FF = 704
        N_EXPERTS = 8
        key = jax.random.key(seed)
        k_in, k1, k2, k3 = jax.random.split(key, 4)
        scale = 0.02
        inputs = jax.random.normal(k_in, (4, N_EXPERTS * 512, D_MODEL), dtype=jnp.float32)
        w1 = jax.random.normal(k1, (N_EXPERTS, D_MODEL, D_FF), dtype=jnp.float32) * scale
        w3 = jax.random.normal(k3, (N_EXPERTS, D_MODEL, D_FF), dtype=jnp.float32) * scale
        w2 = jax.random.normal(k2, (N_EXPERTS, D_FF, D_MODEL), dtype=jnp.float32) * scale
        return {'inputs': inputs, 'w1': w1, 'w3': w3, 'w2': w2}
    _L1_ffn_in = _L1_ffn_setup()
    _d = {'L0_attn_hidden_states': _L0_attn_in['hidden_states'], 'L0_attn_x_proj_mu': _L0_attn_in['x_proj_mu'], 'L0_attn_xl_w1': _L0_attn_in['xl_w1'], 'L0_attn_xl_w2': _L0_attn_in['xl_w2'], 'L0_attn_xl_b2': _L0_attn_in['xl_b2'], 'L0_attn_x_out_w': _L0_attn_in['x_out_w'], 'L0_attn_x_bias': _L0_attn_in['x_bias'], 'L0_attn_r_w': _L0_attn_in['r_w'], 'L0_attn_w_w1': _L0_attn_in['w_w1'], 'L0_attn_w_w2': _L0_attn_in['w_w2'], 'L0_attn_w_b': _L0_attn_in['w_b'], 'L0_attn_k_w': _L0_attn_in['k_w'], 'L0_attn_v_w': _L0_attn_in['v_w'], 'L0_attn_g_w': _L0_attn_in['g_w'], 'L0_attn_bonus': _L0_attn_in['bonus'], 'L0_attn_gn_weight': _L0_attn_in['gn_weight'], 'L0_attn_gn_bias': _L0_attn_in['gn_bias'], 'L0_attn_o_w': _L0_attn_in['o_w'], 'L0_ffn_router_w': _L0_ffn_in['router_w'], 'L0_ffn_w1': _L0_ffn_in['w1'], 'L0_ffn_b1': _L0_ffn_in['b1'], 'L0_ffn_w2': _L0_ffn_in['w2'], 'L0_ffn_b2': _L0_ffn_in['b2'], 'L1_attn_steps_raw': _L1_attn_in['steps_raw'], 'L1_attn_G_raw': _L1_attn_in['G_raw'], 'L1_attn_A_raw': _L1_attn_in['A_raw'], 'L1_attn_B_mat': _L1_attn_in['B_mat'], 'L1_attn_C_mat': _L1_attn_in['C_mat'], 'L1_attn_D_vec': _L1_attn_in['D_vec'], 'L1_ffn_w1': _L1_ffn_in['w1'], 'L1_ffn_w3': _L1_ffn_in['w3'], 'L1_ffn_w2': _L1_ffn_in['w2']}
    _x0 = _d['L0_attn_hidden_states']
    _d['L0_attn_hidden_states'] = jax.random.normal(jax.random.fold_in(jax.random.key(seed), 1), (16, 1024, 256), dtype=_x0.dtype)
    del _x0
    return _d

def reference(L0_attn_hidden_states, L0_attn_x_proj_mu, L0_attn_xl_w1, L0_attn_xl_w2, L0_attn_xl_b2, L0_attn_x_out_w, L0_attn_x_bias, L0_attn_r_w, L0_attn_w_w1, L0_attn_w_w2, L0_attn_w_b, L0_attn_k_w, L0_attn_v_w, L0_attn_g_w, L0_attn_bonus, L0_attn_gn_weight, L0_attn_gn_bias, L0_attn_o_w, L0_ffn_router_w, L0_ffn_w1, L0_ffn_b1, L0_ffn_w2, L0_ffn_b2, L1_attn_steps_raw, L1_attn_G_raw, L1_attn_A_raw, L1_attn_B_mat, L1_attn_C_mat, L1_attn_D_vec, L1_ffn_w1, L1_ffn_w3, L1_ffn_w2):

    def _L0_attn_ref(hidden_states, x_proj_mu, xl_w1, xl_w2, xl_b2, x_out_w, x_bias, r_w, w_w1, w_w2, w_b, k_w, v_w, g_w, bonus, gn_weight, gn_bias, o_w):
        import jax, jax.numpy as jnp
        import numpy as np
        from jax import lax
        B, T, H = (4, 256, 256)
        NH, KD, VD = (4, 128, 256)
        DK, DV = (KD // NH, VD // NH)
        R, R5, G = (32, 160, 64)
        EPS = 1e-05

        def _forward(h, x_proj_mu, xl_w1, xl_w2, xl_b2, x_out_w, x_bias, r_w, w_w1, w_w2, w_b, k_w, v_w, g_w, bonus, gn_weight, gn_bias, o_w):
            B_, T_, H_ = h.shape
            shifted = jnp.pad(h, ((0, 0), (1, 0), (0, 0)))[:, :T_]
            delta = shifted - h
            x_lerp = h + delta * x_proj_mu
            x0 = jnp.tanh(x_lerp @ xl_w1.T) @ xl_w2.T + xl_b2
            x1 = jnp.tanh(x0).reshape(B_, T_, 5, R)
            x2 = jnp.einsum('btnr,hnr->btnh', x1, x_out_w.reshape(H_, 5, R))
            mus = x2 + x_bias
            r_mu, w_mu, k_mu, v_mu, g_mu = (mus[:, :, i] for i in range(5))
            r = (h + delta * r_mu) @ r_w.T
            w_in = h + delta * w_mu
            w = jnp.tanh(w_in @ w_w1.T) @ w_w2.T + w_b
            k = (h + delta * k_mu) @ k_w.T
            v = (h + delta * v_mu) @ v_w.T
            g = (h + delta * g_mu) @ g_w.T
            r = r.reshape(B_, T_, NH, DK)
            k = k.reshape(B_, T_, NH, DK)
            v = v.reshape(B_, T_, NH, DV)
            wd = jnp.exp(-jnp.exp(w.reshape(B_, T_, NH, DK)))

            def step(S, xs):
                r_t, k_t, v_t, w_t = xs
                o_t = jnp.einsum('bhk,bhkv->bhv', r_t, S) + jnp.sum(r_t * bonus * k_t, -1, keepdims=True) * v_t
                S = S * w_t[..., None] + k_t[..., None] * v_t[..., None, :]
                return (S, o_t)
            xs = tuple((jnp.swapaxes(a, 0, 1) for a in (r, k, v, wd)))
            S0 = jnp.zeros((B_, NH, DK, DV), jnp.float32)
            _, oT = lax.scan(step, S0, xs)
            o = jnp.swapaxes(oT, 0, 1)
            mean = o.mean(-1, keepdims=True)
            var = o.var(-1, keepdims=True)
            o = ((o - mean) * lax.rsqrt(var + EPS)).reshape(B_, T_, VD)
            o = (o * gn_weight + gn_bias) * jax.nn.silu(g)
            return o @ o_w.T
        return _forward(hidden_states, x_proj_mu, xl_w1, xl_w2, xl_b2, x_out_w, x_bias, r_w, w_w1, w_w2, w_b, k_w, v_w, g_w, bonus, gn_weight, gn_bias, o_w)

    def _L0_ffn_ref(x, router_w, w1, b1, w2, b2):
        import jax, jax.numpy as jnp
        import numpy as np
        DIM = 256
        NUM_EXPERTS = 8
        HIDDEN = 1024
        CAP_FACTOR = 2.0
        B, S = (4, 512)
        Bz, Sz, Dz = x.shape
        E = router_w.shape[0]
        capacity = max(1, int(Sz * CAP_FACTOR / E) + 1)
        scores = jax.nn.softmax(jnp.einsum('bsd,ed->bse', x, router_w), axis=-1)
        scores_t = jnp.swapaxes(scores, 1, 2)
        gate_vals, sel_idx = jax.lax.top_k(scores_t, capacity)
        b_idx = jnp.arange(Bz)[:, None, None]
        tokens = x[b_idx, sel_idx]
        h = jnp.einsum('becd,edh->bech', tokens, w1) + b1[None, :, None, :]
        h = jax.nn.gelu(h, approximate=False)
        y = jnp.einsum('bech,ehd->becd', h, w2) + b2[None, :, None, :]
        gated = y * gate_vals[..., None]
        out = jnp.zeros_like(x).at[b_idx, sel_idx].add(gated)
        return out

    def _L1_attn_ref(input_sequence, steps_raw, G_raw, A_raw, B_mat, C_mat, D_vec):
        import jax, jax.numpy as jnp
        import numpy as np
        import math
        P = 64
        H = 256
        B = 8
        L = 1024
        R_MIN, R_MAX, THETA_MAX = (0.9, 0.999, math.pi)

        def _map_theta_to_A(thetas, G_diag, steps):
            cos_t = jnp.cos(thetas)
            tan_sq = jnp.tan(thetas) ** 2
            sqrt_term = 4.0 * jnp.sqrt(steps ** 4 / cos_t ** 2 + steps ** 5 * G_diag / cos_t ** 2)
            common = steps ** 2 * (-4.0 - 2.0 * steps * G_diag - 4.0 * tan_sq - 2.0 * steps * G_diag * tan_sq)
            denom = 2.0 * steps ** 4 * (1.0 + tan_sq)
            A_plus = (sqrt_term - common) / denom
            A_minus = (-sqrt_term - common) / denom
            return jnp.where(thetas > math.pi / 2, A_plus, A_minus)

        def _binary_operator(q_i, q_j):
            A_i, b_i = q_i
            A_j, b_j = q_j
            iA, iB, iC, iD = jnp.split(A_i, 4, axis=-1)
            jA, jB, jC, jD = jnp.split(A_j, 4, axis=-1)
            A_new = jnp.concatenate([jA * iA + jB * iC, jA * iB + jB * iD, jC * iA + jD * iC, jC * iB + jD * iD], axis=-1)
            b_i1, b_i2 = jnp.split(b_i, 2, axis=-2)
            new_b1 = jA[..., None] * b_i1 + jB[..., None] * b_i2
            new_b2 = jC[..., None] * b_i1 + jD[..., None] * b_i2
            return (A_new, jnp.concatenate([new_b1, new_b2], axis=-2) + b_j)

        def _forward(x, steps_raw, G_raw, A_raw, B_mat, C_mat, D_vec):
            steps = jax.nn.sigmoid(steps_raw)
            G_diag = jax.nn.relu(G_raw)
            A_diag = jax.nn.relu(A_raw)
            Bu = jnp.einsum('blh,pht->blpt', x, B_mat)
            S = 1.0 + steps * G_diag
            alpha = steps ** 2 * A_diag / S
            alpha = 1.99 * jnp.tanh(alpha / 1.99)
            M = jnp.concatenate([1.0 / S, -alpha / steps, steps / S, 1.0 - alpha])
            M_exp = jnp.broadcast_to(M, (x.shape[0], x.shape[1], 4 * steps.shape[0]))
            step_b = steps[None, None, :, None]
            S_b = S[None, None, :, None]
            F1 = step_b * (1.0 / S_b) * Bu
            F2 = step_b ** 2 * (1.0 / S_b) * Bu
            F_mat = jnp.concatenate([F1, F2], axis=-2)
            _, xs = jax.lax.associative_scan(_binary_operator, (M_exp, F_mat), axis=1)
            ys = xs[..., steps.shape[0]:, :]
            Cy = jnp.einsum('blpt,hpt->blht', ys, C_mat)
            return Cy[..., 0] - Cy[..., 1] + x * D_vec
        return _forward(input_sequence, steps_raw, G_raw, A_raw, B_mat, C_mat, D_vec)

    def _L1_ffn_ref(inputs, w1, w3, w2):
        import jax, jax.numpy as jnp
        import numpy as np
        D_MODEL = 256
        D_FF = 704
        N_EXPERTS = 8
        B, T, D = inputs.shape
        E = w1.shape[0]
        C = T // E
        x = inputs.reshape(B, E, C, D)
        gate = jnp.einsum('becd,edf->becf', x, w1)
        up = jnp.einsum('becd,edf->becf', x, w3)
        h = jax.nn.silu(gate) * up
        out = jnp.einsum('becf,efd->becd', h, w2)
        return out.reshape(B, T, D)
    x = L0_attn_hidden_states
    xn = _layernorm(x, axis=-1)
    s = _L0_attn_ref(xn, L0_attn_x_proj_mu, L0_attn_xl_w1, L0_attn_xl_w2, L0_attn_xl_b2, L0_attn_x_out_w, L0_attn_x_bias, L0_attn_r_w, L0_attn_w_w1, L0_attn_w_w2, L0_attn_w_b, L0_attn_k_w, L0_attn_v_w, L0_attn_g_w, L0_attn_bonus, L0_attn_gn_weight, L0_attn_gn_bias, L0_attn_o_w)
    g = _silu(_L0_ffn_ref(xn, L0_ffn_router_w, L0_ffn_w1, L0_ffn_b1, L0_ffn_w2, L0_ffn_b2))
    x = x + s * g
    xn = _layernorm(x, axis=-1)
    s = _L1_attn_ref(xn, L1_attn_steps_raw, L1_attn_G_raw, L1_attn_A_raw, L1_attn_B_mat, L1_attn_C_mat, L1_attn_D_vec)
    g = _silu(_L1_ffn_ref(xn, L1_ffn_w1, L1_ffn_w3, L1_ffn_w2))
    x = x + s * g
    return x

_drawn_inputs = setup_inputs


def setup_inputs(seed=0):
    import zlib

    import numpy as np

    out = dict(_drawn_inputs(seed))
    spreads = {'L0_attn_xl_b2': (0.0, 0.8),
     'L0_attn_gn_weight': (1.0, 0.6),
     'L0_attn_gn_bias': (0.0, 0.8)}
    factors = {'L0_attn_x_proj_mu': 8.0,
     'L0_attn_xl_w1': 8.0,
     'L0_attn_xl_w2': 8.0,
     'L0_attn_x_out_w': 8.0,
     'L0_attn_x_bias': 8.0,
     'L0_attn_r_w': 8.0,
     'L0_attn_w_w1': 8.0,
     'L0_attn_w_w2': 8.0,
     'L0_attn_w_b': 8.0,
     'L0_attn_k_w': 8.0,
     'L0_attn_v_w': 8.0,
     'L0_attn_g_w': 8.0,
     'L0_attn_bonus': 8.0,
     'L0_attn_o_w': 8.0,
     'L0_ffn_router_w': 8.0,
     'L0_ffn_w1': 8.0,
     'L0_ffn_b1': 8.0,
     'L0_ffn_w2': 8.0,
     'L0_ffn_b2': 8.0,
     'L1_attn_steps_raw': 7.487,
     'L1_attn_G_raw': 4.529,
     'L1_attn_A_raw': 2.76,
     'L1_attn_B_mat': 3.918,
     'L1_attn_C_mat': 4.004,
     'L1_attn_D_vec': 3.871,
     'L1_ffn_w1': 2.781,
     'L1_ffn_w3': 2.751,
     'L1_ffn_w2': 2.749}
    for name, (base, spread) in spreads.items():
        noise = np.random.default_rng([zlib.crc32(name.encode()), seed]).standard_normal(out[name].shape)
        drawn = base * np.exp(spread * noise) if base else spread * noise
        out[name] = jnp.asarray(drawn.astype(out[name].dtype))
    for name, factor in factors.items():
        out[name] = (out[name] * factor).astype(out[name].dtype)
    return out
```

```python
from contextlib import ExitStack

import concourse.bass as bass
from concourse import mybir

ALU = mybir.AluOpType
ACT = mybir.ActivationFunctionType
F32 = mybir.dt.float32
F32R = mybir.dt.float32r
U32 = mybir.dt.uint32
I32 = mybir.dt.int32
AX_X = mybir.AxisListType.X

P = 128
B, T, D = 16, 1024, 256
N = B * T
KD = D // P
GT = 4
GN = GT * P
NG = N // GN
HALVES = T // GN
EPS = 1e-5

NH, KW, VW = 4, 128, 256
DK, DV = KW // NH, VW // NH
NMU, RANK, GATE = 5, 32, 64
LEVELS = 7

NE, HID = 8, 1024
HC = HID // P
CAP = T * 2 // NE + 1
ROUNDS = (CAP + 7) // 8
QN = B // 2

PS = 64
FF = 704
FC = (FF + P - 1) // P
BLK = 32
NBLK = T // BLK


def width(m):
    return min(P, FF - m * P)


class Order:

    def __init__(self, eng, sem, base=0):
        self.eng, self.sem, self.base, self.n = eng, sem, base, 0

    def did(self, ins):
        self.n += 1
        ins.then_inc(self.sem, 1)

    def wait(self):
        self.eng.wait_ge(self.sem, self.base + self.n)

    def hold(self, spare):
        self.wait()
        self.eng.sem_inc(spare, 1)

    def link(self, ins):
        self.did(ins)
        self.wait()


def phase_semaphores(nc, mem):
    taken = []

    def give_back():
        nc.all_engine_barrier()
        nc.clear_and_free_semaphores(taken)
        nc.all_engine_barrier()

    def sem(name):
        taken.append(nc.alloc_semaphore(name=name))
        return taken[-1]

    mem.callback(give_back)
    return sem


def route_phase(nc, ctx, ps, x, xn_d, xnT_d, acc_d, left_d, router_w, ident, idxT, gateT, idxL, gateL):
    with ExitStack() as mem:
        def sb(name, shape, dt=F32):
            return mem.enter_context(nc.sbuf_tensor(name, shape, dt))

        sem = phase_semaphores(nc, mem)

        xg = [sb(f"r_x{r}", [P, GT, D]) for r in range(2)]
        xn = [sb(f"r_xn{r}", [P, GT, D]) for r in range(2)]
        xT = [sb(f"r_xT{r}", [P, KD, GN]) for r in range(2)]
        stats = sb("r_stats", [P, GT, 6])
        mv = sb("r_mv", [P, GT, 2])
        vare = sb("r_vare", [P, GT])
        power = sb("r_power", [P, GT])
        rstd = sb("r_rstd", [P, GT])
        wr = sb("r_wr", [P, KD, NE])
        zeros = sb("r_zeros", [P, 2048])
        logit = sb("r_logit", [P, N // P, NE])
        prob = sb("r_prob", [P, T // P, NE, B])
        red = sb("r_red", [P, N // P])
        score = [sb(f"r_score{r}", [P, T]) for r in range(1)]
        v8 = sb("r_v8", [P, 8])
        i8 = sb("r_i8", [P, 8], U32)
        vals = sb("r_vals", [P, ROUNDS * 8])
        idxf = sb("r_idxf", [P, ROUNDS * 8])
        rowi = sb("r_rowi", [P, 1], I32)
        rowb = sb("r_rowb", [P, 1], I32)
        rowf = sb("r_rowf", [P, 1])
        leftf = sb("r_leftf", [B, NE])

        x_in = [sem(f"r_x_in{r}") for r in range(2)]
        x_free = sem("r_x_free")
        xn_out = [sem(f"r_xn_out{r}") for r in range(2)]
        xT_out = [sem(f"r_xT_out{r}") for r in range(2)]
        normed = sem("r_normed")
        turned = sem("r_turned")
        xT_sb = sem("r_xT_sb")
        routed = sem("r_routed")
        logit_sb = sem("r_logit_sb")
        w_in = sem("r_w_in")
        zeroed = sem("r_zeroed")
        acc_out = sem("r_acc_out")
        iota_done = sem("r_iota_done")
        dve_o = sem("r_dve_o")
        top_o = sem("r_top_o")
        centred = sem("r_centred")
        exped = sem("r_exped")
        soft = sem("r_soft")
        score_t = sem("r_score_t")
        topped = sem("r_topped")
        idx_t = sem("r_idx_t")
        left_out = sem("r_left_out")
        left_in = sem("r_left_in")
        idx_done = sem("r_idx_done")
        spare = sem("r_spare")
        var_ready = sem("r_var_ready")
        rstd_ready = sem("r_rstd_ready")

        x_v = x.rearrange("(g t p) d -> p (g t) d", t=GT, p=P)
        xn_v = xn_d.rearrange("(g t p) d -> p (g t) d", t=GT, p=P)
        xT_v = xnT_d.rearrange("k p n -> p k n")
        acc_v = acc_d.rearrange("(a p c) d -> a p (c d)", p=P, c=8)

        block = mem.enter_context(nc.Block())

        @block.sync
        def _(sp):
            sp.dma_start(wr[:], router_w).then_inc(w_in, 16)
            with sp.Fori(0, NG // 2) as i:
                for r in range(2):
                    sp.wait_ge(x_free, 2 * i + r + 1)
                    sp.dma_start(xg[r][:], x_v[:, bass.ds(GT * (2 * i + r), GT), :]).then_inc(x_in[r], 16)
            sp.wait_ge(topped, 1)
            sp.dma_start(left_d[0:1, :].rearrange("o p -> p o"), idxf[:, CAP - 1:CAP]).then_inc(left_out, 16)
            sp.dma_start(left_d[1:2, :].rearrange("o p -> p o"), vals[:, CAP - 1:CAP]).then_inc(left_out, 16)
            sp.wait_ge(left_out, 32)
            with nc.allow_non_contiguous_dma("256 words"):
                sp.dma_start(leftf[:], left_d[0, :].rearrange("(e b) -> b e", b=B)).then_inc(left_in, 16)
                sp.dma_start(gateL[:], left_d[1, :].rearrange("(e b) -> b e", b=B)).then_inc(left_in, 16)
            sp.wait_ge(left_in, 32)

        @block.gpsimd
        def _(pool):
            nc.gpsimd.iota(rowi[:], pattern=[[0, 1]], base=0, channel_multiplier=1).then_inc(iota_done, 1)
            nc.gpsimd.memset(zeros[:], 0.0).then_inc(zeroed, 1)
            pool.wait_ge(zeroed, 1)
            for a in range(N // (P * 8)):
                pool.dma_start(acc_v[a], zeros[:]).then_inc(acc_out, 16)
            nc.gpsimd.memset(power[:], -0.5).then_inc(zeroed, 1)
            pool.wait_ge(zeroed, 2)
            with pool.Fori(0, NG) as it:
                pool.wait_ge(var_ready, it + 1)
                nc.gpsimd.tensor_tensor(rstd[:], vare[:], power[:], ALU.pow).then_inc(rstd_ready, 1)
            pool.wait_ge(acc_out, 16 * (N // (P * 8)))

        @block.vector
        def _(dve):
            dve.sem_inc(x_free, 2)
            with dve.Fori(0, NG // 2) as i:
                for r in range(2):
                    it = 2 * i + r
                    o = Order(dve, dve_o, it * (3 * GT))
                    dve.wait_ge(x_in[r], 16 * i + 16)
                    dve.wait_ge(xn_out[r], 16 * i + 16)
                    dve.wait_ge(turned, it + 1)
                    for t in range(GT):
                        o.did(nc.vector.bn_stats(out=stats[:, t, :], in_=xg[r][:, t, :]))
                    o.hold(spare)
                    for t in range(GT):
                        o.did(nc.vector.bn_aggr(out=mv[:, t, :], in_=stats[:, t, :]))
                    o.wait()
                    nc.vector.tensor_scalar(vare[:], mv[:, :, 1], EPS, None, ALU.add).then_inc(var_ready, 1)
                    dve.wait_ge(rstd_ready, it + 1)
                    for t in range(GT):
                        last = nc.vector.tensor_scalar(xn[r][:, t, :], xg[r][:, t, :], mv[:, t, 0:1], rstd[:, t:t + 1],
                                                       ALU.subtract, ALU.mult)
                        o.did(last)
                    o.wait()
                    nc.vector.sem_inc(x_free, 1)
                    nc.vector.sem_inc(normed, 1)
            o = Order(dve, top_o)
            dve.wait_ge(logit_sb, NG + 2)
            o.link(nc.vector.tensor_reduce(red[:], logit[:], AX_X, ALU.max))
            nc.vector.tensor_tensor(logit[:], logit[:], red[:].unsqueeze(2).to_broadcast([P, N // P, NE]),
                                    ALU.subtract).then_inc(centred, 1)
            dve.wait_ge(exped, 1)
            o.link(nc.vector.tensor_reduce(red[:], logit[:], AX_X, ALU.add))
            o.link(nc.vector.reciprocal(red[:], red[:]))
            nc.vector.tensor_tensor(prob[:].rearrange("p j e b -> p b j e"),
                                    logit[:].rearrange("p (b j) e -> p b j e", b=B),
                                    red[:].rearrange("p (b j) -> p b j", b=B).unsqueeze(3)
                                    .to_broadcast([P, B, T // P, NE]), ALU.mult).then_inc(soft, 1)
            dve.wait_ge(score_t, 1)
            for h in range(2):
                o.did(nc.vector.tensor_copy(score[0][:, h * 512:(h + 1) * 512], ps[h][:]))
            o.wait()
            base = o.n
            with dve.Fori(0, ROUNDS) as k:
                oo = Order(dve, top_o, base + 5 * k)
                oo.did(nc.vector.max(v8[:], score[0][:]))
                oo.hold(spare)
                oo.did(nc.vector.max_index(i8[:], v8[:], score[0][:]))
                oo.hold(spare)
                oo.did(nc.vector.match_replace(score[0][:], v8[:], score[0][:], -1.0))
                oo.did(nc.vector.tensor_copy(vals[:, bass.ds(8 * k, 8)], v8[:]))
                oo.did(nc.vector.tensor_copy(idxf[:, bass.ds(8 * k, 8)], i8[:]))
                oo.wait()
            o.n = base + 5 * ROUNDS
            dve.wait_ge(iota_done, 1)
            o.link(nc.vector.tensor_scalar(rowb[:], rowi[:], B - 1, None, ALU.bitwise_and))
            o.link(nc.vector.tensor_scalar(rowf[:], rowb[:], float(T), None, ALU.mult))
            nc.vector.tensor_scalar(idxf[:], idxf[:], rowf[:, 0:1], None, ALU.add).then_inc(topped, 1)
            dve.wait_ge(idx_t, 1)
            for h in range(2):
                nc.vector.tensor_copy(idxT[:, :, h], ps[2 + h][:, 0:P])
                last = nc.vector.tensor_copy(gateT[:, :, h], ps[4 + h][:, 0:P])
            last.then_inc(idx_done, 1)
            dve.wait_ge(left_in, 32)
            nc.vector.tensor_copy(idxL[:], leftf[:]).then_inc(idx_done, 1)
            dve.wait_ge(idx_done, 2)

        @block.scalar
        def _(act):
            act.sem_inc(xT_sb, 4)
            act.sem_inc(logit_sb, 2)
            for r in range(2):
                act.sem_inc(xn_out[r], 16)
                act.sem_inc(xT_out[r], 16)
            with act.Fori(0, NG // 2) as i:
                for r in range(2):
                    it = 2 * i + r
                    act.wait_ge(normed, it + 1)
                    act.dma_start(xn_v[:, bass.ds(GT * it, GT), :], xn[r][:]).then_inc(xn_out[r], 16)
                    act.wait_ge(turned, it + 3)
                    act.wait_ge(xT_out[r], 16 * i + 16)
                    act.wait_ge(routed, it + 1)
                    for k in range(KD):
                        nc.scalar.copy(xT[r][:, k, :], ps[2 * r + k][:]).then_inc(xT_sb, 1)
                    act.wait_ge(xT_sb, 4 + 2 * (it + 1))
                    act.dma_start(xT_v[:, :, bass.ds(GN * it, GN)], xT[r][:]).then_inc(xT_out[r], 16)
                    act.wait_ge(routed, 2 + it + 1)
                    nc.scalar.copy(logit[:, bass.ds(GT * it, GT), :],
                                   ps[4 + r][:, 0:GT * NE].rearrange("p (t e) -> p t e", t=GT)).then_inc(logit_sb, 1)
            act.wait_ge(centred, 1)
            nc.scalar.activation(logit[:], logit[:], ACT.Exp).then_inc(exped, 1)
            for r in range(2):
                act.wait_ge(xn_out[r], 16 * (NG // 2) + 16)
                act.wait_ge(xT_out[r], 16 * (NG // 2) + 16)

        @block.tensor
        def _(pe):
            pe.sem_inc(routed, 2)
            pe.sem_inc(turned, 2)
            pe.wait_ge(w_in, 16)
            with pe.Fori(0, NG // 2) as i:
                for r in range(2):
                    it = 2 * i + r
                    pe.wait_ge(normed, it + 1)
                    pe.wait_ge(xT_sb, 2 * it + 2)
                    for k in range(KD):
                        for t in range(GT):
                            last = nc.tensor.transpose(ps[2 * r + k][:, t * P:(t + 1) * P],
                                                       xn[r][:, t, k * P:(k + 1) * P], ident[:])
                    last.then_inc(turned, 1)
                    pe.wait_ge(xT_sb, 4 + 2 * (it + 1))
                    pe.wait_ge(logit_sb, it + 1)
                    for t in range(GT):
                        for k in range(KD):
                            last = nc.tensor.matmul(ps[4 + r][:, t * NE:(t + 1) * NE], xT[r][:, k, t * P:(t + 1) * P],
                                                    wr[:, k, :], start=(k == 0), stop=(k == KD - 1))
                    last.then_inc(routed, 1)
            pe.wait_ge(soft, 1)
            for j in range(T // P):
                last = nc.tensor.transpose(ps[j // 4][:, (j % 4) * P:(j % 4 + 1) * P], prob[:, j].rearrange("p e b -> p (e b)"), ident[:])
            last.then_inc(score_t, 1)
            pe.wait_ge(topped, 1)
            for h in range(2):
                nc.tensor.transpose(ps[2 + h][:, 0:P], idxf[:, h * P:(h + 1) * P], ident[:])
                last = nc.tensor.transpose(ps[4 + h][:, 0:P], vals[:, h * P:(h + 1) * P], ident[:])
            last.then_inc(idx_t, 1)


def experts_phase(nc, ctx, ps, xn_d, acc_d, w1, b1, w2, b2, ident, idxT, gateT, idxL, gateL):
    with ExitStack() as mem:
        def sb(name, shape, dt=F32):
            return mem.enter_context(nc.sbuf_tensor(name, shape, dt))

        sem = phase_semaphores(nc, mem)

        w1s = sb("e_w1", [P, KD, HID])
        w2s = sb("e_w2", [P, HC, D])
        w1p = [sb(f"e_w1{n}", [P, KD, HID], F32R) for n in "hl"]
        w2p = [sb(f"e_w2{n}", [P, HC, D], F32R) for n in "hl"]
        b1i = sb("e_b1i", [P, HC])
        b2i = sb("e_b2i", [P, D])
        b1s = sb("e_b1", [P, HC])
        b2s = sb("e_b2", [P, D])
        ids = sb("e_ids", [P, 2 * B], U32)
        idl = sb("e_idl", [B, 1], U32)
        gts = sb("e_gts", [P, 2 * B])
        gtl = sb("e_gtl", [B, 1])
        xg = [sb(f"e_x{r}", [P, GT, D]) for r in range(2)]
        xT = [[sb(f"e_xT{n}{r}", [P, KD, GN], F32R) for n in "hl"] for r in range(2)]
        hf = [sb(f"e_hf{r}", [P, GN]) for r in range(2)]
        hT = [sb(f"e_hT{n}", [P, HC, GN], F32R) for n in "hl"]
        ys = [sb(f"e_y{r}", [P, GT, D]) for r in range(2)]
        xl = sb("e_xl", [B, D])
        xTl = [sb(f"e_xTl{n}", [P, KD, B], F32R) for n in "hl"]
        hfl = sb("e_hfl", [P, HC, B])
        hTl = [sb(f"e_hTl{n}", [P, HC, P], F32R) for n in "hl"]
        yl = sb("e_yl", [B, D])

        up_in = sem("e_up_in")
        up_split = sem("e_up_split")
        down_split = sem("e_down_split")
        w1h_set = sem("e_w1h_set")
        w2h_set = sem("e_w2h_set")
        padded = sem("e_padded")
        xh_sb = sem("e_xh_sb")
        hi_sb = sem("e_hi_sb")
        down_in = sem("e_down_in")
        ids_set = sem("e_ids_set")
        gts_set = sem("e_gts_set")
        x_in = [sem(f"e_x_in{r}") for r in range(3)]
        turned = sem("e_turned")
        xT_sb = sem("e_xT_sb")
        up_ps = sem("e_up_ps")
        h_sb = sem("e_h_sb")
        down_ps = sem("e_down_ps")
        y_sum = sem("e_y_sum")
        y_sb = sem("e_y_sb")
        y_out = [sem(f"e_y_out{r}") for r in range(3)]
        spare = sem("e_spare")

        GR = QN + 1
        UP = QN * HC + 1
        DOWN = QN * 2 + 1
        HS = QN * HC + HC
        YS = QN * 2 + 1

        block = mem.enter_context(nc.Block())

        @block.sync
        def _(sp):
            with sp.Fori(0, NE) as e:
                sp.wait_ge(up_split, e + 1)
                sp.sem_inc(spare, 1)
                sp.dma_start(w1s[:], w1[bass.ds(e, 1)].rearrange("o p k n -> p (o k) n")).then_inc(up_in, 16)
                sp.dma_start(b1i[:], b1[bass.ds(e, 1)].rearrange("o p n -> p (o n)")).then_inc(up_in, 16)
                sp.wait_ge(down_split, e + 1)
                sp.sem_inc(spare, 1)
                sp.dma_start(w2s[:], w2[bass.ds(e, 1)].rearrange("o p k n -> p (o k) n")).then_inc(down_in, 16)
                sp.dma_start(b2i[:], b2[bass.ds(e, 1)].rearrange("o q n -> (o q) n").to_broadcast([P, D])
                             ).then_inc(down_in, 16)

        @block.gpsimd
        def _(pool):
            for s in (up_ps, h_sb, down_ps, y_sum, up_split, down_split):
                pool.sem_inc(s, 1)
            for part in hTl:
                nc.gpsimd.memset(part[:].bitcast(F32), 0.0).then_inc(padded, 1)
            pool.sem_inc(y_sb, 1)

            def gather(e, q):
                r = q % 2
                pool.wait_ge(turned, GR * e + (q - 1 if q >= 2 else 0) + 1)
                pool.sem_inc(spare, 1)
                for t in range(GT):
                    pool.indirect_dma_start(
                        xg[r][:, t, :], None, xn_d,
                        bass.IndirectOffsetOnAxis(ap=ids[:, GT * q + t:GT * q + t + 1], axis=0)).then_inc(x_in[r], 16)

            def scatter(e, q):
                r = q % 2
                pool.wait_ge(y_sb, YS * e + 2 * (q + 1) + 1)
                pool.sem_inc(spare, 1)
                for t in range(GT):
                    pool.indirect_dma_start(
                        acc_d, bass.IndirectOffsetOnAxis(ap=ids[:, GT * q + t:GT * q + t + 1], axis=0),
                        ys[r][:, t, :], None, compute_op=ALU.add).then_inc(y_out[r], 16)

            with pool.Fori(0, NE) as e:
                nc.gpsimd.tensor_copy(ids[:], idxT[:, bass.ds(B * e, B), :].rearrange("p a b -> p (a b)")
                                      ).then_inc(ids_set, 1)
                nc.gpsimd.tensor_copy(idl[:], idxL[:, bass.ds(e, 1)]).then_inc(ids_set, 1)
                pool.wait_ge(ids_set, 2 * e + 2)
                gather(e, 0)
                pool.indirect_dma_start(xl[:], None, xn_d, bass.IndirectOffsetOnAxis(ap=idl[:, 0:1], axis=0)
                                        ).then_inc(x_in[2], 16)
                for q in range(QN):
                    if q + 1 < QN:
                        gather(e, q + 1)
                    scatter(e, q)
                pool.wait_ge(y_sb, YS * (e + 1) + 1)
                pool.sem_inc(spare, 1)
                pool.indirect_dma_start(acc_d, bass.IndirectOffsetOnAxis(ap=idl[:, 0:1], axis=0), yl[:], None,
                                        compute_op=ALU.add).then_inc(y_out[2], 16)
                for r in range(2):
                    pool.wait_ge(y_out[r], 32 * QN * (e + 1))
                pool.wait_ge(y_out[2], 16 * (e + 1))

        @block.scalar
        def _(act):
            def turn(e, q):
                r = q % 2
                act.wait_ge(turned, GR * e + q + 2)
                for k in range(KD):
                    last = nc.scalar.copy(xT[r][0][:, k, :], ps[k][:])
                last.then_inc(xh_sb, 1)

            act.wait_ge(padded, 2)
            with act.Fori(0, NE) as e:
                act.wait_ge(up_ps, UP * e + 1)
                act.wait_ge(h_sb, HS * e + 1)
                act.wait_ge(up_in, 32 * e + 32)
                nc.scalar.copy(w1p[0][:], w1s[:]).then_inc(w1h_set, 1)
                nc.scalar.copy(b1s[:], b1i[:]).then_inc(w1h_set, 1)
                turn(e, 0)
                act.wait_ge(down_ps, DOWN * e + 1)
                act.wait_ge(down_in, 32 * e + 32)
                nc.scalar.copy(w2p[0][:], w2s[:]).then_inc(w2h_set, 1)
                act.wait_ge(w1h_set, 2 * e + 2)
                for q in range(QN):
                    for m in range(HC):
                        act.wait_ge(up_ps, UP * e + HC * q + m + 2)
                        n = HC * q + m - 2
                        act.wait_ge(h_sb, HS * e + (n + 1 if n >= 0 else 0) + 1)
                        nc.scalar.activation(hf[m % 2][:], ps[2 + m % 2][:], ACT.Gelu, bias=b1s[:, m:m + 1])
                        nc.scalar.activation(hT[0][:, m, :], ps[2 + m % 2][:], ACT.Gelu, bias=b1s[:, m:m + 1]
                                             ).then_inc(hi_sb, 1)
                    if q + 1 < QN:
                        turn(e, q + 1)
                    else:
                        act.wait_ge(turned, GR * (e + 1) + 1)
                        nc.scalar.copy(xTl[0][:], ps[0][:, 0:KD * B].rearrange("p (k n) -> p k n", k=KD)
                                       ).then_inc(xh_sb, 1)
                act.wait_ge(up_ps, UP * (e + 1) + 1)
                for m in range(HC):
                    z = ps[2][:, m * B:(m + 1) * B]
                    nc.scalar.activation(hfl[:, m, :], z, ACT.Gelu, bias=b1s[:, m:m + 1])
                    nc.scalar.activation(hTl[0][:, m, 0:B], z, ACT.Gelu, bias=b1s[:, m:m + 1]).then_inc(hi_sb, 1)

        @block.vector
        def _(dve):
            def turn(e, q):
                r = q % 2
                dve.wait_ge(xh_sb, GR * e + q + 1)
                for k in range(KD):
                    nc.vector.tensor_tensor(xT[r][1][:, k, :], ps[k][:], xT[r][0][:, k, :].bitcast(F32), ALU.subtract
                                            ).then_inc(xT_sb, 1)

            def low_parts(e, q):
                for m in range(HC):
                    dve.wait_ge(hi_sb, HS * e + HC * q + m + 1)
                    nc.vector.tensor_tensor(hT[1][:, m, :], hf[m % 2][:], hT[0][:, m, :].bitcast(F32), ALU.subtract
                                            ).then_inc(h_sb, 1)

            def result(e, q):
                r = q % 2
                if q >= 2:
                    dve.wait_ge(y_out[r], 32 * QN * e + 64 * (q // 2))
                for h in range(2):
                    dve.wait_ge(down_ps, DOWN * e + 2 * q + h + 2)
                    nc.vector.tensor_tensor(ys[r][:, 2 * h:2 * h + 2, :],
                                            ps[4 + 2 * r + h][:].rearrange("p (t n) -> p t n", t=2),
                                            b2s[:].unsqueeze(1).to_broadcast([P, 2, D]), ALU.add).then_inc(y_sum, 1)
                dve.wait_ge(y_sum, YS * e + 2 * q + 3)
                for t in range(GT):
                    last = nc.vector.tensor_scalar(ys[r][:, t, :], ys[r][:, t, :], gts[:, GT * q + t:GT * q + t + 1],
                                                   None, ALU.mult)
                    if t % 2:
                        last.then_inc(y_sb, 1)

            with dve.Fori(0, NE) as e:
                dve.wait_ge(ids_set, 2 * e + 2)
                dve.wait_ge(y_sb, YS * e + 1)
                dve.wait_ge(y_sum, YS * e + 1)
                dve.wait_ge(down_in, 32 * e + 32)
                dve.wait_ge(up_ps, UP * e + 1)
                dve.wait_ge(down_ps, DOWN * e + 1)
                nc.vector.tensor_copy(gts[:], gateT[:, bass.ds(B * e, B), :].rearrange("p a b -> p (a b)")
                                      ).then_inc(gts_set, 1)
                nc.vector.tensor_copy(gtl[:], gateL[:, bass.ds(e, 1)]).then_inc(gts_set, 1)
                nc.vector.tensor_copy(b2s[:], b2i[:]).then_inc(gts_set, 1)
                dve.wait_ge(gts_set, 3 * e + 3)
                dve.wait_ge(w1h_set, 2 * e + 2)
                nc.vector.tensor_tensor(w1p[1][:], w1s[:], w1p[0][:].bitcast(F32), ALU.subtract).then_inc(up_split, 1)
                turn(e, 0)
                dve.wait_ge(w2h_set, e + 1)
                nc.vector.tensor_tensor(w2p[1][:], w2s[:], w2p[0][:].bitcast(F32), ALU.subtract
                                        ).then_inc(down_split, 1)
                for q in range(QN):
                    low_parts(e, q)
                    if q + 1 < QN:
                        turn(e, q + 1)
                    else:
                        dve.wait_ge(xh_sb, GR * (e + 1))
                        nc.vector.tensor_tensor(xTl[1][:], ps[0][:, 0:KD * B].rearrange("p (k n) -> p k n", k=KD),
                                                xTl[0][:].bitcast(F32), ALU.subtract).then_inc(xT_sb, 2)
                    result(e, q)
                dve.wait_ge(hi_sb, HS * (e + 1))
                nc.vector.tensor_tensor(hTl[1][:, :, 0:B], hfl[:], hTl[0][:, :, 0:B].bitcast(F32), ALU.subtract
                                        ).then_inc(h_sb, HC)
                dve.wait_ge(down_ps, DOWN * (e + 1) + 1)
                nc.vector.tensor_tensor(yl[:], ps[4][0:B, 0:D], b2s[0:B, :], ALU.add).then_inc(y_sum, 1)
                dve.wait_ge(y_sum, YS * (e + 1) + 1)
                nc.vector.tensor_scalar(yl[:], yl[:], gtl[:, 0:1], None, ALU.mult).then_inc(y_sb, 1)

        @block.tensor
        def _(pe):
            pe.sem_inc(turned, 1)
            pe.sem_inc(xT_sb, 2)

            def turn(e, q):
                r = q % 2
                pe.wait_ge(x_in[r], 32 * QN * e + 64 * (q // 2) + 64)
                pe.wait_ge(xT_sb, 2 * GR * e + 2 * q + 2)
                for k in range(KD):
                    for t in range(GT):
                        last = nc.tensor.transpose(ps[k][:, t * P:(t + 1) * P], xg[r][:, t, k * P:(k + 1) * P],
                                                   ident[:])
                last.then_inc(turned, 1)

            def turn_last(e):
                pe.wait_ge(x_in[2], 16 * e + 16)
                pe.wait_ge(xT_sb, 2 * GR * e + 2 * QN + 2)
                pe.sem_inc(spare, 1)
                for k in range(KD):
                    last = nc.tensor.transpose(ps[0][:, k * B:(k + 1) * B], xl[:, k * P:(k + 1) * P], ident[0:B, 0:B])
                last.then_inc(turned, 1)

            def product(out, terms):
                pairs = [(a[i], b[j]) for a, b in terms for i, j in ((0, 0), (1, 0), (0, 1))]
                for n, (lhsT, rhs) in enumerate(pairs):
                    last = nc.tensor.matmul(out, lhsT, rhs, start=(n == 0), stop=(n == len(pairs) - 1))
                return last

            pe.wait_ge(padded, 2)
            with pe.Fori(0, NE) as e:
                turn(e, 0)
                pe.wait_ge(up_split, e + 2)
                for q in range(QN):
                    r = q % 2
                    pe.wait_ge(xT_sb, 2 * GR * e + 2 * (q + 1) + 2)
                    for m in range(HC):
                        n = HC * q + m - 2
                        pe.wait_ge(h_sb, HS * e + (n + 1 if n >= 0 else 0) + 1)
                        product(ps[2 + m % 2][:], [([w[:, k, m * P:(m + 1) * P] for w in w1p],
                                                    [v[:, k, :] for v in xT[r]]) for k in range(KD)]
                                ).then_inc(up_ps, 1)
                    if q + 1 < QN:
                        turn(e, q + 1)
                    else:
                        turn_last(e)
                    if q == 0:
                        pe.wait_ge(down_split, e + 2)
                    pe.wait_ge(h_sb, HS * e + HC * (q + 1) + 1)
                    for h in range(2):
                        n = 2 * (q - 2) + h
                        pe.wait_ge(y_sum, YS * e + (n + 1 if n >= 0 else 0) + 1)
                        for t in (2 * h, 2 * h + 1):
                            last = product(ps[4 + 2 * r + h][:, (t % 2) * D:(t % 2 + 1) * D],
                                           [([v[:, m, t * P:(t + 1) * P] for v in hT], [w[:, m, :] for w in w2p])
                                            for m in range(HC)])
                        last.then_inc(down_ps, 1)
                pe.wait_ge(xT_sb, 2 * GR * (e + 1) + 2)
                pe.wait_ge(h_sb, HS * e + HC * QN + 1)
                for m in range(HC):
                    last = product(ps[2][:, m * B:(m + 1) * B], [([w[:, k, m * P:(m + 1) * P] for w in w1p],
                                                                  [v[:, k, :] for v in xTl]) for k in range(KD)])
                last.then_inc(up_ps, 1)
                pe.wait_ge(h_sb, HS * (e + 1) + 1)
                pe.wait_ge(y_sum, YS * e + 2 * QN + 1)
                product(ps[4][:, 0:D], [([v[:, m, :] for v in hTl], [w[:, m, :] for w in w2p]) for m in range(HC)]
                        ).then_inc(down_ps, 1)


def recurrence_phase(nc, ctx, ps, xnT_d, s0_d, ident, w):
    with ExitStack() as mem:
        def sb(name, shape, dt=F32):
            return mem.enter_context(nc.sbuf_tensor(name, shape, dt))

        sem = phase_semaphores(nc, mem)

        mu = sb("a_mu", [P, KD])
        w1 = sb("a_w1", [P, KD, RANK])
        w2 = sb("a_w2", [RANK, NMU * RANK])
        b2 = sb("a_b2", [P, 1])
        b2t = sb("a_b2t", [RANK, 1])
        xo = sb("a_xo", [P, NMU - 1, D])
        xot = sb("a_xot", [RANK, D])
        xb = sb("a_xb", [P, NMU, KD])
        rw = sb("a_rw", [P, KD, KW])
        kw = sb("a_kw", [P, KD, KW])
        vw = sb("a_vw", [P, KD, VW])
        gw = sb("a_gw", [P, KD, VW])
        dw1 = sb("a_dw1", [P, KD, GATE])
        dw2 = sb("a_dw2", [GATE, KW])
        db = sb("a_db", [KW, 1])
        bonus = sb("a_bonus", [KW, 1])
        gnw = sb("a_gnw", [P, VW])
        gnb = sb("a_gnb", [P, VW])
        ow = sb("a_ow", [P, KD, D])
        power = sb("a_power", [P, NH])

        h = [sb(f"a_h{r}", [P, KD, GN + 1]) for r in range(2)]
        delta = sb("a_delta", [P, KD, GN])
        lerp = sb("a_lerp", [P, KD, GN])
        low = sb("a_low", [RANK, GN])
        x1 = sb("a_x1", [P, GN])
        x1t = sb("a_x1t", [RANK, GN])
        tmp = [sb(f"a_tmp{r}", [P, GN]) for r in range(2)]
        mix = [sb(f"a_mix{n}", [P, KD, GN]) for n in range(NMU)]
        dlow = sb("a_dlow", [GATE, GN])
        dexp = sb("a_dexp", [KW, GN])
        decay = [sb(f"a_decay{lv}", [KW, GN >> lv]) for lv in range(LEVELS + 1)]
        R = sb("a_R", [KW, NH, GN])
        K = sb("a_K", [KW, GN])
        rk = sb("a_rk", [KW, GN])
        heads = sb("a_heads", [KW, NH])
        V = sb("a_V", [P, GT, VW])
        th = sb("a_th", [P, GT, VW])
        G = sb("a_G", [P, GT, VW])
        A = [sb(f"a_A{c}", [P, NH * P]) for c in range(GT)]
        KT = [sb(f"a_KT{r}", [P, KW]) for r in range(2)]
        S = sb("a_S", [KW, DV])
        on = [sb(f"a_on{r}", [P, VW]) for r in range(2)]
        ogT = [sb(f"a_ogT{r}", [P, KD, P]) for r in range(2)]
        s0 = sb("a_s0", [P, GT, D])
        stats = sb("a_stats", [P, NH, 6])
        mv = sb("a_mv", [P, NH, 2])
        vare = sb("a_vare", [P, NH])
        rstd = sb("a_rstd", [P, NH])
        mask = [sb(f"a_mask{lv}", [P, P], U32) for lv in range(LEVELS)]
        col = sb("a_col", [P, P], I32)
        row = sb("a_row", [P, P], I32)
        bits = sb("a_bits", [P, P], I32)
        shifted = sb("a_shifted", [P, P], I32)
        after = sb("a_after", [P, P])
        level = sb("a_level", [P, P])

        w_in = sem("a_w_in")
        set_up = sem("a_set_up")
        masks = sem("a_masks")
        h_in = [sem(f"a_h_in{r}") for r in range(2)]
        deltas = sem("a_deltas")
        lerped = sem("a_lerped")
        low_ps = sem("a_low_ps")
        low_sb = sem("a_low_sb")
        x0_ps = sem("a_x0_ps")
        x1_sb = sem("a_x1_sb")
        mu_ps = sem("a_mu_ps")
        mu_sb = sem("a_mu_sb")
        mixed = sem("a_mixed")
        dlow_ps = sem("a_dlow_ps")
        dlow_sb = sem("a_dlow_sb")
        dexp_ps = sem("a_dexp_ps")
        dexp_sb = sem("a_dexp_sb")
        decay_sb = sem("a_decay_sb")
        rk_ps = sem("a_rk_ps")
        rk_sb = sem("a_rk_sb")
        v_ps = sem("a_v_ps")
        v_sb = sem("a_v_sb")
        g_ps = sem("a_g_ps")
        th_sb = sem("a_th_sb")
        G_sb = sem("a_G_sb")
        rkb = sem("a_rkb")
        own_ps = sem("a_own_ps")
        own_sb = sem("a_own_sb")
        A_ps = sem("a_A_ps")
        A_sb = sem("a_A_sb")
        stepped = sem("a_stepped")
        KT_ps = sem("a_KT_ps")
        KT_sb = sem("a_KT_sb")
        U_ps = sem("a_U_ps")
        S_sb = sem("a_S_sb")
        o_ps = sem("a_o_ps")
        on_sb = sem("a_on_sb")
        norm_o = sem("a_norm_o")
        var_sb = sem("a_var_sb")
        rstd_sb = sem("a_rstd_sb")
        gated = sem("a_gated")
        gate_o = sem("a_gate_o")
        ogT_ps = sem("a_ogT_ps")
        ogT_sb = sem("a_ogT_sb")
        s0_ps = sem("a_s0_ps")
        s0_sb = sem("a_s0_sb")
        s0_out = sem("a_s0_out")
        spare = sem("a_spare")

        hT_v = xnT_d.rearrange("k p n -> p k n")
        s0_v = s0_d.rearrange("(g t p) d -> p (g t) d", t=GT, p=P)
        NMM = NMU * KD
        NA = LEVELS * GT
        NSTEP = LEVELS * GT
        LOADS = 21
        order = [1, 0, 2, 3, 4]

        block = mem.enter_context(nc.Block())

        @block.sync
        def _(sp):
            loads = [(mu[:], w["L0_attn_x_proj_mu"]), (w1[:], w["L0_attn_xl_w1"]), (w2[:], w["L0_attn_xl_w2"]),
                     (b2[:], w["L0_attn_xl_b2"][0:P]), (b2t[:], w["L0_attn_xl_b2"][P:P + RANK]),
                     (xot[:], w["L0_attn_x_out_w"][P:P + RANK]), (xb[:], w["L0_attn_x_bias"]),
                     (rw[:], w["L0_attn_r_w"]), (kw[:], w["L0_attn_k_w"]), (vw[:], w["L0_attn_v_w"]),
                     (gw[:], w["L0_attn_g_w"]), (dw1[:], w["L0_attn_w_w1"]), (dw2[:], w["L0_attn_w_w2"]),
                     (db[:], w["L0_attn_w_b"]), (bonus[:], w["L0_attn_bonus"]),
                     (gnw[:], w["L0_attn_gn_weight"].to_broadcast([P, VW])),
                     (gnb[:], w["L0_attn_gn_bias"].to_broadcast([P, VW])), (ow[:], w["L0_attn_o_w"])]
            for dst, src in loads:
                sp.dma_start(dst, src).then_inc(w_in, 16)
            sp.wait_ge(set_up, 5)
            for n in range(NMU - 1):
                sp.dma_start(xo[RANK * n:RANK * (n + 1), n, :], w["L0_attn_x_out_w"][RANK * n:RANK * (n + 1)]
                             ).then_inc(w_in, 16)
            assert len(loads) + NMU - 1 == LOADS + 1
            with sp.Fori(0, B) as b:
                for r in range(HALVES):
                    g = HALVES * b + r
                    sp.wait_ge(mixed, NMM * g + NMM)
                    sp.sem_inc(spare, 1)
                    if r == 0:
                        sp.dma_start(h[0][:, :, 1:GN + 1], hT_v[:, :, bass.ds(T * b, GN)]).then_inc(h_in[0], 16)
                    else:
                        sp.dma_start(h[1][:], hT_v[:, :, bass.ds(T * b + GN - 1, GN + 1)]).then_inc(h_in[1], 16)

        @block.gpsimd
        def _(pool):
            pool.sem_inc(mixed, 2 * NMM)
            nc.gpsimd.memset(xo[:], 0.0).then_inc(set_up, 1)
            nc.gpsimd.memset(R[:], 0.0).then_inc(set_up, 1)
            nc.gpsimd.memset(h[0][:, :, 0:1], 0.0).then_inc(set_up, 1)
            nc.gpsimd.memset(power[:], -0.5).then_inc(set_up, 1)
            nc.gpsimd.memset(heads[:], 0.0).then_inc(set_up, 1)
            nc.gpsimd.iota(col[:], pattern=[[1, P]], base=0, channel_multiplier=0).then_inc(masks, 1)
            nc.gpsimd.iota(row[:], pattern=[[0, P]], base=0, channel_multiplier=1).then_inc(masks, 1)
            pool.wait_ge(set_up, 5)
            pool.wait_ge(masks, 2)
            for hd in range(NH):
                nc.gpsimd.memset(heads[hd * DK:(hd + 1) * DK, hd:hd + 1], 1.0).then_inc(set_up, 1)
            pool.wait_ge(set_up, 9)
            pool.wait_ge(w_in, 16 * (LOADS + 1))
            nc.gpsimd.tensor_scalar(gnw[:], gnw[:], 0.5, None, ALU.mult).then_inc(set_up, 1)
            nc.gpsimd.tensor_scalar(gnb[:], gnb[:], 0.5, None, ALU.mult).then_inc(set_up, 1)
            pool.wait_ge(set_up, 11)
            with pool.Fori(0, B) as b:
                for r in range(HALVES):
                    g = HALVES * b + r
                    pool.wait_ge(h_in[r], 16 * b + 16)
                    pool.wait_ge(mu_sb, NMM * g + 2)
                    nc.gpsimd.tensor_tensor(delta[:], h[r][:, :, 0:GN], h[r][:, :, 1:GN + 1], ALU.subtract
                                            ).then_inc(deltas, 1)
                    pool.wait_ge(s0_sb, GT * g + 1)
                    for i in range(NMM):
                        n, m = order[i // KD], i % KD
                        pool.wait_ge(mu_sb, NMM * g + i + 1 + 2)
                        nc.gpsimd.tensor_tensor(mix[n][:, m, :], tmp[i % 2][:], h[r][:, m, 1:GN + 1], ALU.add
                                                ).then_inc(mixed, 1)
                    pool.wait_ge(decay_sb, g + 1)
                    pool.wait_ge(rk_sb, 2 * g + 2)
                    pool.wait_ge(rkb, g + 1)
                    for lv in range(LEVELS):
                        half = 1 << lv
                        nb = P // (2 * half)
                        for c in range(GT):
                            pool.wait_ge(A_ps, NA * g + lv * GT + c + 1)
                            if lv:
                                pool.wait_ge(stepped, NSTEP * g + (lv - 1) * GT + c + 1)
                            dk = decay[lv][:, c * 2 * nb:(c + 1) * 2 * nb].rearrange("p (n s) -> p n s", s=2)
                            Rv = R[:, :, c * P:(c + 1) * P].rearrange("p h (n s t) -> p h n s t", s=2, t=half)
                            nc.gpsimd.tensor_tensor(
                                Rv[:, :, :, 1, :], Rv[:, :, :, 1, :],
                                dk[:, :, 0].unsqueeze(1).unsqueeze(3).to_broadcast([P, NH, nb, half]), ALU.mult)
                            Kv = K[:, c * P:(c + 1) * P].rearrange("p (n s t) -> p n s t", s=2, t=half)
                            nc.gpsimd.tensor_tensor(Kv[:, :, 0, :], Kv[:, :, 0, :],
                                                    dk[:, :, 1].unsqueeze(2).to_broadcast([P, nb, half]), ALU.mult)
                            nc.gpsimd.tensor_tensor(decay[lv + 1][:, c * nb:(c + 1) * nb], dk[:, :, 0], dk[:, :, 1],
                                                    ALU.mult).then_inc(stepped, 1)
                    for c in range(GT):
                        o = Order(pool, gate_o, (g * GT + c) * 2)
                        pool.wait_ge(var_sb, GT * g + c + 1)
                        nc.gpsimd.tensor_tensor(rstd[:], vare[:], power[:], ALU.pow).then_inc(rstd_sb, 1)
                        pool.wait_ge(on_sb, GT * g + c + 1)
                        o.link(nc.gpsimd.tensor_tensor(on[c % 2][:], on[c % 2][:], gnw[:], ALU.mult))
                        o.link(nc.gpsimd.tensor_tensor(on[c % 2][:], on[c % 2][:], gnb[:], ALU.add))
                        pool.wait_ge(G_sb, 2 * g + 2)
                        nc.gpsimd.tensor_tensor(on[c % 2][:], on[c % 2][:], G[:, c, :], ALU.mult).then_inc(gated, 1)

        @block.vector
        def _(dve):
            dve.sem_inc(mu_sb, 2)
            o = Order(dve, masks, 2)
            dve.wait_ge(masks, 2)
            o.link(nc.vector.tensor_tensor(bits[:], row[:], col[:], ALU.bitwise_xor))
            o.link(nc.vector.tensor_tensor(after[:], col[:], row[:], ALU.is_gt))
            for lv in range(LEVELS):
                o.link(nc.vector.tensor_scalar(shifted[:], bits[:], lv, None, ALU.logical_shift_right))
                o.link(nc.vector.tensor_scalar(level[:], shifted[:], 1.0, None, ALU.is_equal))
                o.link(nc.vector.tensor_tensor(mask[lv][:], level[:], after[:], ALU.mult))
            dve.wait_ge(w_in, 16 * (LOADS + 1))
            with dve.Fori(0, B) as b:
                for r in range(HALVES):
                    g = HALVES * b + r
                    dve.wait_ge(deltas, g + 1)
                    dve.wait_ge(s0_sb, GT * g + 1)
                    for m in range(KD):
                        nc.vector.scalar_tensor_tensor(out=lerp[:, m, :], in0=delta[:, m, :], scalar=mu[:, m:m + 1],
                                                       in1=h[r][:, m, 1:GN + 1], op0=ALU.mult, op1=ALU.add
                                                       ).then_inc(lerped, 1)
                    for i in range(NMM):
                        n, m = order[i // KD], i % KD
                        dve.wait_ge(mu_ps, NMM * g + i + 1)
                        dve.wait_ge(mixed, NMM * (g + 2) + i - 1)
                        nc.vector.scalar_tensor_tensor(out=tmp[i % 2][:], in0=ps[i % 2][:], scalar=xb[:, n, m:m + 1],
                                                       in1=delta[:, m, :], op0=ALU.add, op1=ALU.mult
                                                       ).then_inc(mu_sb, 1)
                    dve.wait_ge(rk_sb, 2 * g + 2)
                    nc.vector.scalar_tensor_tensor(out=rk[:], in0=K[:], scalar=bonus[:, 0:1], in1=ps[4][:],
                                                   op0=ALU.mult, op1=ALU.mult).then_inc(rkb, 1)
                    for u in range(2):
                        dve.wait_ge(th_sb, 2 * g + u + 1)
                        nc.vector.scalar_tensor_tensor(
                            out=G[:, 2 * u:2 * u + 2, :].rearrange("p t n -> p (t n)"),
                            in0=th[:, 2 * u:2 * u + 2, :].rearrange("p t n -> p (t n)"), scalar=1.0,
                            in1=ps[2 + u][:], op0=ALU.add, op1=ALU.mult).then_inc(G_sb, 1)
                    dve.wait_ge(own_ps, g + 1)
                    for c in range(GT):
                        for hd in range(NH):
                            last = nc.vector.tensor_scalar(A[c][:, hd * P:(hd + 1) * P], ident[:],
                                                           ps[5][:, c * NH + hd:c * NH + hd + 1], None, ALU.mult)
                        last.then_inc(own_sb, 1)
                    for lv in range(LEVELS):
                        half = 1 << lv
                        for c in range(GT):
                            n = lv * GT + c
                            dve.wait_ge(A_ps, NA * g + n + 1)
                            if lv:
                                dve.wait_ge(A_sb, NA * g + n - GT + 1)
                            else:
                                dve.wait_ge(own_sb, GT * g + c + 1)
                            dve.sem_inc(spare, 1)
                            a3 = A[c][:].rearrange("p (h n s t) -> p h n s t", h=NH, s=2, t=half)[:, :, :, 1, :]
                            m3 = mask[lv][:].rearrange("p (n s t) -> p n s t", s=2, t=half)[:, :, 1, :]
                            p3 = ps[n % 2][:, 0:NH * P // 2].rearrange("p (h n t) -> p h n t", h=NH, t=half)
                            nc.vector.copy_predicated(
                                a3, m3.unsqueeze(1).to_broadcast([P, NH, P // (2 * half), half]), p3
                            ).then_inc(A_sb, 1)
                    if r == 0:
                        dve.wait_ge(s0_sb, GT * g + 1)
                        nc.vector.memset(S[:], 0.0).then_inc(S_sb, 1)
                    for c in range(GT):
                        sc = (1 + GT * HALVES) * b + 1 + r * GT + c
                        dve.wait_ge(U_ps, GT * g + c + 1)
                        dve.wait_ge(o_ps, GT * g + c + 1)
                        dve.wait_ge(S_sb, sc)
                        nc.vector.scalar_tensor_tensor(out=S[:], in0=S[:], scalar=decay[LEVELS][:, c:c + 1],
                                                       in1=ps[7][:, 0:DV], op0=ALU.mult, op1=ALU.add
                                                       ).then_inc(S_sb, 1)
                        o = Order(dve, norm_o, (g * GT + c) * 2 * NH)
                        op = ps[4 + c % 2][:, 0:VW].rearrange("p (h v) -> p h v", h=NH)
                        for hd in range(NH):
                            o.did(nc.vector.bn_stats(out=stats[:, hd, :], in_=op[:, hd, :]))
                        o.hold(spare)
                        for hd in range(NH):
                            o.did(nc.vector.bn_aggr(out=mv[:, hd, :], in_=stats[:, hd, :]))
                        o.wait()
                        nc.vector.tensor_scalar(vare[:], mv[:, :, 1], EPS, None, ALU.add).then_inc(var_sb, 1)
                        dve.wait_ge(rstd_sb, GT * g + c + 1)
                        if c >= 2:
                            dve.wait_ge(ogT_ps, GT * g + c - 1)
                        for hd in range(NH):
                            last = nc.vector.tensor_scalar(on[c % 2][:, hd * DV:(hd + 1) * DV], op[:, hd, :],
                                                           mv[:, hd, 0:1], rstd[:, hd:hd + 1], ALU.subtract, ALU.mult)
                        last.then_inc(on_sb, 1)

        @block.scalar
        def _(act):
            act.sem_inc(s0_sb, 1)
            act.sem_inc(s0_out, 16)
            act.wait_ge(w_in, 16 * (LOADS + 1))
            act.wait_ge(set_up, 11)
            with act.Fori(0, B) as b:
                for r in range(HALVES):
                    g = HALVES * b + r
                    act.wait_ge(s0_sb, GT * g + 1)
                    act.wait_ge(low_ps, g + 1)
                    nc.scalar.activation(low[:], ps[2][0:RANK, :], ACT.Tanh).then_inc(low_sb, 1)
                    act.wait_ge(x0_ps, g + 1)
                    nc.scalar.activation(x1[:], ps[3][:], ACT.Tanh, bias=b2[:, 0:1]).then_inc(x1_sb, 1)
                    nc.scalar.activation(x1t[:], ps[4][0:RANK, :], ACT.Tanh, bias=b2t[:, 0:1]).then_inc(x1_sb, 1)
                    act.wait_ge(dlow_ps, g + 1)
                    nc.scalar.activation(dlow[:], ps[2][0:GATE, :], ACT.Tanh).then_inc(dlow_sb, 1)
                    act.wait_ge(dexp_ps, g + 1)
                    nc.scalar.activation(dexp[:], ps[3][:], ACT.Exp, bias=db[:, 0:1]).then_inc(dexp_sb, 1)
                    act.wait_ge(dexp_sb, g + 1)
                    nc.scalar.activation(decay[0][:], dexp[:], ACT.Exp, scale=-1.0).then_inc(decay_sb, 1)
                    act.wait_ge(rk_ps, 2 * g + 1)
                    for hd in range(NH):
                        rows = slice(hd * DK, (hd + 1) * DK)
                        last = nc.scalar.copy(R[rows, hd, :], ps[4][rows, :])
                    last.then_inc(rk_sb, 1)
                    act.wait_ge(rk_ps, 2 * g + 2)
                    nc.scalar.copy(K[:], ps[5][:]).then_inc(rk_sb, 1)
                    for u in range(2):
                        act.wait_ge(v_ps, 2 * g + u + 1)
                        nc.scalar.copy(V[:, 2 * u:2 * u + 2, :].rearrange("p t n -> p (t n)"), ps[6 + u][:]
                                       ).then_inc(v_sb, 1)
                    for u in range(2):
                        act.wait_ge(g_ps, 2 * g + u + 1)
                        nc.scalar.activation(th[:, 2 * u:2 * u + 2, :].rearrange("p t n -> p (t n)"), ps[2 + u][:],
                                             ACT.Tanh, scale=0.5).then_inc(th_sb, 1)
                    act.wait_ge(s0_out, 16 * g + 16)
                    for c in range(GT + 1):
                        if c < GT:
                            act.wait_ge(KT_ps, GT * g + c + 1)
                            if c >= 2:
                                act.wait_ge(U_ps, GT * g + c - 1)
                            nc.scalar.copy(KT[c % 2][:], ps[6][:, 0:KW]).then_inc(KT_sb, 1)
                        if c:
                            act.wait_ge(ogT_ps, GT * g + c)
                            if c >= 3:
                                act.wait_ge(s0_ps, GT * g + c - 2)
                            nc.scalar.copy(ogT[(c - 1) % 2][:].rearrange("p k n -> p (k n)"), ps[2][:, 0:KD * P]
                                           ).then_inc(ogT_sb, 1)
                            act.wait_ge(s0_ps, GT * g + c)
                            nc.scalar.copy(s0[:, c - 1, :], ps[3][:, 0:D]).then_inc(s0_sb, 1)
                    act.wait_ge(s0_sb, GT * (g + 1) + 1)
                    act.dma_start(s0_v[:, bass.ds(GT * g, GT), :], s0[:]).then_inc(s0_out, 16)
            act.wait_ge(s0_out, 16 * B * HALVES + 16)

        @block.tensor
        def _(pe):
            pe.wait_ge(w_in, 16 * (LOADS + 1))
            pe.wait_ge(set_up, 11)

            def product(out, sem_, pairs):
                for k, (lhsT, rhs) in enumerate(pairs):
                    last = nc.tensor.matmul(out, lhsT, rhs, start=(k == 0), stop=(k == len(pairs) - 1))
                if sem_ is not None:
                    last.then_inc(sem_, 1)

            with pe.Fori(0, B) as b:
                for r in range(HALVES):
                    g = HALVES * b + r

                    def mixes(i):
                        n, m = order[i // KD], i % KD
                        pe.wait_ge(mu_sb, NMM * g + i + 1)
                        lhsT = xo[:, n, m * P:(m + 1) * P] if n < NMU - 1 else xot[:, m * P:(m + 1) * P]
                        product(ps[i % 2][:], mu_ps, [(lhsT, x1[:] if n < NMU - 1 else x1t[:])])

                    def have_mix(j):
                        pe.wait_ge(mixed, NMM * (g + 2) + KD * (j + 1))

                    pe.wait_ge(s0_sb, GT * g + 1)
                    pe.wait_ge(lerped, 2 * g + 2)
                    product(ps[2][0:RANK, :], low_ps, [(w1[:, k, :], lerp[:, k, :]) for k in range(KD)])
                    pe.wait_ge(low_sb, g + 1)
                    product(ps[3][:], None, [(w2[:, 0:P], low[:])])
                    product(ps[4][0:RANK, :], x0_ps, [(w2[:, P:P + RANK], low[:])])
                    pe.wait_ge(x1_sb, 2 * g + 2)
                    for i in range(4):
                        mixes(i)
                    have_mix(0)
                    product(ps[2][0:GATE, :], dlow_ps, [(dw1[:, k, :], mix[1][:, k, :]) for k in range(KD)])
                    mixes(4)
                    mixes(5)
                    pe.wait_ge(dlow_sb, g + 1)
                    product(ps[3][:], dexp_ps, [(dw2[:], dlow[:])])
                    have_mix(1)
                    product(ps[4][:], rk_ps, [(rw[:, k, :], mix[0][:, k, :]) for k in range(KD)])
                    mixes(6)
                    mixes(7)
                    have_mix(2)
                    product(ps[5][:], rk_ps, [(kw[:, k, :], mix[2][:, k, :]) for k in range(KD)])
                    mixes(8)
                    mixes(9)
                    have_mix(3)
                    for t in range(GT):
                        product(ps[6 + t // 2][:, (t % 2) * VW:(t % 2 + 1) * VW], v_ps if t % 2 else None,
                                [(mix[3][:, k, t * P:(t + 1) * P], vw[:, k, :]) for k in range(KD)])
                    have_mix(4)
                    pe.wait_ge(decay_sb, g + 1)
                    for t in range(GT):
                        product(ps[2 + t // 2][:, (t % 2) * VW:(t % 2 + 1) * VW], g_ps if t % 2 else None,
                                [(mix[4][:, k, t * P:(t + 1) * P], gw[:, k, :]) for k in range(KD)])
                    pe.wait_ge(rkb, g + 1)
                    for c in range(GT):
                        last = nc.tensor.matmul(ps[5][:, c * NH:(c + 1) * NH], rk[:, c * P:(c + 1) * P], heads[:],
                                                start=True, stop=True)
                    last.then_inc(own_ps, 1)
                    pe.wait_ge(mu_sb, NMM * (g + 1) + 2)
                    for lv in range(LEVELS):
                        half = 1 << lv
                        for c in range(GT):
                            n = lv * GT + c
                            if n >= 2:
                                pe.wait_ge(A_sb, NA * g + n - 1)
                            if lv:
                                pe.wait_ge(stepped, NSTEP * g + (lv - 1) * GT + c + 1)
                            tok = slice(c * P, (c + 1) * P)
                            product(ps[n % 2][:, 0:NH * P // 2].rearrange("p (h n t) -> p h n t", h=NH, t=half), A_ps,
                                    [(K[:, tok], R[:, :, tok].rearrange("p h (n s t) -> p h n s t", s=2, t=half)
                                      [:, :, :, 1, :])])
                    pe.wait_ge(v_sb, 2 * g + 2)
                    pe.wait_ge(G_sb, 2 * g + 2)

                    def finish(c):
                        pe.wait_ge(gated, GT * g + c + 1)
                        if c:
                            pe.wait_ge(ogT_sb, GT * g + c)
                        for k in range(KD):
                            last = nc.tensor.transpose(ps[2][:, k * P:(k + 1) * P], on[c % 2][:, k * P:(k + 1) * P],
                                                       ident[:])
                        last.then_inc(ogT_ps, 1)
                        pe.wait_ge(ogT_sb, GT * g + c + 1)
                        if c:
                            pe.wait_ge(s0_sb, GT * g + c + 1)
                        product(ps[3][:, 0:D], s0_ps, [(ogT[c % 2][:, k, :], ow[:, k, :]) for k in range(KD)])

                    for c in range(GT):
                        tok = slice(c * P, (c + 1) * P)
                        pe.wait_ge(stepped, NSTEP * g + (LEVELS - 1) * GT + c + 1)
                        if c:
                            pe.wait_ge(KT_sb, GT * g + c)
                        nc.tensor.transpose(ps[6][:, 0:KW], K[:, tok], ident[:]).then_inc(KT_ps, 1)
                        pe.wait_ge(A_sb, NA * g + (LEVELS - 1) * GT + c + 1)
                        pe.wait_ge(S_sb, (1 + GT * HALVES) * b + 1 + r * GT + c)
                        if c >= 2:
                            pe.wait_ge(on_sb, GT * g + c - 1)
                        for hd in range(NH):
                            product(ps[4 + c % 2][:, hd * DV:(hd + 1) * DV], o_ps if hd == NH - 1 else None,
                                    [(A[c][:, hd * P:(hd + 1) * P], V[:, c, hd * DV:(hd + 1) * DV]),
                                     (R[:, hd, tok], S[:])])
                        pe.wait_ge(KT_sb, GT * g + c + 1)
                        for hd in range(NH):
                            product(ps[7][hd * DK:(hd + 1) * DK, 0:DV], U_ps if hd == NH - 1 else None,
                                    [(KT[c % 2][:, hd * DK:(hd + 1) * DK], V[:, c, hd * DV:(hd + 1) * DV])])
                        if c:
                            finish(c - 1)
                    finish(GT - 1)


def layer1_phase(nc, ctx, ps, x, s0_d, acc_d, x1_d, xn1_d, g_d, ident, w, Y, coef):
    with ExitStack() as mem:
        def sb(name, shape, dt=F32):
            return mem.enter_context(nc.sbuf_tensor(name, shape, dt))

        sem = phase_semaphores(nc, mem)

        w1s = sb("f_w1", [P, KD, FF])
        w3s = sb("f_w3", [P, KD, FF])
        w2s = sb("f_w2", [P, FC, D])
        w1p, w3p = ([sb(f"f_w{m}{n}", [P, KD, FC * P], F32R) for n in "hl"] for m in (1, 3))
        w2p = [sb(f"f_w2{n}", [P, FC, D], F32R) for n in "hl"]
        bm = sb("f_bm", [P, KD, 2 * PS])
        bmp = [sb(f"f_bm{n}", [P, KD, 2 * PS], F32R) for n in "hl"]
        raw = sb("f_raw", [P, 4])
        xg = [sb(f"f_x{r}", [P, GT, D]) for r in range(2)]
        sg = [sb(f"f_s{r}", [P, GT, D]) for r in range(2)]
        ag = [sb(f"f_a{r}", [P, GT, D]) for r in range(2)]
        xn = sb("f_xn", [P, GT, D])
        xT = [[sb(f"f_xT{n}{r}", [P, KD, GN], F32R) for n in "hl"] for r in range(2)]
        act_ = [sb(f"f_act{r}", [P, GN]) for r in range(2)]
        hf = [sb(f"f_hf{r}", [P, GN]) for r in range(2)]
        hT = [sb(f"f_hT{n}", [P, FC, GN], F32R) for n in "hl"]
        gs = sb("f_gs", [P, GT, D])
        stats = sb("f_stats", [P, GT, 6])
        mv = sb("f_mv", [P, GT, 2])
        vare = sb("f_vare", [P, GT])
        power = sb("f_power", [P, GT])
        rstd = sb("f_rstd", [P, GT])

        raw_in = sem("f_raw_in")
        power_set = sem("f_power_set")
        coef_o = sem("f_coef_o")
        sig = sem("f_sig")
        alpha_in = sem("f_alpha_in")
        alpha_out = sem("f_alpha_out")
        up_in = sem("f_up_in")
        padded = sem("f_padded")
        bm_high = sem("f_bm_high")
        bm_split = sem("f_bm_split")
        up_high = sem("f_up_high")
        up_split = sem("f_up_split")
        down_high = sem("f_down_high")
        down_split = sem("f_down_split")
        xh_sb = sem("f_xh_sb")
        hf_sb = sem("f_hf_sb")
        hh_sb = sem("f_hh_sb")
        down_in = sem("f_down_in")
        x_in = [sem(f"f_x_in{r}") for r in range(2)]
        silu = sem("f_silu")
        prod = sem("f_prod")
        summed = sem("f_summed")
        norm_o = sem("f_norm_o")
        var_sb = sem("f_var_sb")
        rstd_sb = sem("f_rstd_sb")
        normed = sem("f_normed")
        x_out = [sem(f"f_x_out{r}") for r in range(2)]
        xn_out = sem("f_xn_out")
        turned = sem("f_turned")
        xT_sb = sem("f_xT_sb")
        drive_ps = sem("f_drive_ps")
        drive_sb = sem("f_drive_sb")
        gate_ps = sem("f_gate_ps")
        up_ps = sem("f_up_ps")
        act_sb = sem("f_act_sb")
        h_sb = sem("f_h_sb")
        down_ps = sem("f_down_ps")
        gs_sb = sem("f_gs_sb")
        gs_out = sem("f_gs_out")
        spare = sem("f_spare")

        QB = B // GT
        ROWS = NE * QB

        def tiles(d):
            return d.rearrange("(b j p) d -> j p b d", j=NE, p=P)

        x_v, s_v, a_v, x1_v, xn1_v, g_v = (tiles(d) for d in (x, s0_d, acc_d, x1_d, xn1_d, g_d))

        def at(v, j, q):
            return v[bass.ds(j, 1), :, GT * q:GT * (q + 1), :].rearrange("o p b d -> (o p) b d")

        block = mem.enter_context(nc.Block())

        @block.sync
        def _(sp):
            for c in range(2):
                for n, name in enumerate(("L1_attn_steps_raw", "L1_attn_G_raw", "L1_attn_A_raw")):
                    sp.dma_start(raw[c * PS:(c + 1) * PS, n:n + 1], w[name]).then_inc(raw_in, 16)
            sp.dma_start(bm[:], w["L1_attn_B_mat"]).then_inc(raw_in, 16)
            with sp.Fori(0, NE) as j:
                for q in range(QB):
                    r = q % 2
                    if q == 0:
                        sp.wait_ge(up_split, j + 1)
                        sp.sem_inc(spare, 1)
                        sp.dma_start(w1s[:], w["L1_ffn_w1"][bass.ds(j, 1)].rearrange("o p k n -> p (o k) n")
                                     ).then_inc(up_in, 16)
                        sp.dma_start(w3s[:], w["L1_ffn_w3"][bass.ds(j, 1)].rearrange("o p k n -> p (o k) n")
                                     ).then_inc(up_in, 16)
                    n = (q - 2) // 2 + 1 if q >= 2 else 0
                    sp.wait_ge(x_out[r], 16 * (QB // 2) * j + 16 * n + 16)
                    sp.sem_inc(spare, 1)
                    sp.wait_ge(normed, QB * j + max(q - 1, 0) + 1)
                    sp.sem_inc(spare, 1)
                    for dst, v in ((xg, x_v), (sg, s_v), (ag, a_v)):
                        sp.dma_start(dst[r][:], at(v, j, q)).then_inc(x_in[r], 16)
                    if q == 0:
                        sp.wait_ge(down_split, j + 1)
                        sp.sem_inc(spare, 1)
                        w2j = w["L1_ffn_w2"][bass.ds(j, 1)]
                        sp.dma_start(w2s[:, 0:FC - 1, :], w2j[:, 0:(FC - 1) * P, :].rearrange("o (k p) n -> p (o k) n", p=P)
                                     ).then_inc(down_in, 16)
                        sp.dma_start(w2s[0:width(FC - 1), FC - 1, :], w2j[:, (FC - 1) * P:FF, :].rearrange("o p n -> (o p) n")
                                     ).then_inc(down_in, 16)

        @block.gpsimd
        def _(pool):
            for s in (up_ps, down_ps, summed, xT_sb, normed, up_split, down_split):
                pool.sem_inc(s, 1)
            pool.sem_inc(h_sb, 2)
            for s in (gs_out, xn_out, x_out[0], x_out[1]):
                pool.sem_inc(s, 16)
            for part in w1p + w3p + w2p:
                nc.gpsimd.memset(part[:].bitcast(F32), 0.0).then_inc(padded, 1)
            nc.gpsimd.memset(power[:], -0.5).then_inc(power_set, 1)
            pool.wait_ge(power_set, 1)
            with pool.Fori(0, NE) as j:
                for q in range(QB):
                    r = q % 2
                    g = QB * j + q
                    pool.wait_ge(silu, g + 1)
                    nc.gpsimd.tensor_tensor(sg[r][:], sg[r][:], ag[r][:], ALU.mult).then_inc(prod, 1)
                    pool.wait_ge(var_sb, g + 1)
                    nc.gpsimd.tensor_tensor(rstd[:], vare[:], power[:], ALU.pow).then_inc(rstd_sb, 1)

        @block.vector
        def _(dve):
            o = Order(dve, coef_o)
            st, gd, ad, al = (raw[:, n:n + 1] for n in range(4))
            dve.wait_ge(raw_in, 16 * 7)
            o.link(nc.vector.tensor_scalar(gd, gd, 0.0, None, ALU.max))
            o.link(nc.vector.tensor_scalar(ad, ad, 0.0, None, ALU.max))
            dve.wait_ge(sig, 1)
            o.link(nc.vector.tensor_copy(coef[:, 2:3], st))
            o.link(nc.vector.tensor_tensor(gd, gd, st, ALU.mult))
            o.link(nc.vector.tensor_scalar(gd, gd, 1.0, None, ALU.add))
            o.link(nc.vector.reciprocal(coef[:, 0:1], gd))
            o.link(nc.vector.tensor_tensor(coef[:, 3:4], st, coef[:, 0:1], ALU.mult))
            o.link(nc.vector.tensor_tensor(al, st, coef[:, 3:4], ALU.mult))
            nc.vector.tensor_tensor(al, al, ad, ALU.mult).then_inc(alpha_in, 1)
            dve.wait_ge(alpha_out, 1)
            o.link(nc.vector.reciprocal(gd, st))
            o.link(nc.vector.tensor_scalar(al, al, -1.99, None, ALU.mult))
            o.link(nc.vector.tensor_tensor(coef[:, 1:2], al, gd, ALU.mult))

            def norm(j, q):
                g, r = QB * j + q, q % 2
                o = Order(dve, norm_o, g * (2 * GT))
                dve.wait_ge(prod, g + 1)
                nc.vector.tensor_tensor(xg[r][:], xg[r][:], sg[r][:], ALU.add).then_inc(summed, 1)
                dve.wait_ge(summed, g + 2)
                dve.sem_inc(spare, 1)
                for t in range(GT):
                    o.did(nc.vector.bn_stats(out=stats[:, t, :], in_=xg[r][:, t, :]))
                o.hold(spare)
                for t in range(GT):
                    o.did(nc.vector.bn_aggr(out=mv[:, t, :], in_=stats[:, t, :]))
                o.wait()
                nc.vector.tensor_scalar(vare[:], mv[:, :, 1], EPS, None, ALU.add).then_inc(var_sb, 1)
                dve.wait_ge(rstd_sb, g + 1)
                dve.wait_ge(xn_out, 16 * g + 16)
                dve.wait_ge(turned, g + 1)
                for t in range(GT):
                    last = nc.vector.tensor_scalar(xn[:, t, :], xg[r][:, t, :], mv[:, t, 0:1], rstd[:, t:t + 1],
                                                   ALU.subtract, ALU.mult)
                last.then_inc(normed, 1)

            def low(part, whole, high, **_):
                return nc.vector.tensor_tensor(part, whole, high.bitcast(F32), ALU.subtract)

            def turn(j, q):
                g, r = QB * j + q, q % 2
                dve.wait_ge(xh_sb, g + 1)
                for k in range(KD):
                    last = low(xT[r][1][:, k, :], ps[k][:], xT[r][0][:, k, :])
                last.then_inc(xT_sb, 1)

            def low_h(g, m):
                n = FC * g + m
                dve.wait_ge(hh_sb, n + 1)
                low(hT[1][:, m, :], hf[m % 2][:], hT[0][:, m, :]).then_inc(h_sb, 1)

            dve.wait_ge(bm_high, 1)
            low(bmp[1][:], bm[:], bmp[0][:]).then_inc(bm_split, 1)
            dve.wait_ge(padded, 6)
            LAST = width(FC - 1)

            with dve.Fori(0, NE) as j:
                norm(j, 0)
                dve.wait_ge(up_high, 2 * j + 2)
                dve.wait_ge(up_ps, QB * FC * j + 1)
                low(w1p[1][:, :, 0:FF], w1s[:], w1p[0][:, :, 0:FF])
                low(w3p[1][:, :, 0:FF], w3s[:], w3p[0][:, :, 0:FF]).then_inc(up_split, 1)
                turn(j, 0)
                dve.wait_ge(down_high, 2 * j + 2)
                dve.wait_ge(down_ps, QB * 2 * j + 1)
                low(w2p[1][:, 0:FC - 1, :], w2s[:, 0:FC - 1, :], w2p[0][:, 0:FC - 1, :])
                low(w2p[1][0:LAST, FC - 1, :], w2s[0:LAST, FC - 1, :], w2p[0][0:LAST, FC - 1, :]
                    ).then_inc(down_split, 1)
                for q in range(QB):
                    g = QB * j + q
                    for m in range(FC):
                        n = FC * g + m
                        dve.wait_ge(act_sb, n + 1)
                        dve.wait_ge(up_ps, n + 2)
                        dve.wait_ge(h_sb, n + 1)
                        nc.vector.tensor_tensor(hf[m % 2][:], act_[m % 2][:], ps[4 + m % 2][:], ALU.mult
                                                ).then_inc(hf_sb, 1)
                        if m:
                            low_h(g, m - 1)
                        if m == 2 and q + 1 < QB:
                            norm(j, q + 1)
                    low_h(g, FC - 1)
                    if q + 1 < QB:
                        turn(j, q + 1)

        @block.scalar
        def _(act):
            act.sem_inc(turned, 1)
            act.wait_ge(raw_in, 16 * 7)
            nc.scalar.activation(raw[:, 0:1], raw[:, 0:1], ACT.Sigmoid).then_inc(sig, 1)
            act.wait_ge(alpha_in, 1)
            nc.scalar.activation(raw[:, 3:4], raw[:, 3:4], ACT.Tanh, scale=1.0 / 1.99).then_inc(alpha_out, 1)

            def before(j, q):
                before_silu(j, q)
                before_stores(j, q)

            def before_silu(j, q):
                g, r = QB * j + q, q % 2
                act.wait_ge(x_in[r], 48 * (QB // 2) * j + 48 * (q // 2) + 48)
                nc.scalar.activation(ag[r][:], ag[r][:], ACT.Silu).then_inc(silu, 1)

            def before_stores(j, q):
                g, r = QB * j + q, q % 2
                act.wait_ge(summed, g + 2)
                act.dma_start(at(x1_v, j, q), xg[r][:]).then_inc(x_out[r], 16)
                act.wait_ge(normed, g + 2)
                act.dma_start(at(xn1_v, j, q), xn[:]).then_inc(xn_out, 16)

            def turn(j, q):
                g, r = QB * j + q, q % 2
                act.wait_ge(turned, g + 2)
                for k in range(KD):
                    last = nc.scalar.copy(xT[r][0][:, k, :], ps[k][:])
                last.then_inc(xh_sb, 1)

            def high_h(g, m):
                act.wait_ge(hf_sb, FC * g + m + 1)
                nc.scalar.copy(hT[0][:, m, :], hf[m % 2][:]).then_inc(hh_sb, 1)

            nc.scalar.copy(bmp[0][:], bm[:]).then_inc(bm_high, 1)
            act.wait_ge(padded, 6)
            LAST = width(FC - 1)
            with act.Fori(0, NE) as j:
                before(j, 0)
                act.wait_ge(up_in, 32 * j + 32)
                act.wait_ge(up_ps, QB * FC * j + 1)
                nc.scalar.copy(w1p[0][:, :, 0:FF], w1s[:]).then_inc(up_high, 1)
                nc.scalar.copy(w3p[0][:, :, 0:FF], w3s[:]).then_inc(up_high, 1)
                turn(j, 0)
                act.wait_ge(down_in, 32 * j + 32)
                act.wait_ge(down_ps, QB * 2 * j + 1)
                nc.scalar.copy(w2p[0][:, 0:FC - 1, :], w2s[:, 0:FC - 1, :]).then_inc(down_high, 1)
                nc.scalar.copy(w2p[0][0:LAST, FC - 1, :], w2s[0:LAST, FC - 1, :]).then_inc(down_high, 1)
                for q in range(QB):
                    g = QB * j + q
                    act.wait_ge(coef_o, 11)
                    act.wait_ge(drive_ps, g + 1)
                    nc.scalar.activation(Y[:, GT * q:GT * (q + 1), bass.ds(P * j, P)],
                                         ps[0][:].rearrange("p (b t) -> p b t", b=GT), ACT.Copy,
                                         scale=coef[:, 3:4]).then_inc(drive_sb, 1)
                    for m in range(FC):
                        n = FC * g + m
                        act.wait_ge(gate_ps, n + 1)
                        if m >= 2:
                            act.wait_ge(hf_sb, n - 1)
                        nc.scalar.activation(act_[m % 2][:], ps[2 + m % 2][:], ACT.Silu).then_inc(act_sb, 1)
                        if m:
                            high_h(g, m - 1)
                        if m == 1 and q + 1 < QB:
                            before_silu(j, q + 1)
                    high_h(g, FC - 1)
                    if q + 1 < QB:
                        before_stores(j, q + 1)
                        turn(j, q + 1)
                    act.wait_ge(gs_out, 16 * g + 16)
                    for u in range(2):
                        act.wait_ge(down_ps, 2 * g + u + 2)
                        nc.scalar.activation(gs[:, 2 * u:2 * u + 2, :].rearrange("p t n -> p (t n)"), ps[6 + u][:],
                                             ACT.Silu).then_inc(gs_sb, 1)
                    act.wait_ge(gs_sb, 2 * g + 4)
                    act.dma_start(at(g_v, j, q), gs[:]).then_inc(gs_out, 16)
            act.wait_ge(gs_out, 16 * ROWS + 16)
            act.wait_ge(xn_out, 16 * ROWS + 16)
            for r in range(2):
                act.wait_ge(x_out[r], 16 * (ROWS // 2) + 16)

        @block.tensor
        def _(pe):
            pe.wait_ge(raw_in, 16 * 7)

            def turn(j, q):
                g = QB * j + q
                pe.wait_ge(normed, g + 2)
                pe.wait_ge(drive_sb, g + 1)
                for k in range(KD):
                    for t in range(GT):
                        last = nc.tensor.transpose(ps[k][:, t * P:(t + 1) * P], xn[:, t, k * P:(k + 1) * P], ident[:])
                last.then_inc(turned, 1)

            def product(out, terms):
                pairs = [(a[i], b[j]) for a, b in terms for i, j in ((0, 0), (1, 0), (0, 1))]
                for n, (lhsT, rhs) in enumerate(pairs):
                    last = nc.tensor.matmul(out, lhsT, rhs, start=(n == 0), stop=(n == len(pairs) - 1))
                return last

            pe.wait_ge(bm_split, 1)
            pe.sem_inc(drive_sb, 1)
            pe.sem_inc(gs_sb, 2)
            with pe.Fori(0, NE) as j:
                turn(j, 0)
                for q in range(QB):
                    g, r = QB * j + q, q % 2
                    pe.wait_ge(xT_sb, g + 2)
                    product(ps[0][:], [([v[:, k, :] for v in bmp], [v[:, k, :] for v in xT[r]]) for k in range(KD)]
                            ).then_inc(drive_ps, 1)
                    if q == 0:
                        pe.wait_ge(up_split, j + 2)
                    for m in range(FC):
                        n = FC * g + m
                        if m >= 2:
                            pe.wait_ge(act_sb, n - 1)
                        for wp, bank, s in ((w1p, 2, gate_ps), (w3p, 4, up_ps)):
                            if bank == 4 and m >= 2:
                                pe.wait_ge(hf_sb, n - 1)
                            product(ps[bank + m % 2][:], [([v[:, k, m * P:(m + 1) * P] for v in wp],
                                                           [v[:, k, :] for v in xT[r]]) for k in range(KD)]
                                    ).then_inc(s, 1)
                    if q + 1 < QB:
                        turn(j, q + 1)
                    if q == 0:
                        pe.wait_ge(down_split, j + 2)
                    pe.wait_ge(h_sb, FC * (g + 1) + 2)
                    for u in range(2):
                        pe.wait_ge(gs_sb, 2 * g + u + 1)
                        for t in (2 * u, 2 * u + 1):
                            last = product(ps[6 + u][:, (t % 2) * D:(t % 2 + 1) * D],
                                           [([v[:, m, t * P:(t + 1) * P] for v in hT], [v[:, m, :] for v in w2p])
                                            for m in range(FC)])
                        last.then_inc(down_ps, 1)


def out_phase(nc, ctx, ps, x1_d, xn1_d, g_d, out, w, Y, coef):
    with ExitStack() as mem:
        def sb(name, shape, dt=F32):
            return mem.enter_context(nc.sbuf_tensor(name, shape, dt))

        sem = phase_semaphores(nc, mem)

        NB = B * NBLK
        z = sb("o_z", [P, NB])
        t = sb("o_t", [P, NB])
        zc = sb("o_zc", [P, B, NBLK])
        yc = sb("o_yc", [P, B, NBLK])
        t1 = sb("o_t1", [P, B])
        t2 = sb("o_t2", [P, B])
        qz = sb("o_qz", [P, 2])
        qt = sb("o_qt", [P, 2])
        qy = sb("o_qy", [P, BLK + 1, 2])
        q2 = sb("o_q2", [P, 2])
        cm = sb("o_cm", [P, D])
        dv = sb("o_dv", [P, D])
        yg = [sb(f"o_yg{r}", [P, GN]) for r in range(2)]
        xg = [sb(f"o_x{r}", [P, GT, D]) for r in range(2)]
        ng = [sb(f"o_n{r}", [P, GT, D]) for r in range(2)]
        gg = [sb(f"o_g{r}", [P, GT, D]) for r in range(2)]

        w_in = sem("o_w_in")
        set_up = sem("o_set_up")
        scan_o = sem("o_scan_o")
        scanned = sem("o_scanned")
        x_in = [sem(f"o_x_in{r}") for r in range(2)]
        skip = sem("o_skip")
        yg_sb = sem("o_yg_sb")
        c_ps = sem("o_c_ps")
        s_sb = sem("o_s_sb")
        sg_sb = sem("o_sg_sb")
        o_sb = sem("o_o_sb")
        o_out = [sem(f"o_o_out{r}") for r in range(2)]

        block = mem.enter_context(nc.Block())
        tv = [d.rearrange("(g t p) d -> p (g t) d", t=GT, p=P) for d in (x1_d, xn1_d, g_d, out)]
        Yb = Y[:].rearrange("p b (k i) -> p (b k) i", i=BLK)
        Yc = Y[:].rearrange("p b (k i) -> p b k i", i=BLK)
        m11, m12, step = (coef[:, n:n + 1] for n in range(3))

        @block.sync
        def _(sp):
            sp.dma_start(cm[:], w["L1_attn_C_mat"]).then_inc(w_in, 16)
            sp.dma_start(dv[:], w["L1_attn_D_vec"].to_broadcast([P, D])).then_inc(w_in, 16)
            with sp.Fori(0, NG // 2) as i:
                for r in range(2):
                    sp.wait_ge(o_out[r], 16 * i + 16)
                    for dst, v in zip((xg, ng, gg), tv):
                        sp.dma_start(dst[r][:], v[:, bass.ds(GT * (2 * i + r), GT), :]).then_inc(x_in[r], 16)

        @block.gpsimd
        def _(pool):
            for r in range(2):
                pool.sem_inc(o_out[r], 16)
            nc.gpsimd.memset(qz[:, 0:1], 1.0).then_inc(set_up, 1)
            nc.gpsimd.memset(qz[:, 1:2], 0.0).then_inc(set_up, 1)
            nc.gpsimd.memset(qy[:, 0, 0:1], 0.0).then_inc(set_up, 1)
            nc.gpsimd.memset(qy[:, 0, 1:2], 1.0).then_inc(set_up, 1)
            nc.gpsimd.memset(zc[:, :, 0:1], 0.0).then_inc(set_up, 1)
            nc.gpsimd.memset(yc[:, :, 0:1], 0.0).then_inc(set_up, 1)
            pool.wait_ge(w_in, 32)
            pool.wait_ge(set_up, 6)
            nc.gpsimd.tensor_scalar(cm[PS:2 * PS, :], cm[PS:2 * PS, :], -1.0, None, ALU.mult).then_inc(set_up, 1)
            pool.wait_ge(set_up, 7)
            with pool.Fori(0, NG // 2) as i:
                for r in range(2):
                    g = 2 * i + r
                    pool.wait_ge(x_in[r], 48 * i + 48)
                    nc.gpsimd.tensor_tensor(ng[r][:], ng[r][:], dv[:].unsqueeze(1).to_broadcast([P, GT, D]), ALU.mult
                                            ).then_inc(skip, 1)
                    pool.wait_ge(s_sb, g + 3)
                    nc.gpsimd.tensor_tensor(ng[r][:], ng[r][:], gg[r][:], ALU.mult).then_inc(sg_sb, 1)

        @block.vector
        def _(dve):
            stt = nc.vector.scalar_tensor_tensor
            dve.wait_ge(set_up, 6)
            o = Order(dve, scan_o)
            o.link(nc.vector.tensor_copy(z[:], Yb[:, :, 0]))
            o.link(nc.vector.tensor_scalar(Yb[:, :, 0], z[:], step, None, ALU.mult))

            def powers(o, i):
                a, c = qy[:, bass.ds(i, 1), :], qy[:, bass.ds(i + 1, 1), :]
                a, c = (v.rearrange("p o q -> p (o q)") for v in (a, c))
                o.link(nc.vector.tensor_scalar(qt[:], a, m12, None, ALU.mult))
                o.link(stt(out=qz[:], in0=qz[:], scalar=m11, in1=qt[:], op0=ALU.mult, op1=ALU.add))
                o.link(stt(out=c, in0=qz[:], scalar=step, in1=a, op0=ALU.mult, op1=ALU.add))

            powers(o, 0)
            n0 = o.n
            with dve.Fori(1, BLK) as i:
                oi = Order(dve, scan_o, n0 + 6 * (i - 1))
                was, now = (Yb[:, :, bass.ds(i - 1, 1)].rearrange("p n o -> p (n o)"),
                            Yb[:, :, bass.ds(i, 1)].rearrange("p n o -> p (n o)"))
                oi.link(stt(out=t[:], in0=was, scalar=m12, in1=now, op0=ALU.mult, op1=ALU.add))
                oi.link(stt(out=z[:], in0=z[:], scalar=m11, in1=t[:], op0=ALU.mult, op1=ALU.add))
                oi.link(stt(out=now, in0=z[:], scalar=step, in1=was, op0=ALU.mult, op1=ALU.add))
                powers(oi, i)
            n0 += 6 * (BLK - 1)
            zb = z[:].rearrange("p (b k) -> p b k", k=NBLK)

            def col(v, k):
                return v[:, :, bass.ds(k, 1)].rearrange("p b o -> p (b o)")

            ends = Yc[:, :, :, BLK - 1]
            with dve.Fori(0, NBLK - 1) as k:
                ok = Order(dve, scan_o, n0 + 4 * k)
                ok.did(stt(out=t1[:], in0=col(zc, k), scalar=qz[:, 0:1], in1=col(zb, k), op0=ALU.mult, op1=ALU.add))
                ok.link(stt(out=t2[:], in0=col(zc, k), scalar=qy[:, BLK, 0:1], in1=col(ends, k),
                            op0=ALU.mult, op1=ALU.add))
                ok.did(stt(out=col(zc, k + 1), in0=col(yc, k), scalar=qz[:, 1:2], in1=t1[:],
                           op0=ALU.mult, op1=ALU.add))
                ok.link(stt(out=col(yc, k + 1), in0=col(yc, k), scalar=qy[:, BLK, 1:2], in1=t2[:],
                            op0=ALU.mult, op1=ALU.add))
            n0 += 4 * (NBLK - 1)
            zcf, ycf = (v[:].rearrange("p b k -> p (b k)") for v in (zc, yc))
            with dve.Fori(0, BLK) as i:
                oi = Order(dve, scan_o, n0 + 3 * i)
                now = Yb[:, :, bass.ds(i, 1)].rearrange("p n o -> p (n o)")
                oi.link(nc.vector.tensor_copy(q2[:], qy[:, bass.ds(i + 1, 1), :].rearrange("p o q -> p (o q)")))
                oi.link(stt(out=t[:], in0=zcf, scalar=q2[:, 0:1], in1=now, op0=ALU.mult, op1=ALU.add))
                oi.link(stt(out=now, in0=ycf, scalar=q2[:, 1:2], in1=t[:], op0=ALU.mult, op1=ALU.add))
            dve.sem_inc(scanned, 1)
            with dve.Fori(0, NG // 2) as i:
                for r in range(2):
                    g = 2 * i + r
                    dve.wait_ge(skip, g + 1)
                    dve.wait_ge(c_ps, g + 3)
                    for u in range(2):
                        last = nc.vector.tensor_tensor(
                            ng[r][:, 2 * u:2 * u + 2, :].rearrange("p t n -> p (t n)"), ps[2 * r + u][:],
                            ng[r][:, 2 * u:2 * u + 2, :].rearrange("p t n -> p (t n)"), ALU.add)
                    last.then_inc(s_sb, 1)
                    dve.wait_ge(sg_sb, g + 1)
                    nc.vector.tensor_tensor(ng[r][:], ng[r][:], xg[r][:], ALU.add).then_inc(o_sb, 1)

        @block.scalar
        def _(act):
            act.wait_ge(scanned, 1)
            with act.Fori(0, NG // 2) as i:
                for r in range(2):
                    g = 2 * i + r
                    act.wait_ge(c_ps, g + 1)
                    nc.scalar.copy(yg[r][:], Y[:].rearrange("p b t -> p (b t)")[:, bass.ds(GN * g, GN)]
                                   ).then_inc(yg_sb, 1)
                    act.wait_ge(o_sb, g + 1)
                    act.dma_start(tv[3][:, bass.ds(GT * g, GT), :], ng[r][:]).then_inc(o_out[r], 16)
            for r in range(2):
                act.wait_ge(o_out[r], 16 * (NG // 2) + 16)

        @block.tensor
        def _(pe):
            pe.sem_inc(c_ps, 2)
            pe.sem_inc(s_sb, 2)
            pe.wait_ge(set_up, 7)
            with pe.Fori(0, NG // 2) as i:
                for r in range(2):
                    g = 2 * i + r
                    pe.wait_ge(yg_sb, g + 1)
                    pe.wait_ge(s_sb, g + 1)
                    for q in range(GT):
                        last = nc.tensor.matmul(ps[2 * r + q // 2][:, (q % 2) * D:(q % 2 + 1) * D],
                                                yg[r][:, q * P:(q + 1) * P], cm[:], start=True, stop=True)
                    last.then_inc(c_ps, 1)


def build(nc, a, out):
    def dram(name, shape):
        return nc.dram_tensor(name, shape, F32).ap()

    xn_d = dram("xn_d", (N, D))
    xnT_d = dram("xnT_d", (KD, P, N))
    s0_d = dram("s0_d", (N, D))
    acc_d = dram("acc_d", (N, D))
    left_d = dram("left_d", (2, P))
    x1_d = dram("x1_d", (N, D))
    xn1_d = dram("xn1_d", (N, D))
    g_d = dram("g_d", (N, D))

    with ExitStack() as ctx:
        ps = [ctx.enter_context(nc.psum_tensor(f"ps{i}", [P, 512], F32)) for i in range(8)]
        ident = ctx.enter_context(nc.sbuf_tensor("ident", [P, P], F32))
        with ExitStack() as mem:
            ident_o = ctx.enter_context(nc.semaphore("ident_o"))
            block = mem.enter_context(nc.Block())

            @block.gpsimd
            def _(pool):
                nc.gpsimd.memset(ident[:], 0.0).then_inc(ident_o, 1)
                pool.wait_ge(ident_o, 1)
                nc.gpsimd.affine_select(out=ident[:], in_=ident[:], compare_op=ALU.not_equal, fill=1.0, base=0,
                                        pattern=[[-1, P]], channel_multiplier=1).then_inc(ident_o, 1)
                pool.wait_ge(ident_o, 2)

        with ExitStack() as mem:
            idxT = mem.enter_context(nc.sbuf_tensor("idxT", [P, P, 2], U32))
            gateT = mem.enter_context(nc.sbuf_tensor("gateT", [P, P, 2], F32))
            idxL = mem.enter_context(nc.sbuf_tensor("idxL", [B, NE], U32))
            gateL = mem.enter_context(nc.sbuf_tensor("gateL", [B, NE], F32))
            route_phase(nc, ctx, ps, a["L0_attn_hidden_states"], xn_d, xnT_d, acc_d, left_d,
                        a["L0_ffn_router_w"], ident, idxT, gateT, idxL, gateL)
            experts_phase(nc, ctx, ps, xn_d, acc_d, a["L0_ffn_w1"], a["L0_ffn_b1"], a["L0_ffn_w2"], a["L0_ffn_b2"],
                          ident, idxT, gateT, idxL, gateL)
        recurrence_phase(nc, ctx, ps, xnT_d, s0_d, ident, a)
        with ExitStack() as mem:
            Y = mem.enter_context(nc.sbuf_tensor("Y", [P, B, T], F32))
            coef = mem.enter_context(nc.sbuf_tensor("coef", [P, 4], F32))
            layer1_phase(nc, ctx, ps, a["L0_attn_hidden_states"], s0_d, acc_d, x1_d, xn1_d, g_d, ident, a, Y, coef)
            out_phase(nc, ctx, ps, x1_d, xn1_d, g_d, out, a, Y, coef)


INS = {
    "L0_attn_hidden_states": lambda a: a.reshape(N, D),
    "L0_ffn_router_w": lambda a: a.T.reshape(KD, P, NE).transpose(1, 0, 2),
    "L0_attn_x_proj_mu": lambda a: a.reshape(KD, P).T,
    "L0_attn_xl_w1": lambda a: a.T.reshape(KD, P, RANK).transpose(1, 0, 2),
    "L0_attn_xl_w2": lambda a: a.T,
    "L0_attn_xl_b2": lambda a: a.reshape(NMU * RANK, 1),
    "L0_attn_x_out_w": lambda a: a.T,
    "L0_attn_x_bias": lambda a: a.reshape(NMU, KD, P).transpose(2, 0, 1),
    "L0_attn_r_w": lambda a: a.T.reshape(KD, P, KW).transpose(1, 0, 2),
    "L0_attn_w_w1": lambda a: a.T.reshape(KD, P, GATE).transpose(1, 0, 2),
    "L0_attn_w_w2": lambda a: a.T,
    "L0_attn_w_b": lambda a: a.reshape(KW, 1),
    "L0_attn_k_w": lambda a: a.T.reshape(KD, P, KW).transpose(1, 0, 2),
    "L0_attn_v_w": lambda a: a.T.reshape(KD, P, VW).transpose(1, 0, 2),
    "L0_attn_g_w": lambda a: a.T.reshape(KD, P, VW).transpose(1, 0, 2),
    "L0_attn_bonus": lambda a: a.reshape(KW, 1),
    "L0_attn_gn_weight": lambda a: a.reshape(1, VW),
    "L0_attn_gn_bias": lambda a: a.reshape(1, VW),
    "L0_attn_o_w": lambda a: a.T.reshape(KD, P, D).transpose(1, 0, 2),
    "L0_ffn_w1": lambda a: a.reshape(NE, KD, P, HID).transpose(0, 2, 1, 3),
    "L0_ffn_b1": lambda a: a.reshape(NE, HC, P).transpose(0, 2, 1),
    "L0_ffn_w2": lambda a: a.reshape(NE, HC, P, D).transpose(0, 2, 1, 3),
    "L0_ffn_b2": lambda a: a.reshape(NE, 1, D),
    "L1_attn_steps_raw": lambda a: a.reshape(PS, 1),
    "L1_attn_G_raw": lambda a: a.reshape(PS, 1),
    "L1_attn_A_raw": lambda a: a.reshape(PS, 1),
    "L1_attn_B_mat": lambda a: a.transpose(1, 2, 0).reshape(KD, P, 2 * PS).transpose(1, 0, 2),
    "L1_attn_C_mat": lambda a: a.transpose(2, 1, 0).reshape(2 * PS, D),
    "L1_attn_D_vec": lambda a: a.reshape(1, D),
    "L1_ffn_w1": lambda a: a.reshape(NE, KD, P, FF).transpose(0, 2, 1, 3),
    "L1_ffn_w3": lambda a: a.reshape(NE, KD, P, FF).transpose(0, 2, 1, 3),
    "L1_ffn_w2": lambda a: a,
}


def kernel(**inputs):
    import numpy as np
    import concourse.bacc as bacc
    from concourse.bass_utils import run_bass_kernel_spmd

    nc = bacc.Bacc("TRN2", target_bir_lowering=False, num_devices=1)
    arrays, args = {}, {}
    for name, lay in INS.items():
        a = np.ascontiguousarray(lay(np.asarray(inputs[name])))
        arrays[f"in_{name}"] = a
        args[name] = nc.dram_tensor(f"in_{name}", a.shape, mybir.dt.from_np(a.dtype), kind="ExternalInput").ap()
    out = nc.dram_tensor("out_0", (N, D), F32, kind="ExternalOutput").ap()
    build(nc, args, out)
    r = run_bass_kernel_spmd(nc, [arrays], core_ids=[0])
    return r.results[0]["out_0"].reshape(B, T, D)
```

```python
from contextlib import ExitStack

import concourse.bass as bass
from concourse import mybir

ALU = mybir.AluOpType
ACT = mybir.ActivationFunctionType
F32 = mybir.dt.float32
F32R = mybir.dt.float32r
U32 = mybir.dt.uint32
I32 = mybir.dt.int32
AX_X = mybir.AxisListType.X

P = 128
B, T, D = 16, 1024, 256
N = B * T
KD = D // P
GT = 4
GN = GT * P
NG = N // GN
HALVES = T // GN
EPS = 1e-5

NH, KW, VW = 4, 128, 256
DK, DV = KW // NH, VW // NH
NMU, RANK, GATE = 5, 32, 64
LEVELS = 7

NE, HID = 8, 1024
HC = HID // P
CAP = T * 2 // NE + 1
ROUNDS = (CAP + 7) // 8
QN = B // 2

PS = 64
FF = 704
FC = (FF + P - 1) // P
BLK = 32
NBLK = T // BLK


def width(m):
    return min(P, FF - m * P)


class Order:

    def __init__(self, eng, sem, base=0):
        self.eng, self.sem, self.base, self.n = eng, sem, base, 0

    def did(self, ins):
        self.n += 1
        ins.then_inc(self.sem, 1)

    def wait(self):
        self.eng.wait_ge(self.sem, self.base + self.n)

    def hold(self, spare):
        self.wait()
        self.eng.sem_inc(spare, 1)

    def link(self, ins):
        self.did(ins)
        self.wait()


def phase_semaphores(nc, mem):
    taken = []

    def give_back():
        nc.all_engine_barrier()
        nc.clear_and_free_semaphores(taken)
        nc.all_engine_barrier()

    def sem(name):
        taken.append(nc.alloc_semaphore(name=name))
        return taken[-1]

    mem.callback(give_back)
    return sem


def route_phase(nc, ctx, ps, x, xn_d, xnT_d, acc_d, left_d, router_w, ident, idxT, gateT, idxL, gateL):
    with ExitStack() as mem:
        def sb(name, shape, dt=F32):
            return mem.enter_context(nc.sbuf_tensor(name, shape, dt))

        sem = phase_semaphores(nc, mem)

        xg = [sb(f"r_x{r}", [P, GT, D]) for r in range(2)]
        xn = [sb(f"r_xn{r}", [P, GT, D]) for r in range(2)]
        xT = [sb(f"r_xT{r}", [P, KD, GN]) for r in range(2)]
        stats = sb("r_stats", [P, GT, 6])
        mv = sb("r_mv", [P, GT, 2])
        vare = sb("r_vare", [P, GT])
        power = sb("r_power", [P, GT])
        rstd = sb("r_rstd", [P, GT])
        wr = sb("r_wr", [P, KD, NE])
        zeros = sb("r_zeros", [P, 2048])
        logit = sb("r_logit", [P, N // P, NE])
        prob = sb("r_prob", [P, T // P, NE, B])
        red = sb("r_red", [P, N // P])
        score = [sb(f"r_score{r}", [P, T]) for r in range(1)]
        v8 = sb("r_v8", [P, 8])
        i8 = sb("r_i8", [P, 8], U32)
        vals = sb("r_vals", [P, ROUNDS * 8])
        idxf = sb("r_idxf", [P, ROUNDS * 8])
        rowi = sb("r_rowi", [P, 1], I32)
        rowb = sb("r_rowb", [P, 1], I32)
        rowf = sb("r_rowf", [P, 1])
        leftf = sb("r_leftf", [B, NE])

        x_in = [sem(f"r_x_in{r}") for r in range(2)]
        x_free = sem("r_x_free")
        xn_out = [sem(f"r_xn_out{r}") for r in range(2)]
        xT_out = [sem(f"r_xT_out{r}") for r in range(2)]
        normed = sem("r_normed")
        turned = sem("r_turned")
        xT_sb = sem("r_xT_sb")
        routed = sem("r_routed")
        logit_sb = sem("r_logit_sb")
        w_in = sem("r_w_in")
        zeroed = sem("r_zeroed")
        acc_out = sem("r_acc_out")
        iota_done = sem("r_iota_done")
        dve_o = sem("r_dve_o")
        top_o = sem("r_top_o")
        centred = sem("r_centred")
        exped = sem("r_exped")
        soft = sem("r_soft")
        score_t = sem("r_score_t")
        topped = sem("r_topped")
        idx_t = sem("r_idx_t")
        left_out = sem("r_left_out")
        left_in = sem("r_left_in")
        idx_done = sem("r_idx_done")
        spare = sem("r_spare")
        var_ready = sem("r_var_ready")
        rstd_ready = sem("r_rstd_ready")

        x_v = x.rearrange("(g t p) d -> p (g t) d", t=GT, p=P)
        xn_v = xn_d.rearrange("(g t p) d -> p (g t) d", t=GT, p=P)
        xT_v = xnT_d.rearrange("k p n -> p k n")
        acc_v = acc_d.rearrange("(a p c) d -> a p (c d)", p=P, c=8)

        block = mem.enter_context(nc.Block())

        @block.sync
        def _(sp):
            sp.dma_start(wr[:], router_w).then_inc(w_in, 16)
            with sp.Fori(0, NG // 2) as i:
                for r in range(2):
                    sp.wait_ge(x_free, 2 * i + r + 1)
                    sp.dma_start(xg[r][:], x_v[:, bass.ds(GT * (2 * i + r), GT), :]).then_inc(x_in[r], 16)
            sp.wait_ge(topped, 1)
            sp.dma_start(left_d[0:1, :].rearrange("o p -> p o"), idxf[:, CAP - 1:CAP]).then_inc(left_out, 16)
            sp.dma_start(left_d[1:2, :].rearrange("o p -> p o"), vals[:, CAP - 1:CAP]).then_inc(left_out, 16)
            sp.wait_ge(left_out, 32)
            with nc.allow_non_contiguous_dma("256 words"):
                sp.dma_start(leftf[:], left_d[0, :].rearrange("(e b) -> b e", b=B)).then_inc(left_in, 16)
                sp.dma_start(gateL[:], left_d[1, :].rearrange("(e b) -> b e", b=B)).then_inc(left_in, 16)
            sp.wait_ge(left_in, 32)

        @block.gpsimd
        def _(pool):
            nc.gpsimd.iota(rowi[:], pattern=[[0, 1]], base=0, channel_multiplier=1).then_inc(iota_done, 1)
            nc.gpsimd.memset(zeros[:], 0.0).then_inc(zeroed, 1)
            pool.wait_ge(zeroed, 1)
            for a in range(N // (P * 8)):
                pool.dma_start(acc_v[a], zeros[:]).then_inc(acc_out, 16)
            nc.gpsimd.memset(power[:], -0.5).then_inc(zeroed, 1)
            pool.wait_ge(zeroed, 2)
            with pool.Fori(0, NG) as it:
                pool.wait_ge(var_ready, it + 1)
                nc.gpsimd.tensor_tensor(rstd[:], vare[:], power[:], ALU.pow).then_inc(rstd_ready, 1)
            pool.wait_ge(acc_out, 16 * (N // (P * 8)))

        @block.vector
        def _(dve):
            dve.sem_inc(x_free, 2)
            with dve.Fori(0, NG // 2) as i:
                for r in range(2):
                    it = 2 * i + r
                    o = Order(dve, dve_o, it * (3 * GT))
                    dve.wait_ge(x_in[r], 16 * i + 16)
                    dve.wait_ge(xn_out[r], 16 * i + 16)
                    dve.wait_ge(turned, it + 1)
                    for t in range(GT):
                        o.did(nc.vector.bn_stats(out=stats[:, t, :], in_=xg[r][:, t, :]))
                    o.hold(spare)
                    for t in range(GT):
                        o.did(nc.vector.bn_aggr(out=mv[:, t, :], in_=stats[:, t, :]))
                    o.wait()
                    nc.vector.tensor_scalar(vare[:], mv[:, :, 1], EPS, None, ALU.add).then_inc(var_ready, 1)
                    dve.wait_ge(rstd_ready, it + 1)
                    for t in range(GT):
                        last = nc.vector.tensor_scalar(xn[r][:, t, :], xg[r][:, t, :], mv[:, t, 0:1], rstd[:, t:t + 1],
                                                       ALU.subtract, ALU.mult)
                        o.did(last)
                    o.wait()
                    nc.vector.sem_inc(x_free, 1)
                    nc.vector.sem_inc(normed, 1)
            o = Order(dve, top_o)
            dve.wait_ge(logit_sb, NG + 2)
            o.link(nc.vector.tensor_reduce(red[:], logit[:], AX_X, ALU.max))
            nc.vector.tensor_tensor(logit[:], logit[:], red[:].unsqueeze(2).to_broadcast([P, N // P, NE]),
                                    ALU.subtract).then_inc(centred, 1)
            dve.wait_ge(exped, 1)
            o.link(nc.vector.tensor_reduce(red[:], logit[:], AX_X, ALU.add))
            o.link(nc.vector.reciprocal(red[:], red[:]))
            nc.vector.tensor_tensor(prob[:].rearrange("p j e b -> p b j e"),
                                    logit[:].rearrange("p (b j) e -> p b j e", b=B),
                                    red[:].rearrange("p (b j) -> p b j", b=B).unsqueeze(3)
                                    .to_broadcast([P, B, T // P, NE]), ALU.mult).then_inc(soft, 1)
            dve.wait_ge(score_t, 1)
            for h in range(2):
                o.did(nc.vector.tensor_copy(score[0][:, h * 512:(h + 1) * 512], ps[h][:]))
            o.wait()
            base = o.n
            with dve.Fori(0, ROUNDS) as k:
                oo = Order(dve, top_o, base + 5 * k)
                oo.did(nc.vector.max(v8[:], score[0][:]))
                oo.hold(spare)
                oo.did(nc.vector.max_index(i8[:], v8[:], score[0][:]))
                oo.hold(spare)
                oo.did(nc.vector.match_replace(score[0][:], v8[:], score[0][:], -1.0))
                oo.did(nc.vector.tensor_copy(vals[:, bass.ds(8 * k, 8)], v8[:]))
                oo.did(nc.vector.tensor_copy(idxf[:, bass.ds(8 * k, 8)], i8[:]))
                oo.wait()
            o.n = base + 5 * ROUNDS
            dve.wait_ge(iota_done, 1)
            o.link(nc.vector.tensor_scalar(rowb[:], rowi[:], B - 1, None, ALU.bitwise_and))
            o.link(nc.vector.tensor_scalar(rowf[:], rowb[:], float(T), None, ALU.mult))
            nc.vector.tensor_scalar(idxf[:], idxf[:], rowf[:, 0:1], None, ALU.add).then_inc(topped, 1)
            dve.wait_ge(idx_t, 1)
            for h in range(2):
                nc.vector.tensor_copy(idxT[:, :, h], ps[2 + h][:, 0:P])
                last = nc.vector.tensor_copy(gateT[:, :, h], ps[4 + h][:, 0:P])
            last.then_inc(idx_done, 1)
            dve.wait_ge(left_in, 32)
            nc.vector.tensor_copy(idxL[:], leftf[:]).then_inc(idx_done, 1)
            dve.wait_ge(idx_done, 2)

        @block.scalar
        def _(act):
            act.sem_inc(xT_sb, 4)
            act.sem_inc(logit_sb, 2)
            for r in range(2):
                act.sem_inc(xn_out[r], 16)
                act.sem_inc(xT_out[r], 16)
            with act.Fori(0, NG // 2) as i:
                for r in range(2):
                    it = 2 * i + r
                    act.wait_ge(normed, it + 1)
                    act.dma_start(xn_v[:, bass.ds(GT * it, GT), :], xn[r][:]).then_inc(xn_out[r], 16)
                    act.wait_ge(turned, it + 3)
                    act.wait_ge(xT_out[r], 16 * i + 16)
                    act.wait_ge(routed, it + 1)
                    for k in range(KD):
                        nc.scalar.copy(xT[r][:, k, :], ps[2 * r + k][:]).then_inc(xT_sb, 1)
                    act.wait_ge(xT_sb, 4 + 2 * (it + 1))
                    act.dma_start(xT_v[:, :, bass.ds(GN * it, GN)], xT[r][:]).then_inc(xT_out[r], 16)
                    act.wait_ge(routed, 2 + it + 1)
                    nc.scalar.copy(logit[:, bass.ds(GT * it, GT), :],
                                   ps[4 + r][:, 0:GT * NE].rearrange("p (t e) -> p t e", t=GT)).then_inc(logit_sb, 1)
            act.wait_ge(centred, 1)
            nc.scalar.activation(logit[:], logit[:], ACT.Exp).then_inc(exped, 1)
            for r in range(2):
                act.wait_ge(xn_out[r], 16 * (NG // 2) + 16)
                act.wait_ge(xT_out[r], 16 * (NG // 2) + 16)

        @block.tensor
        def _(pe):
            pe.sem_inc(routed, 2)
            pe.sem_inc(turned, 2)
            pe.wait_ge(w_in, 16)
            with pe.Fori(0, NG // 2) as i:
                for r in range(2):
                    it = 2 * i + r
                    pe.wait_ge(normed, it + 1)
                    pe.wait_ge(xT_sb, 2 * it + 2)
                    for k in range(KD):
                        for t in range(GT):
                            last = nc.tensor.transpose(ps[2 * r + k][:, t * P:(t + 1) * P],
                                                       xn[r][:, t, k * P:(k + 1) * P], ident[:])
                    last.then_inc(turned, 1)
                    pe.wait_ge(xT_sb, 4 + 2 * (it + 1))
                    pe.wait_ge(logit_sb, it + 1)
                    for t in range(GT):
                        for k in range(KD):
                            last = nc.tensor.matmul(ps[4 + r][:, t * NE:(t + 1) * NE], xT[r][:, k, t * P:(t + 1) * P],
                                                    wr[:, k, :], start=(k == 0), stop=(k == KD - 1))
                    last.then_inc(routed, 1)
            pe.wait_ge(soft, 1)
            for j in range(T // P):
                last = nc.tensor.transpose(ps[j // 4][:, (j % 4) * P:(j % 4 + 1) * P], prob[:, j].rearrange("p e b -> p (e b)"), ident[:])
            last.then_inc(score_t, 1)
            pe.wait_ge(topped, 1)
            for h in range(2):
                nc.tensor.transpose(ps[2 + h][:, 0:P], idxf[:, h * P:(h + 1) * P], ident[:])
                last = nc.tensor.transpose(ps[4 + h][:, 0:P], vals[:, h * P:(h + 1) * P], ident[:])
            last.then_inc(idx_t, 1)


def experts_phase(nc, ctx, ps, xn_d, acc_d, w1, b1, w2, b2, ident, idxT, gateT, idxL, gateL):
    with ExitStack() as mem:
        def sb(name, shape, dt=F32):
            return mem.enter_context(nc.sbuf_tensor(name, shape, dt))

        sem = phase_semaphores(nc, mem)

        w1s = sb("e_w1", [P, KD, HID])
        w2s = sb("e_w2", [P, HC, D])
        w1p = [sb(f"e_w1{n}", [P, KD, HID], F32R) for n in "hl"]
        w2p = [sb(f"e_w2{n}", [P, HC, D], F32R) for n in "hl"]
        b1i = sb("e_b1i", [P, HC])
        b2i = sb("e_b2i", [P, D])
        b1s = sb("e_b1", [P, HC])
        b2s = sb("e_b2", [P, D])
        ids = sb("e_ids", [P, 2 * B], U32)
        idl = sb("e_idl", [B, 1], U32)
        gts = sb("e_gts", [P, 2 * B])
        gtl = sb("e_gtl", [B, 1])
        xg = [sb(f"e_x{r}", [P, GT, D]) for r in range(2)]
        xT = [[sb(f"e_xT{n}{r}", [P, KD, GN], F32R) for n in "hl"] for r in range(2)]
        hf = [sb(f"e_hf{r}", [P, GN]) for r in range(2)]
        hT = [sb(f"e_hT{n}", [P, HC, GN], F32R) for n in "hl"]
        ys = [sb(f"e_y{r}", [P, GT, D]) for r in range(2)]
        xl = sb("e_xl", [B, D])
        xTl = [sb(f"e_xTl{n}", [P, KD, B], F32R) for n in "hl"]
        hfl = sb("e_hfl", [P, HC, B])
        hTl = [sb(f"e_hTl{n}", [P, HC, P], F32R) for n in "hl"]
        yl = sb("e_yl", [B, D])

        up_in = sem("e_up_in")
        up_split = sem("e_up_split")
        down_split = sem("e_down_split")
        w1h_set = sem("e_w1h_set")
        w2h_set = sem("e_w2h_set")
        padded = sem("e_padded")
        xh_sb = sem("e_xh_sb")
        hi_sb = sem("e_hi_sb")
        down_in = sem("e_down_in")
        ids_set = sem("e_ids_set")
        gts_set = sem("e_gts_set")
        x_in = [sem(f"e_x_in{r}") for r in range(3)]
        turned = sem("e_turned")
        xT_sb = sem("e_xT_sb")
        up_ps = sem("e_up_ps")
        h_sb = sem("e_h_sb")
        down_ps = sem("e_down_ps")
        y_sum = sem("e_y_sum")
        y_sb = sem("e_y_sb")
        y_out = [sem(f"e_y_out{r}") for r in range(3)]
        spare = sem("e_spare")

        GR = QN + 1
        UP = QN * HC + 1
        DOWN = QN * 2 + 1
        HS = QN * HC + HC
        YS = QN * 2 + 1

        block = mem.enter_context(nc.Block())

        @block.sync
        def _(sp):
            with sp.Fori(0, NE) as e:
                sp.wait_ge(up_split, e + 1)
                sp.sem_inc(spare, 1)
                sp.dma_start(w1s[:], w1[bass.ds(e, 1)].rearrange("o p k n -> p (o k) n")).then_inc(up_in, 16)
                sp.dma_start(b1i[:], b1[bass.ds(e, 1)].rearrange("o p n -> p (o n)")).then_inc(up_in, 16)
                sp.wait_ge(down_split, e + 1)
                sp.sem_inc(spare, 1)
                sp.dma_start(w2s[:], w2[bass.ds(e, 1)].rearrange("o p k n -> p (o k) n")).then_inc(down_in, 16)
                sp.dma_start(b2i[:], b2[bass.ds(e, 1)].rearrange("o q n -> (o q) n").to_broadcast([P, D])
                             ).then_inc(down_in, 16)

        @block.gpsimd
        def _(pool):
            for s in (up_ps, h_sb, down_ps, y_sum, up_split, down_split):
                pool.sem_inc(s, 1)
            for part in hTl:
                nc.gpsimd.memset(part[:].bitcast(F32), 0.0).then_inc(padded, 1)
            pool.sem_inc(y_sb, 1)

            def gather(e, q):
                r = q % 2
                pool.wait_ge(turned, GR * e + (q - 1 if q >= 2 else 0) + 1)
                pool.sem_inc(spare, 1)
                for t in range(GT):
                    pool.indirect_dma_start(
                        xg[r][:, t, :], None, xn_d,
                        bass.IndirectOffsetOnAxis(ap=ids[:, GT * q + t:GT * q + t + 1], axis=0)).then_inc(x_in[r], 16)

            def scatter(e, q):
                r = q % 2
                pool.wait_ge(y_sb, YS * e + 2 * (q + 1) + 1)
                pool.sem_inc(spare, 1)
                for t in range(GT):
                    pool.indirect_dma_start(
                        acc_d, bass.IndirectOffsetOnAxis(ap=ids[:, GT * q + t:GT * q + t + 1], axis=0),
                        ys[r][:, t, :], None, compute_op=ALU.add).then_inc(y_out[r], 16)

            with pool.Fori(0, NE) as e:
                nc.gpsimd.tensor_copy(ids[:], idxT[:, bass.ds(B * e, B), :].rearrange("p a b -> p (a b)")
                                      ).then_inc(ids_set, 1)
                nc.gpsimd.tensor_copy(idl[:], idxL[:, bass.ds(e, 1)]).then_inc(ids_set, 1)
                pool.wait_ge(ids_set, 2 * e + 2)
                gather(e, 0)
                pool.indirect_dma_start(xl[:], None, xn_d, bass.IndirectOffsetOnAxis(ap=idl[:, 0:1], axis=0)
                                        ).then_inc(x_in[2], 16)
                for q in range(QN):
                    if q + 1 < QN:
                        gather(e, q + 1)
                    scatter(e, q)
                pool.wait_ge(y_sb, YS * (e + 1) + 1)
                pool.sem_inc(spare, 1)
                pool.indirect_dma_start(acc_d, bass.IndirectOffsetOnAxis(ap=idl[:, 0:1], axis=0), yl[:], None,
                                        compute_op=ALU.add).then_inc(y_out[2], 16)
                for r in range(2):
                    pool.wait_ge(y_out[r], 32 * QN * (e + 1))
                pool.wait_ge(y_out[2], 16 * (e + 1))

        @block.scalar
        def _(act):
            def turn(e, q):
                r = q % 2
                act.wait_ge(turned, GR * e + q + 2)
                for k in range(KD):
                    last = nc.scalar.copy(xT[r][0][:, k, :], ps[k][:])
                last.then_inc(xh_sb, 1)

            act.wait_ge(padded, 2)
            with act.Fori(0, NE) as e:
                act.wait_ge(up_ps, UP * e + 1)
                act.wait_ge(h_sb, HS * e + 1)
                act.wait_ge(up_in, 32 * e + 32)
                nc.scalar.copy(w1p[0][:], w1s[:]).then_inc(w1h_set, 1)
                nc.scalar.copy(b1s[:], b1i[:]).then_inc(w1h_set, 1)
                turn(e, 0)
                act.wait_ge(down_ps, DOWN * e + 1)
                act.wait_ge(down_in, 32 * e + 32)
                nc.scalar.copy(w2p[0][:], w2s[:]).then_inc(w2h_set, 1)
                act.wait_ge(w1h_set, 2 * e + 2)
                for q in range(QN):
                    for m in range(HC):
                        act.wait_ge(up_ps, UP * e + HC * q + m + 2)
                        n = HC * q + m - 2
                        act.wait_ge(h_sb, HS * e + (n + 1 if n >= 0 else 0) + 1)
                        nc.scalar.activation(hf[m % 2][:], ps[2 + m % 2][:], ACT.Gelu, bias=b1s[:, m:m + 1])
                        nc.scalar.activation(hT[0][:, m, :], ps[2 + m % 2][:], ACT.Gelu, bias=b1s[:, m:m + 1]
                                             ).then_inc(hi_sb, 1)
                    if q + 1 < QN:
                        turn(e, q + 1)
                    else:
                        act.wait_ge(turned, GR * (e + 1) + 1)
                        nc.scalar.copy(xTl[0][:], ps[0][:, 0:KD * B].rearrange("p (k n) -> p k n", k=KD)
                                       ).then_inc(xh_sb, 1)
                act.wait_ge(up_ps, UP * (e + 1) + 1)
                for m in range(HC):
                    z = ps[2][:, m * B:(m + 1) * B]
                    nc.scalar.activation(hfl[:, m, :], z, ACT.Gelu, bias=b1s[:, m:m + 1])
                    nc.scalar.activation(hTl[0][:, m, 0:B], z, ACT.Gelu, bias=b1s[:, m:m + 1]).then_inc(hi_sb, 1)

        @block.vector
        def _(dve):
            def turn(e, q):
                r = q % 2
                dve.wait_ge(xh_sb, GR * e + q + 1)
                for k in range(KD):
                    nc.vector.tensor_tensor(xT[r][1][:, k, :], ps[k][:], xT[r][0][:, k, :].bitcast(F32), ALU.subtract
                                            ).then_inc(xT_sb, 1)

            def low_parts(e, q):
                for m in range(HC):
                    dve.wait_ge(hi_sb, HS * e + HC * q + m + 1)
                    nc.vector.tensor_tensor(hT[1][:, m, :], hf[m % 2][:], hT[0][:, m, :].bitcast(F32), ALU.subtract
                                            ).then_inc(h_sb, 1)

            def result(e, q):
                r = q % 2
                if q >= 2:
                    dve.wait_ge(y_out[r], 32 * QN * e + 64 * (q // 2))
                for h in range(2):
                    dve.wait_ge(down_ps, DOWN * e + 2 * q + h + 2)
                    nc.vector.tensor_tensor(ys[r][:, 2 * h:2 * h + 2, :],
                                            ps[4 + 2 * r + h][:].rearrange("p (t n) -> p t n", t=2),
                                            b2s[:].unsqueeze(1).to_broadcast([P, 2, D]), ALU.add).then_inc(y_sum, 1)
                dve.wait_ge(y_sum, YS * e + 2 * q + 3)
                for t in range(GT):
                    last = nc.vector.tensor_scalar(ys[r][:, t, :], ys[r][:, t, :], gts[:, GT * q + t:GT * q + t + 1],
                                                   None, ALU.mult)
                    if t % 2:
                        last.then_inc(y_sb, 1)

            with dve.Fori(0, NE) as e:
                dve.wait_ge(ids_set, 2 * e + 2)
                dve.wait_ge(y_sb, YS * e + 1)
                dve.wait_ge(y_sum, YS * e + 1)
                dve.wait_ge(down_in, 32 * e + 32)
                dve.wait_ge(up_ps, UP * e + 1)
                dve.wait_ge(down_ps, DOWN * e + 1)
                nc.vector.tensor_copy(gts[:], gateT[:, bass.ds(B * e, B), :].rearrange("p a b -> p (a b)")
                                      ).then_inc(gts_set, 1)
                nc.vector.tensor_copy(gtl[:], gateL[:, bass.ds(e, 1)]).then_inc(gts_set, 1)
                nc.vector.tensor_copy(b2s[:], b2i[:]).then_inc(gts_set, 1)
                dve.wait_ge(gts_set, 3 * e + 3)
                dve.wait_ge(w1h_set, 2 * e + 2)
                nc.vector.tensor_tensor(w1p[1][:], w1s[:], w1p[0][:].bitcast(F32), ALU.subtract).then_inc(up_split, 1)
                turn(e, 0)
                dve.wait_ge(w2h_set, e + 1)
                nc.vector.tensor_tensor(w2p[1][:], w2s[:], w2p[0][:].bitcast(F32), ALU.subtract
                                        ).then_inc(down_split, 1)
                for q in range(QN):
                    low_parts(e, q)
                    if q + 1 < QN:
                        turn(e, q + 1)
                    else:
                        dve.wait_ge(xh_sb, GR * (e + 1))
                        nc.vector.tensor_tensor(xTl[1][:], ps[0][:, 0:KD * B].rearrange("p (k n) -> p k n", k=KD),
                                                xTl[0][:].bitcast(F32), ALU.subtract).then_inc(xT_sb, 2)
                    result(e, q)
                dve.wait_ge(hi_sb, HS * (e + 1))
                nc.vector.tensor_tensor(hTl[1][:, :, 0:B], hfl[:], hTl[0][:, :, 0:B].bitcast(F32), ALU.subtract
                                        ).then_inc(h_sb, HC)
                dve.wait_ge(down_ps, DOWN * (e + 1) + 1)
                nc.vector.tensor_tensor(yl[:], ps[4][0:B, 0:D], b2s[0:B, :], ALU.add).then_inc(y_sum, 1)
                dve.wait_ge(y_sum, YS * (e + 1) + 1)
                nc.vector.tensor_scalar(yl[:], yl[:], gtl[:, 0:1], None, ALU.mult).then_inc(y_sb, 1)

        @block.tensor
        def _(pe):
            pe.sem_inc(turned, 1)
            pe.sem_inc(xT_sb, 2)

            def turn(e, q):
                r = q % 2
                pe.wait_ge(x_in[r], 32 * QN * e + 64 * (q // 2) + 64)
                pe.wait_ge(xT_sb, 2 * GR * e + 2 * q + 2)
                for k in range(KD):
                    for t in range(GT):
                        last = nc.tensor.transpose(ps[k][:, t * P:(t + 1) * P], xg[r][:, t, k * P:(k + 1) * P],
                                                   ident[:])
                last.then_inc(turned, 1)

            def turn_last(e):
                pe.wait_ge(x_in[2], 16 * e + 16)
                pe.wait_ge(xT_sb, 2 * GR * e + 2 * QN + 2)
                pe.sem_inc(spare, 1)
                for k in range(KD):
                    last = nc.tensor.transpose(ps[0][:, k * B:(k + 1) * B], xl[:, k * P:(k + 1) * P], ident[0:B, 0:B])
                last.then_inc(turned, 1)

            def product(out, terms):
                pairs = [(a[i], b[j]) for a, b in terms for i, j in ((0, 0), (1, 0), (0, 1))]
                for n, (lhsT, rhs) in enumerate(pairs):
                    last = nc.tensor.matmul(out, lhsT, rhs, start=(n == 0), stop=(n == len(pairs) - 1))
                return last

            pe.wait_ge(padded, 2)
            with pe.Fori(0, NE) as e:
                turn(e, 0)
                pe.wait_ge(up_split, e + 2)
                for q in range(QN):
                    r = q % 2
                    pe.wait_ge(xT_sb, 2 * GR * e + 2 * (q + 1) + 2)
                    for m in range(HC):
                        n = HC * q + m - 2
                        pe.wait_ge(h_sb, HS * e + (n + 1 if n >= 0 else 0) + 1)
                        product(ps[2 + m % 2][:], [([w[:, k, m * P:(m + 1) * P] for w in w1p],
                                                    [v[:, k, :] for v in xT[r]]) for k in range(KD)]
                                ).then_inc(up_ps, 1)
                    if q + 1 < QN:
                        turn(e, q + 1)
                    else:
                        turn_last(e)
                    if q == 0:
                        pe.wait_ge(down_split, e + 2)
                    pe.wait_ge(h_sb, HS * e + HC * (q + 1) + 1)
                    for h in range(2):
                        n = 2 * (q - 2) + h
                        pe.wait_ge(y_sum, YS * e + (n + 1 if n >= 0 else 0) + 1)
                        for t in (2 * h, 2 * h + 1):
                            last = product(ps[4 + 2 * r + h][:, (t % 2) * D:(t % 2 + 1) * D],
                                           [([v[:, m, t * P:(t + 1) * P] for v in hT], [w[:, m, :] for w in w2p])
                                            for m in range(HC)])
                        last.then_inc(down_ps, 1)
                pe.wait_ge(xT_sb, 2 * GR * (e + 1) + 2)
                pe.wait_ge(h_sb, HS * e + HC * QN + 1)
                for m in range(HC):
                    last = product(ps[2][:, m * B:(m + 1) * B], [([w[:, k, m * P:(m + 1) * P] for w in w1p],
                                                                  [v[:, k, :] for v in xTl]) for k in range(KD)])
                last.then_inc(up_ps, 1)
                pe.wait_ge(h_sb, HS * (e + 1) + 1)
                pe.wait_ge(y_sum, YS * e + 2 * QN + 1)
                product(ps[4][:, 0:D], [([v[:, m, :] for v in hTl], [w[:, m, :] for w in w2p]) for m in range(HC)]
                        ).then_inc(down_ps, 1)


def recurrence_phase(nc, ctx, ps, xnT_d, s0_d, ident, w):
    with ExitStack() as mem:
        def sb(name, shape, dt=F32):
            return mem.enter_context(nc.sbuf_tensor(name, shape, dt))

        sem = phase_semaphores(nc, mem)

        mu = sb("a_mu", [P, KD])
        w1 = sb("a_w1", [P, KD, RANK])
        w2 = sb("a_w2", [RANK, NMU * RANK])
        b2 = sb("a_b2", [P, 1])
        b2t = sb("a_b2t", [RANK, 1])
        xo = sb("a_xo", [P, NMU - 1, D])
        xot = sb("a_xot", [RANK, D])
        xb = sb("a_xb", [P, NMU, KD])
        rw = sb("a_rw", [P, KD, KW])
        kw = sb("a_kw", [P, KD, KW])
        vw = sb("a_vw", [P, KD, VW])
        gw = sb("a_gw", [P, KD, VW])
        dw1 = sb("a_dw1", [P, KD, GATE])
        dw2 = sb("a_dw2", [GATE, KW])
        db = sb("a_db", [KW, 1])
        bonus = sb("a_bonus", [KW, 1])
        gnw = sb("a_gnw", [P, VW])
        gnb = sb("a_gnb", [P, VW])
        ow = sb("a_ow", [P, KD, D])
        power = sb("a_power", [P, NH])

        h = [sb(f"a_h{r}", [P, KD, GN + 1]) for r in range(2)]
        delta = sb("a_delta", [P, KD, GN])
        lerp = sb("a_lerp", [P, KD, GN])
        low = sb("a_low", [RANK, GN])
        x1 = sb("a_x1", [P, GN])
        x1t = sb("a_x1t", [RANK, GN])
        tmp = [sb(f"a_tmp{r}", [P, GN]) for r in range(2)]
        mix = [sb(f"a_mix{n}", [P, KD, GN]) for n in range(NMU)]
        dlow = sb("a_dlow", [GATE, GN])
        dexp = sb("a_dexp", [KW, GN])
        decay0 = [sb(f"a_decay{r}", [KW, GN]) for r in range(2)]
        decays = [None] + [sb(f"a_decays{lv}", [KW, GN >> lv]) for lv in range(1, LEVELS + 1)]
        R2 = [sb(f"a_R{r}", [KW, NH, GN]) for r in range(2)]
        K2 = [sb(f"a_K{r}", [KW, GN]) for r in range(2)]
        rk2 = [sb(f"a_rk{r}", [KW, GN]) for r in range(2)]
        heads = sb("a_heads", [KW, NH])
        V2 = [sb(f"a_V{r}", [P, GT, VW]) for r in range(2)]
        th = sb("a_th", [P, 2, 2 * VW])
        G2 = [sb(f"a_G{r}", [P, GT, VW]) for r in range(2)]
        A = [sb(f"a_A{c}", [P, NH * P]) for c in range(GT)]
        KT = [sb(f"a_KT{r}", [P, KW]) for r in range(2)]
        S = sb("a_S", [KW, DV])
        on = [sb(f"a_on{r}", [P, VW]) for r in range(2)]
        ogT = [sb(f"a_ogT{r}", [P, KD, P]) for r in range(2)]
        s0 = sb("a_s0", [P, GT, D])
        stats = sb("a_stats", [P, NH, 6])
        mv = sb("a_mv", [P, NH, 2])
        vare = sb("a_vare", [P, NH])
        rstd = sb("a_rstd", [P, NH])
        mask = [sb(f"a_mask{lv}", [P, P], U32) for lv in range(LEVELS)]
        col = sb("a_col", [P, P], I32)
        row = sb("a_row", [P, P], I32)
        bits = sb("a_bits", [P, P], I32)
        shifted = sb("a_shifted", [P, P], I32)
        after = sb("a_after", [P, P])
        one_level = sb("a_level", [P, P])

        w_in = sem("a_w_in")
        set_up = sem("a_set_up")
        masks = sem("a_masks")
        h_in = [sem(f"a_h_in{r}") for r in range(2)]
        deltas = sem("a_deltas")
        lerped = sem("a_lerped")
        low_ps = sem("a_low_ps")
        low_sb = sem("a_low_sb")
        x0_ps = sem("a_x0_ps")
        x1_sb = sem("a_x1_sb")
        mu_ps = sem("a_mu_ps")
        mu_sb = sem("a_mu_sb")
        mixed = sem("a_mixed")
        dlow_ps = sem("a_dlow_ps")
        dlow_sb = sem("a_dlow_sb")
        dexp_ps = sem("a_dexp_ps")
        dexp_sb = sem("a_dexp_sb")
        decay_sb = sem("a_decay_sb")
        rk_ps = sem("a_rk_ps")
        rk_sb = sem("a_rk_sb")
        v_ps = sem("a_v_ps")
        v_sb = sem("a_v_sb")
        g_ps = sem("a_g_ps")
        th_sb = sem("a_th_sb")
        G_sb = sem("a_G_sb")
        rkb = sem("a_rkb")
        own_ps = sem("a_own_ps")
        own_sb = sem("a_own_sb")
        A_ps = sem("a_A_ps")
        A_sb = sem("a_A_sb")
        R_step = sem("a_R_step")
        K_step = sem("a_K_step")
        KT_ps = sem("a_KT_ps")
        KT_sb = sem("a_KT_sb")
        U_ps = sem("a_U_ps")
        S_sb = sem("a_S_sb")
        o_ps = sem("a_o_ps")
        on_sb = sem("a_on_sb")
        norm_o = sem("a_norm_o")
        var_sb = sem("a_var_sb")
        rstd_sb = sem("a_rstd_sb")
        gated = sem("a_gated")
        gate_o = sem("a_gate_o")
        ogT_ps = sem("a_ogT_ps")
        ogT_sb = sem("a_ogT_sb")
        s0_ps = sem("a_s0_ps")
        s0_sb = sem("a_s0_sb")
        s0_out = sem("a_s0_out")
        spare = sem("a_spare")

        hT_v = xnT_d.rearrange("k p n -> p k n")
        s0_v = s0_d.rearrange("(g t p) d -> p (g t) d", t=GT, p=P)
        NMM = NMU * KD
        NA = LEVELS * GT
        NSTEP = LEVELS * GT
        LOADS = 21
        order = [1, 2, 0, 3, 4]
        SEGMENTS = 11
        MIXES = {3: (0, 1), 4: (2, 3), 5: (4, 5), 7: (6, 7), 8: (8, 9)}

        def pipeline(eng, begin, piece, level, chunk):
            def group(b, r, last=False):
                g, nb = HALVES * b + r, b + r
                if not last:
                    begin(g + 1, 1 - r, nb)
                for lv in range(LEVELS):
                    level(g, r, lv)
                    if not last:
                        piece(g + 1, 1 - r, lv)
                for c in range(GT):
                    chunk(b, g, r, c)
                    if not last:
                        piece(g + 1, 1 - r, LEVELS + c)
                chunk(b, g, r, GT)

            begin(0, 0, 0)
            for s in range(SEGMENTS):
                piece(0, 0, s)
            with eng.Fori(0, B - 1) as b:
                for r in range(HALVES):
                    group(b, r)
            for r in range(HALVES):
                group(B - 1, r, last=(r == HALVES - 1))

        block = mem.enter_context(nc.Block())

        @block.sync
        def _(sp):
            loads = [(mu[:], w["L0_attn_x_proj_mu"]), (w1[:], w["L0_attn_xl_w1"]), (w2[:], w["L0_attn_xl_w2"]),
                     (b2[:], w["L0_attn_xl_b2"][0:P]), (b2t[:], w["L0_attn_xl_b2"][P:P + RANK]),
                     (xot[:], w["L0_attn_x_out_w"][P:P + RANK]), (xb[:], w["L0_attn_x_bias"]),
                     (rw[:], w["L0_attn_r_w"]), (kw[:], w["L0_attn_k_w"]), (vw[:], w["L0_attn_v_w"]),
                     (gw[:], w["L0_attn_g_w"]), (dw1[:], w["L0_attn_w_w1"]), (dw2[:], w["L0_attn_w_w2"]),
                     (db[:], w["L0_attn_w_b"]), (bonus[:], w["L0_attn_bonus"]),
                     (gnw[:], w["L0_attn_gn_weight"].to_broadcast([P, VW])),
                     (gnb[:], w["L0_attn_gn_bias"].to_broadcast([P, VW])), (ow[:], w["L0_attn_o_w"])]
            for dst, src in loads:
                sp.dma_start(dst, src).then_inc(w_in, 16)
            sp.wait_ge(set_up, 6)
            for n in range(NMU - 1):
                sp.dma_start(xo[RANK * n:RANK * (n + 1), n, :], w["L0_attn_x_out_w"][RANK * n:RANK * (n + 1)]
                             ).then_inc(w_in, 16)
            assert len(loads) + NMU - 1 == LOADS + 1
            with sp.Fori(0, B) as b:
                for r in range(HALVES):
                    g = HALVES * b + r
                    sp.wait_ge(mixed, NMM * g + NMM)
                    sp.sem_inc(spare, 1)
                    if r == 0:
                        sp.dma_start(h[0][:, :, 1:GN + 1], hT_v[:, :, bass.ds(T * b, GN)]).then_inc(h_in[0], 16)
                    else:
                        sp.dma_start(h[1][:], hT_v[:, :, bass.ds(T * b + GN - 1, GN + 1)]).then_inc(h_in[1], 16)

        @block.gpsimd
        def _(pool):
            pool.sem_inc(mixed, 2 * NMM)
            nc.gpsimd.memset(xo[:], 0.0).then_inc(set_up, 1)
            for r in range(2):
                nc.gpsimd.memset(R2[r][:], 0.0).then_inc(set_up, 1)
            nc.gpsimd.memset(h[0][:, :, 0:1], 0.0).then_inc(set_up, 1)
            nc.gpsimd.memset(power[:], -0.5).then_inc(set_up, 1)
            nc.gpsimd.memset(heads[:], 0.0).then_inc(set_up, 1)
            nc.gpsimd.iota(col[:], pattern=[[1, P]], base=0, channel_multiplier=0).then_inc(masks, 1)
            nc.gpsimd.iota(row[:], pattern=[[0, P]], base=0, channel_multiplier=1).then_inc(masks, 1)
            pool.wait_ge(set_up, 6)
            pool.wait_ge(masks, 2)
            for hd in range(NH):
                nc.gpsimd.memset(heads[hd * DK:(hd + 1) * DK, hd:hd + 1], 1.0).then_inc(set_up, 1)
            pool.wait_ge(set_up, 10)
            pool.wait_ge(w_in, 16 * (LOADS + 1))
            nc.gpsimd.tensor_scalar(gnw[:], gnw[:], 0.5, None, ALU.mult).then_inc(set_up, 1)
            nc.gpsimd.tensor_scalar(gnb[:], gnb[:], 0.5, None, ALU.mult).then_inc(set_up, 1)
            pool.wait_ge(set_up, 12)

            def begin(f, r, b):
                pool.wait_ge(h_in[r], 16 * b + 16)
                pool.wait_ge(mu_sb, NMM * f + 2)
                pool.wait_ge(g_ps, 2 * f + 2)
                nc.gpsimd.tensor_tensor(delta[:], h[r][:, :, 0:GN], h[r][:, :, 1:GN + 1], ALU.subtract
                                        ).then_inc(deltas, 1)

            def piece(f, r, s):
                for i in MIXES.get(s, ()):
                    n, m = order[i // KD], i % KD
                    pool.wait_ge(mu_sb, NMM * f + i + 1 + 2)
                    nc.gpsimd.tensor_tensor(mix[n][:, m, :], tmp[i % 2][:], h[r][:, m, 1:GN + 1], ALU.add
                                            ).then_inc(mixed, 1)

            def level(g, r, lv):
                half = 1 << lv
                nb = P // (2 * half)
                decay = decays[lv] if lv else decay0[r]
                if lv == 0:
                    pool.wait_ge(decay_sb, g + 1)
                    pool.wait_ge(rk_sb, 2 * g + 2)
                for c in range(GT):
                    pool.wait_ge(A_ps, NA * g + lv * GT + c + 1)
                    if lv:
                        pool.wait_ge(R_step, NSTEP * g + (lv - 1) * GT + c + 1)
                        pool.wait_ge(K_step, NSTEP * g + (lv - 1) * GT + c + 1)
                    dk = decay[:, c * 2 * nb:(c + 1) * 2 * nb].rearrange("p (n s) -> p n s", s=2)
                    Rv = R2[r][:, :, c * P:(c + 1) * P].rearrange("p h (n s t) -> p h n s t", s=2, t=half)
                    nc.gpsimd.tensor_tensor(
                        Rv[:, :, :, 1, :], Rv[:, :, :, 1, :],
                        dk[:, :, 0].unsqueeze(1).unsqueeze(3).to_broadcast([P, NH, nb, half]), ALU.mult
                    ).then_inc(R_step, 1)

            def chunk(b, g, r, c):
                if c == GT:
                    return
                o = Order(pool, gate_o, (g * GT + c) * 2)
                pool.wait_ge(var_sb, GT * g + c + 1)
                nc.gpsimd.tensor_tensor(rstd[:], vare[:], power[:], ALU.pow).then_inc(rstd_sb, 1)
                pool.wait_ge(on_sb, GT * g + c + 2)
                o.link(nc.gpsimd.tensor_tensor(on[c % 2][:], on[c % 2][:], gnw[:], ALU.mult))
                o.link(nc.gpsimd.tensor_tensor(on[c % 2][:], on[c % 2][:], gnb[:], ALU.add))
                pool.wait_ge(G_sb, 2 * g + 2 + 2)
                nc.gpsimd.tensor_tensor(on[c % 2][:], on[c % 2][:], G2[r][:, c, :], ALU.mult).then_inc(gated, 1)

            pipeline(pool, begin, piece, level, chunk)

        @block.vector
        def _(dve):
            dve.sem_inc(mu_sb, 2)
            o = Order(dve, masks, 2)
            dve.wait_ge(masks, 2)
            o.link(nc.vector.tensor_tensor(bits[:], row[:], col[:], ALU.bitwise_xor))
            o.link(nc.vector.tensor_tensor(after[:], col[:], row[:], ALU.is_gt))
            for lv in range(LEVELS):
                o.link(nc.vector.tensor_scalar(shifted[:], bits[:], lv, None, ALU.logical_shift_right))
                o.link(nc.vector.tensor_scalar(one_level[:], shifted[:], 1.0, None, ALU.is_equal))
                o.link(nc.vector.tensor_tensor(mask[lv][:], one_level[:], after[:], ALU.mult))
            dve.wait_ge(w_in, 16 * (LOADS + 1))

            def begin(f, r, b):
                dve.wait_ge(deltas, f + 1)
                for m in range(KD):
                    nc.vector.scalar_tensor_tensor(out=lerp[:, m, :], in0=delta[:, m, :], scalar=mu[:, m:m + 1],
                                                   in1=h[r][:, m, 1:GN + 1], op0=ALU.mult, op1=ALU.add
                                                   ).then_inc(lerped, 1)

            def gate(f, r, u):
                dve.wait_ge(th_sb, 2 * f + u + 1)
                nc.vector.scalar_tensor_tensor(
                    out=G2[r][:, 2 * u:2 * u + 2, :].rearrange("p t n -> p (t n)"), in0=th[:, u, :], scalar=1.0,
                    in1=ps[7][:], op0=ALU.add, op1=ALU.mult).then_inc(G_sb, 1)

            def piece(f, r, s):
                for i in MIXES.get(s, ()):
                    n, m = order[i // KD], i % KD
                    dve.wait_ge(mu_ps, NMM * f + i + 1)
                    dve.wait_ge(mixed, NMM * (f + 2) + i - 1)
                    nc.vector.scalar_tensor_tensor(out=tmp[i % 2][:], in0=ps[5 + i % 2][:], scalar=xb[:, n, m:m + 1],
                                                   in1=delta[:, m, :], op0=ALU.add, op1=ALU.mult).then_inc(mu_sb, 1)
                if s == 7:
                    dve.wait_ge(rk_ps, 2 * f + 2)
                    dve.wait_ge(rk_sb, 2 * f + 1)
                    nc.vector.scalar_tensor_tensor(out=rk2[r][:], in0=K2[r][:], scalar=bonus[:, 0:1], in1=ps[7][:],
                                                   op0=ALU.mult, op1=ALU.mult).then_inc(rkb, 1)
                if s >= 9:
                    gate(f, r, s - 9)

            def level(g, r, lv):
                half = 1 << lv
                nb = P // (2 * half)
                decay = decays[lv] if lv else decay0[r]
                if lv == 0:
                    dve.wait_ge(own_ps, g + 1)
                    for c in range(GT):
                        for hd in range(NH):
                            last = nc.vector.tensor_scalar(A[c][:, hd * P:(hd + 1) * P], ident[:],
                                                           ps[3][:, c * NH + hd:c * NH + hd + 1], None, ALU.mult)
                        last.then_inc(own_sb, 1)
                    dve.wait_ge(decay_sb, g + 1)
                for c in range(GT):
                    n = lv * GT + c
                    dve.wait_ge(A_ps, NA * g + n + 1)
                    if lv:
                        dve.wait_ge(A_sb, NA * g + n - GT + 1)
                        dve.wait_ge(K_step, NSTEP * g + n - GT + 1)
                    else:
                        dve.wait_ge(own_sb, GT * g + c + 1)
                    dve.sem_inc(spare, 1)
                    a3 = A[c][:].rearrange("p (h n s t) -> p h n s t", h=NH, s=2, t=half)[:, :, :, 1, :]
                    m3 = mask[lv][:].rearrange("p (n s t) -> p n s t", s=2, t=half)[:, :, 1, :]
                    p3 = ps[n % 2][:, 0:NH * P // 2].rearrange("p (h n t) -> p h n t", h=NH, t=half)
                    nc.vector.copy_predicated(
                        a3, m3.unsqueeze(1).to_broadcast([P, NH, nb, half]), p3).then_inc(A_sb, 1)
                    dk = decay[:, c * 2 * nb:(c + 1) * 2 * nb].rearrange("p (n s) -> p n s", s=2)
                    Kv = K2[r][:, c * P:(c + 1) * P].rearrange("p (n s t) -> p n s t", s=2, t=half)
                    nc.vector.tensor_tensor(Kv[:, :, 0, :], Kv[:, :, 0, :],
                                            dk[:, :, 1].unsqueeze(2).to_broadcast([P, nb, half]), ALU.mult)
                    nc.vector.tensor_tensor(decays[lv + 1][:, c * nb:(c + 1) * nb], dk[:, :, 0], dk[:, :, 1],
                                            ALU.mult).then_inc(K_step, 1)

            def chunk(b, g, r, c):
                if c == GT:
                    return
                if c == 0:
                    dve.wait_ge(K_step, NSTEP * (g + 1))
                    if r == 0:
                        nc.vector.memset(S[:], 0.0).then_inc(S_sb, 1)
                dve.wait_ge(U_ps, GT * g + c + 1)
                dve.wait_ge(o_ps, GT * g + c + 1)
                dve.wait_ge(S_sb, (1 + GT * HALVES) * b + 1 + r * GT + c)
                nc.vector.scalar_tensor_tensor(out=S[:], in0=S[:], scalar=decays[LEVELS][:, c:c + 1],
                                               in1=ps[4][:, 0:DV], op0=ALU.mult, op1=ALU.add).then_inc(S_sb, 1)
                o = Order(dve, norm_o, (g * GT + c) * 2 * NH)
                op = ps[2][:, 0:VW].rearrange("p (h v) -> p h v", h=NH)
                for hd in range(NH):
                    o.did(nc.vector.bn_stats(out=stats[:, hd, :], in_=op[:, hd, :]))
                o.hold(spare)
                for hd in range(NH):
                    o.did(nc.vector.bn_aggr(out=mv[:, hd, :], in_=stats[:, hd, :]))
                o.wait()
                nc.vector.tensor_scalar(vare[:], mv[:, :, 1], EPS, None, ALU.add).then_inc(var_sb, 1)
                dve.wait_ge(rstd_sb, GT * g + c + 1)
                if c >= 2:
                    dve.wait_ge(ogT_ps, GT * g + c - 1)
                for hd in range(NH):
                    last = nc.vector.tensor_scalar(on[c % 2][:, hd * DV:(hd + 1) * DV], op[:, hd, :],
                                                   mv[:, hd, 0:1], rstd[:, hd:hd + 1], ALU.subtract, ALU.mult)
                last.then_inc(on_sb, 1)

            pipeline(dve, begin, piece, level, chunk)

        @block.scalar
        def _(act):
            act.sem_inc(s0_sb, 1)
            act.sem_inc(s0_out, 16)
            act.wait_ge(w_in, 16 * (LOADS + 1))
            act.wait_ge(set_up, 12)

            def begin(f, r, b):
                pass

            def piece(f, r, s):
                if s == 0:
                    act.wait_ge(low_ps, f + 1)
                    nc.scalar.activation(low[:], ps[7][0:RANK, :], ACT.Tanh).then_inc(low_sb, 1)
                if s == 1:
                    act.wait_ge(x0_ps, 2 * f + 1)
                    nc.scalar.activation(x1[:], ps[7][:], ACT.Tanh, bias=b2[:, 0:1]).then_inc(x1_sb, 1)
                if s == 2:
                    act.wait_ge(x0_ps, 2 * f + 2)
                    nc.scalar.activation(x1t[:], ps[7][0:RANK, :], ACT.Tanh, bias=b2t[:, 0:1]).then_inc(x1_sb, 1)
                if s == 4:
                    act.wait_ge(dlow_ps, f + 1)
                    nc.scalar.activation(dlow[:], ps[7][0:GATE, :], ACT.Tanh).then_inc(dlow_sb, 1)
                if s == 5:
                    act.wait_ge(dexp_ps, f + 1)
                    nc.scalar.activation(dexp[:], ps[7][:], ACT.Exp, bias=db[:, 0:1]).then_inc(dexp_sb, 1)
                    act.wait_ge(dexp_sb, f + 1)
                    nc.scalar.activation(decay0[r][:], dexp[:], ACT.Exp, scale=-1.0).then_inc(decay_sb, 1)
                if s == 6:
                    act.wait_ge(rk_ps, 2 * f + 1)
                    nc.scalar.copy(K2[r][:], ps[7][:]).then_inc(rk_sb, 1)
                if s == 7:
                    act.wait_ge(rk_ps, 2 * f + 2)
                    act.wait_ge(rkb, f + 1)
                    for hd in range(NH):
                        rows = slice(hd * DK, (hd + 1) * DK)
                        last = nc.scalar.copy(R2[r][rows, hd, :], ps[7][rows, :])
                    last.then_inc(rk_sb, 1)
                if s in (8, 9):
                    u = s - 8
                    act.wait_ge(v_ps, 2 * f + u + 1)
                    nc.scalar.copy(V2[r][:, 2 * u:2 * u + 2, :].rearrange("p t n -> p (t n)"), ps[7][:]
                                   ).then_inc(v_sb, 1)
                if s in (9, 10):
                    u = s - 9
                    act.wait_ge(g_ps, 2 * f + u + 1 + 2)
                    nc.scalar.activation(th[:, u, :], ps[7][:], ACT.Tanh, scale=0.5).then_inc(th_sb, 1)

            def level(g, r, lv):
                pass

            def chunk(b, g, r, c):
                if c == 0:
                    act.wait_ge(s0_out, 16 * g + 16)
                if c < GT:
                    act.wait_ge(KT_ps, GT * g + c + 1)
                    if c >= 2:
                        act.wait_ge(U_ps, GT * g + c - 1)
                    nc.scalar.copy(KT[c % 2][:], ps[3][:, 0:KW]).then_inc(KT_sb, 1)
                if c:
                    act.wait_ge(ogT_ps, GT * g + c)
                    if c >= 3:
                        act.wait_ge(s0_ps, GT * g + c - 2)
                    nc.scalar.copy(ogT[(c - 1) % 2][:].rearrange("p k n -> p (k n)"), ps[3][:, 0:KD * P]
                                   ).then_inc(ogT_sb, 1)
                    act.wait_ge(s0_ps, GT * g + c)
                    nc.scalar.copy(s0[:, c - 1, :], ps[4][:, 0:D]).then_inc(s0_sb, 1)
                if c == GT:
                    act.wait_ge(s0_sb, GT * (g + 1) + 1)
                    act.dma_start(s0_v[:, GT * g:GT * (g + 1), :] if isinstance(g, int)
                                  else s0_v[:, bass.ds(GT * g, GT), :], s0[:]).then_inc(s0_out, 16)

            pipeline(act, begin, piece, level, chunk)
            act.wait_ge(s0_out, 16 * B * HALVES + 16)

        @block.tensor
        def _(pe):
            pe.wait_ge(w_in, 16 * (LOADS + 1))
            pe.wait_ge(set_up, 12)

            def product(out, sem_, pairs):
                for k, (lhsT, rhs) in enumerate(pairs):
                    last = nc.tensor.matmul(out, lhsT, rhs, start=(k == 0), stop=(k == len(pairs) - 1))
                if sem_ is not None:
                    last.then_inc(sem_, 1)

            pe.sem_inc(g_ps, 2)
            pe.sem_inc(G_sb, 2)
            pe.sem_inc(on_sb, 1)

            def begin(f, r, b):
                pass

            def mixes(f, i):
                n, m = order[i // KD], i % KD
                pe.wait_ge(mu_sb, NMM * f + i + 1)
                lhsT = xo[:, n, m * P:(m + 1) * P] if n < NMU - 1 else xot[:, m * P:(m + 1) * P]
                product(ps[5 + i % 2][:], mu_ps, [(lhsT, x1[:] if n < NMU - 1 else x1t[:])])

            def have_mix(f, j):
                pe.wait_ge(mixed, NMM * (f + 2) + KD * (j + 1))

            def tokens(n, wt, u, s):
                for t in (2 * u, 2 * u + 1):
                    product(ps[7][:, (t % 2) * VW:(t % 2 + 1) * VW], s if t % 2 else None,
                            [(mix[n][:, k, t * P:(t + 1) * P], wt[:, k, :]) for k in range(KD)])

            def piece(f, r, s):
                if s == 0:
                    pe.wait_ge(lerped, 2 * f + 2)
                    pe.wait_ge(G_sb, 2 * f + 2)
                    product(ps[7][0:RANK, :], low_ps, [(w1[:, k, :], lerp[:, k, :]) for k in range(KD)])
                if s == 1:
                    pe.wait_ge(low_sb, f + 1)
                    product(ps[7][:], x0_ps, [(w2[:, 0:P], low[:])])
                if s == 2:
                    pe.wait_ge(x1_sb, 2 * f + 1)
                    pe.sem_inc(spare, 1)
                    product(ps[7][0:RANK, :], x0_ps, [(w2[:, P:P + RANK], low[:])])
                if s == 3:
                    pe.wait_ge(x1_sb, 2 * f + 2)
                for i in MIXES.get(s, ()):
                    mixes(f, i)
                if s == 4:
                    have_mix(f, 0)
                    product(ps[7][0:GATE, :], dlow_ps, [(dw1[:, k, :], mix[1][:, k, :]) for k in range(KD)])
                if s == 5:
                    pe.wait_ge(dlow_sb, f + 1)
                    product(ps[7][:], dexp_ps, [(dw2[:], dlow[:])])
                if s == 6:
                    have_mix(f, 1)
                    pe.wait_ge(dexp_sb, f + 1)
                    product(ps[7][:], rk_ps, [(kw[:, k, :], mix[2][:, k, :]) for k in range(KD)])
                if s == 7:
                    have_mix(f, 2)
                    pe.wait_ge(rk_sb, 2 * f + 1)
                    product(ps[7][:], rk_ps, [(rw[:, k, :], mix[0][:, k, :]) for k in range(KD)])
                if s == 8:
                    have_mix(f, 3)
                    pe.wait_ge(rk_sb, 2 * f + 2)
                    pe.wait_ge(rkb, f + 1)
                    tokens(3, vw, 0, v_ps)
                if s == 9:
                    pe.wait_ge(v_sb, 2 * f + 1)
                    tokens(3, vw, 1, v_ps)
                    have_mix(f, 4)
                    pe.wait_ge(v_sb, 2 * f + 2)
                    tokens(4, gw, 0, g_ps)
                if s == 10:
                    pe.wait_ge(th_sb, 2 * f + 1)
                    pe.wait_ge(G_sb, 2 * f + 1 + 2)
                    tokens(4, gw, 1, g_ps)

            def level(g, r, lv):
                K, R, rk = K2[r], R2[r], rk2[r]
                if lv == 0:
                    pe.wait_ge(rkb, g + 1)
                    for c in range(GT):
                        last = nc.tensor.matmul(ps[3][:, c * NH:(c + 1) * NH], rk[:, c * P:(c + 1) * P], heads[:],
                                                start=True, stop=True)
                    last.then_inc(own_ps, 1)
                    pe.wait_ge(rk_sb, 2 * g + 2)
                half = 1 << lv
                for c in range(GT):
                    n = lv * GT + c
                    if n >= 2:
                        pe.wait_ge(A_sb, NA * g + n - 1)
                    if lv:
                        pe.wait_ge(K_step, NSTEP * g + n - GT + 1)
                        pe.wait_ge(R_step, NSTEP * g + n - GT + 1)
                    tok = slice(c * P, (c + 1) * P)
                    product(ps[n % 2][:, 0:NH * P // 2].rearrange("p (h n t) -> p h n t", h=NH, t=half), A_ps,
                            [(K[:, tok], R[:, :, tok].rearrange("p h (n s t) -> p h n s t", s=2, t=half)
                              [:, :, :, 1, :])])

            def finish(b, g, r, c):
                pe.wait_ge(gated, GT * g + c + 1)
                for k in range(KD):
                    last = nc.tensor.transpose(ps[3][:, k * P:(k + 1) * P], on[c % 2][:, k * P:(k + 1) * P],
                                               ident[:])
                last.then_inc(ogT_ps, 1)
                pe.wait_ge(ogT_sb, GT * g + c + 1)
                pe.wait_ge(S_sb, (1 + GT * HALVES) * b + 1 + r * GT + min(c + 2, GT))
                product(ps[4][:, 0:D], s0_ps, [(ogT[c % 2][:, k, :], ow[:, k, :]) for k in range(KD)])

            def chunk(b, g, r, c):
                if c == GT:
                    finish(b, g, r, GT - 1)
                    return
                K, R, V = K2[r], R2[r], V2[r]
                tok = slice(c * P, (c + 1) * P)
                if c == 0:
                    pe.wait_ge(v_sb, 2 * g + 2)
                pe.wait_ge(K_step, NSTEP * g + (LEVELS - 1) * GT + c + 1)
                nc.tensor.transpose(ps[3][:, 0:KW], K[:, tok], ident[:]).then_inc(KT_ps, 1)
                pe.wait_ge(A_sb, NA * g + (LEVELS - 1) * GT + c + 1)
                pe.wait_ge(R_step, NSTEP * g + (LEVELS - 1) * GT + c + 1)
                pe.wait_ge(S_sb, (1 + GT * HALVES) * b + 1 + r * GT + c)
                pe.wait_ge(on_sb, GT * g + c + 1)
                for hd in range(NH):
                    product(ps[2][:, hd * DV:(hd + 1) * DV], o_ps if hd == NH - 1 else None,
                            [(A[c][:, hd * P:(hd + 1) * P], V[:, c, hd * DV:(hd + 1) * DV]),
                             (R[:, hd, tok], S[:])])
                pe.wait_ge(KT_sb, GT * g + c + 1)
                pe.wait_ge(s0_sb, GT * g + (c if c else 1))
                for hd in range(NH):
                    product(ps[4][hd * DK:(hd + 1) * DK, 0:DV], U_ps if hd == NH - 1 else None,
                            [(KT[c % 2][:, hd * DK:(hd + 1) * DK], V[:, c, hd * DV:(hd + 1) * DV])])
                if c:
                    finish(b, g, r, c - 1)

            pipeline(pe, begin, piece, level, chunk)


def layer1_phase(nc, ctx, ps, x, s0_d, acc_d, x1_d, xn1_d, g_d, ident, w, Y, coef):
    with ExitStack() as mem:
        def sb(name, shape, dt=F32):
            return mem.enter_context(nc.sbuf_tensor(name, shape, dt))

        sem = phase_semaphores(nc, mem)

        w1s = sb("f_w1", [P, KD, FF])
        w3s = sb("f_w3", [P, KD, FF])
        w2s = sb("f_w2", [P, FC, D])
        w1p, w3p = ([sb(f"f_w{m}{n}", [P, KD, FC * P], F32R) for n in "hl"] for m in (1, 3))
        w2p = [sb(f"f_w2{n}", [P, FC, D], F32R) for n in "hl"]
        bm = sb("f_bm", [P, KD, 2 * PS])
        bmp = [sb(f"f_bm{n}", [P, KD, 2 * PS], F32R) for n in "hl"]
        raw = sb("f_raw", [P, 4])
        xg = [sb(f"f_x{r}", [P, GT, D]) for r in range(2)]
        sg = [sb(f"f_s{r}", [P, GT, D]) for r in range(2)]
        ag = [sb(f"f_a{r}", [P, GT, D]) for r in range(2)]
        xn = sb("f_xn", [P, GT, D])
        xT = [[sb(f"f_xT{n}{r}", [P, KD, GN], F32R) for n in "hl"] for r in range(2)]
        act_ = [sb(f"f_act{r}", [P, GN]) for r in range(2)]
        hf = [sb(f"f_hf{r}", [P, GN]) for r in range(2)]
        hT = [sb(f"f_hT{n}", [P, FC, GN], F32R) for n in "hl"]
        gs = sb("f_gs", [P, GT, D])
        stats = sb("f_stats", [P, GT, 6])
        mv = sb("f_mv", [P, GT, 2])
        vare = sb("f_vare", [P, GT])
        power = sb("f_power", [P, GT])
        rstd = sb("f_rstd", [P, GT])

        raw_in = sem("f_raw_in")
        power_set = sem("f_power_set")
        coef_o = sem("f_coef_o")
        sig = sem("f_sig")
        alpha_in = sem("f_alpha_in")
        alpha_out = sem("f_alpha_out")
        up_in = sem("f_up_in")
        padded = sem("f_padded")
        bm_high = sem("f_bm_high")
        bm_split = sem("f_bm_split")
        up_high = sem("f_up_high")
        up_split = sem("f_up_split")
        down_high = sem("f_down_high")
        down_split = sem("f_down_split")
        xh_sb = sem("f_xh_sb")
        hf_sb = sem("f_hf_sb")
        hh_sb = sem("f_hh_sb")
        down_in = sem("f_down_in")
        x_in = [sem(f"f_x_in{r}") for r in range(2)]
        silu = sem("f_silu")
        prod = sem("f_prod")
        summed = sem("f_summed")
        norm_o = sem("f_norm_o")
        var_sb = sem("f_var_sb")
        rstd_sb = sem("f_rstd_sb")
        normed = sem("f_normed")
        x_out = [sem(f"f_x_out{r}") for r in range(2)]
        xn_out = sem("f_xn_out")
        turned = sem("f_turned")
        xT_sb = sem("f_xT_sb")
        drive_ps = sem("f_drive_ps")
        drive_sb = sem("f_drive_sb")
        gate_ps = sem("f_gate_ps")
        up_ps = sem("f_up_ps")
        act_sb = sem("f_act_sb")
        h_sb = sem("f_h_sb")
        down_ps = sem("f_down_ps")
        gs_sb = sem("f_gs_sb")
        gs_out = sem("f_gs_out")
        spare = sem("f_spare")

        QB = B // GT
        ROWS = NE * QB

        def tiles(d):
            return d.rearrange("(b j p) d -> j p b d", j=NE, p=P)

        x_v, s_v, a_v, x1_v, xn1_v, g_v = (tiles(d) for d in (x, s0_d, acc_d, x1_d, xn1_d, g_d))

        def at(v, j, q):
            return v[bass.ds(j, 1), :, GT * q:GT * (q + 1), :].rearrange("o p b d -> (o p) b d")

        block = mem.enter_context(nc.Block())

        @block.sync
        def _(sp):
            for c in range(2):
                for n, name in enumerate(("L1_attn_steps_raw", "L1_attn_G_raw", "L1_attn_A_raw")):
                    sp.dma_start(raw[c * PS:(c + 1) * PS, n:n + 1], w[name]).then_inc(raw_in, 16)
            sp.dma_start(bm[:], w["L1_attn_B_mat"]).then_inc(raw_in, 16)
            with sp.Fori(0, NE) as j:
                for q in range(QB):
                    r = q % 2
                    if q == 0:
                        sp.wait_ge(up_split, j + 1)
                        sp.sem_inc(spare, 1)
                        sp.dma_start(w1s[:], w["L1_ffn_w1"][bass.ds(j, 1)].rearrange("o p k n -> p (o k) n")
                                     ).then_inc(up_in, 16)
                        sp.dma_start(w3s[:], w["L1_ffn_w3"][bass.ds(j, 1)].rearrange("o p k n -> p (o k) n")
                                     ).then_inc(up_in, 16)
                    n = (q - 2) // 2 + 1 if q >= 2 else 0
                    sp.wait_ge(x_out[r], 16 * (QB // 2) * j + 16 * n + 16)
                    sp.sem_inc(spare, 1)
                    sp.wait_ge(normed, QB * j + max(q - 1, 0) + 1)
                    sp.sem_inc(spare, 1)
                    for dst, v in ((xg, x_v), (sg, s_v), (ag, a_v)):
                        sp.dma_start(dst[r][:], at(v, j, q)).then_inc(x_in[r], 16)
                    if q == 0:
                        sp.wait_ge(down_split, j + 1)
                        sp.sem_inc(spare, 1)
                        w2j = w["L1_ffn_w2"][bass.ds(j, 1)]
                        sp.dma_start(w2s[:, 0:FC - 1, :], w2j[:, 0:(FC - 1) * P, :].rearrange("o (k p) n -> p (o k) n", p=P)
                                     ).then_inc(down_in, 16)
                        sp.dma_start(w2s[0:width(FC - 1), FC - 1, :], w2j[:, (FC - 1) * P:FF, :].rearrange("o p n -> (o p) n")
                                     ).then_inc(down_in, 16)

        @block.gpsimd
        def _(pool):
            for s in (up_ps, down_ps, summed, xT_sb, normed, up_split, down_split):
                pool.sem_inc(s, 1)
            pool.sem_inc(h_sb, 2)
            for s in (gs_out, xn_out, x_out[0], x_out[1]):
                pool.sem_inc(s, 16)
            for part in w1p + w3p + w2p:
                nc.gpsimd.memset(part[:].bitcast(F32), 0.0).then_inc(padded, 1)
            nc.gpsimd.memset(power[:], -0.5).then_inc(power_set, 1)
            pool.wait_ge(power_set, 1)
            with pool.Fori(0, NE) as j:
                for q in range(QB):
                    r = q % 2
                    g = QB * j + q
                    pool.wait_ge(silu, g + 1)
                    nc.gpsimd.tensor_tensor(sg[r][:], sg[r][:], ag[r][:], ALU.mult).then_inc(prod, 1)
                    pool.wait_ge(var_sb, g + 1)
                    nc.gpsimd.tensor_tensor(rstd[:], vare[:], power[:], ALU.pow).then_inc(rstd_sb, 1)

        @block.vector
        def _(dve):
            o = Order(dve, coef_o)
            st, gd, ad, al = (raw[:, n:n + 1] for n in range(4))
            dve.wait_ge(raw_in, 16 * 7)
            o.link(nc.vector.tensor_scalar(gd, gd, 0.0, None, ALU.max))
            o.link(nc.vector.tensor_scalar(ad, ad, 0.0, None, ALU.max))
            dve.wait_ge(sig, 1)
            o.link(nc.vector.tensor_copy(coef[:, 2:3], st))
            o.link(nc.vector.tensor_tensor(gd, gd, st, ALU.mult))
            o.link(nc.vector.tensor_scalar(gd, gd, 1.0, None, ALU.add))
            o.link(nc.vector.reciprocal(coef[:, 0:1], gd))
            o.link(nc.vector.tensor_tensor(coef[:, 3:4], st, coef[:, 0:1], ALU.mult))
            o.link(nc.vector.tensor_tensor(al, st, coef[:, 3:4], ALU.mult))
            nc.vector.tensor_tensor(al, al, ad, ALU.mult).then_inc(alpha_in, 1)
            dve.wait_ge(alpha_out, 1)
            o.link(nc.vector.reciprocal(gd, st))
            o.link(nc.vector.tensor_scalar(al, al, -1.99, None, ALU.mult))
            o.link(nc.vector.tensor_tensor(coef[:, 1:2], al, gd, ALU.mult))

            def norm(j, q):
                g, r = QB * j + q, q % 2
                o = Order(dve, norm_o, g * (2 * GT))
                dve.wait_ge(prod, g + 1)
                nc.vector.tensor_tensor(xg[r][:], xg[r][:], sg[r][:], ALU.add).then_inc(summed, 1)
                dve.wait_ge(summed, g + 2)
                dve.sem_inc(spare, 1)
                for t in range(GT):
                    o.did(nc.vector.bn_stats(out=stats[:, t, :], in_=xg[r][:, t, :]))
                o.hold(spare)
                for t in range(GT):
                    o.did(nc.vector.bn_aggr(out=mv[:, t, :], in_=stats[:, t, :]))
                o.wait()
                nc.vector.tensor_scalar(vare[:], mv[:, :, 1], EPS, None, ALU.add).then_inc(var_sb, 1)
                dve.wait_ge(rstd_sb, g + 1)
                dve.wait_ge(xn_out, 16 * g + 16)
                dve.wait_ge(turned, g + 1)
                for t in range(GT):
                    last = nc.vector.tensor_scalar(xn[:, t, :], xg[r][:, t, :], mv[:, t, 0:1], rstd[:, t:t + 1],
                                                   ALU.subtract, ALU.mult)
                last.then_inc(normed, 1)

            def low(part, whole, high, **_):
                return nc.vector.tensor_tensor(part, whole, high.bitcast(F32), ALU.subtract)

            def turn(j, q):
                g, r = QB * j + q, q % 2
                dve.wait_ge(xh_sb, g + 1)
                for k in range(KD):
                    last = low(xT[r][1][:, k, :], ps[k][:], xT[r][0][:, k, :])
                last.then_inc(xT_sb, 1)

            def low_h(g, m):
                n = FC * g + m
                dve.wait_ge(hh_sb, n + 1)
                low(hT[1][:, m, :], hf[m % 2][:], hT[0][:, m, :]).then_inc(h_sb, 1)

            dve.wait_ge(bm_high, 1)
            low(bmp[1][:], bm[:], bmp[0][:]).then_inc(bm_split, 1)
            dve.wait_ge(padded, 6)
            LAST = width(FC - 1)

            with dve.Fori(0, NE) as j:
                norm(j, 0)
                dve.wait_ge(up_high, 2 * j + 2)
                dve.wait_ge(up_ps, QB * FC * j + 1)
                low(w1p[1][:, :, 0:FF], w1s[:], w1p[0][:, :, 0:FF])
                low(w3p[1][:, :, 0:FF], w3s[:], w3p[0][:, :, 0:FF]).then_inc(up_split, 1)
                turn(j, 0)
                dve.wait_ge(down_high, 2 * j + 2)
                dve.wait_ge(down_ps, QB * 2 * j + 1)
                low(w2p[1][:, 0:FC - 1, :], w2s[:, 0:FC - 1, :], w2p[0][:, 0:FC - 1, :])
                low(w2p[1][0:LAST, FC - 1, :], w2s[0:LAST, FC - 1, :], w2p[0][0:LAST, FC - 1, :]
                    ).then_inc(down_split, 1)
                for q in range(QB):
                    g = QB * j + q
                    for m in range(FC):
                        n = FC * g + m
                        dve.wait_ge(act_sb, n + 1)
                        dve.wait_ge(up_ps, n + 2)
                        dve.wait_ge(h_sb, n + 1)
                        nc.vector.tensor_tensor(hf[m % 2][:], act_[m % 2][:], ps[4 + m % 2][:], ALU.mult
                                                ).then_inc(hf_sb, 1)
                        if m:
                            low_h(g, m - 1)
                        if m == 2 and q + 1 < QB:
                            norm(j, q + 1)
                    low_h(g, FC - 1)
                    if q + 1 < QB:
                        turn(j, q + 1)

        @block.scalar
        def _(act):
            act.sem_inc(turned, 1)
            act.wait_ge(raw_in, 16 * 7)
            nc.scalar.activation(raw[:, 0:1], raw[:, 0:1], ACT.Sigmoid).then_inc(sig, 1)
            act.wait_ge(alpha_in, 1)
            nc.scalar.activation(raw[:, 3:4], raw[:, 3:4], ACT.Tanh, scale=1.0 / 1.99).then_inc(alpha_out, 1)

            def before(j, q):
                before_silu(j, q)
                before_stores(j, q)

            def before_silu(j, q):
                g, r = QB * j + q, q % 2
                act.wait_ge(x_in[r], 48 * (QB // 2) * j + 48 * (q // 2) + 48)
                nc.scalar.activation(ag[r][:], ag[r][:], ACT.Silu).then_inc(silu, 1)

            def before_stores(j, q):
                g, r = QB * j + q, q % 2
                act.wait_ge(summed, g + 2)
                act.dma_start(at(x1_v, j, q), xg[r][:]).then_inc(x_out[r], 16)
                act.wait_ge(normed, g + 2)
                act.dma_start(at(xn1_v, j, q), xn[:]).then_inc(xn_out, 16)

            def turn(j, q):
                g, r = QB * j + q, q % 2
                act.wait_ge(turned, g + 2)
                for k in range(KD):
                    last = nc.scalar.copy(xT[r][0][:, k, :], ps[k][:])
                last.then_inc(xh_sb, 1)

            def high_h(g, m):
                act.wait_ge(hf_sb, FC * g + m + 1)
                nc.scalar.copy(hT[0][:, m, :], hf[m % 2][:]).then_inc(hh_sb, 1)

            nc.scalar.copy(bmp[0][:], bm[:]).then_inc(bm_high, 1)
            act.wait_ge(padded, 6)
            LAST = width(FC - 1)
            with act.Fori(0, NE) as j:
                before(j, 0)
                act.wait_ge(up_in, 32 * j + 32)
                act.wait_ge(up_ps, QB * FC * j + 1)
                nc.scalar.copy(w1p[0][:, :, 0:FF], w1s[:]).then_inc(up_high, 1)
                nc.scalar.copy(w3p[0][:, :, 0:FF], w3s[:]).then_inc(up_high, 1)
                turn(j, 0)
                act.wait_ge(down_in, 32 * j + 32)
                act.wait_ge(down_ps, QB * 2 * j + 1)
                nc.scalar.copy(w2p[0][:, 0:FC - 1, :], w2s[:, 0:FC - 1, :]).then_inc(down_high, 1)
                nc.scalar.copy(w2p[0][0:LAST, FC - 1, :], w2s[0:LAST, FC - 1, :]).then_inc(down_high, 1)
                for q in range(QB):
                    g = QB * j + q
                    act.wait_ge(coef_o, 11)
                    act.wait_ge(drive_ps, g + 1)
                    nc.scalar.activation(Y[:, GT * q:GT * (q + 1), bass.ds(P * j, P)],
                                         ps[0][:].rearrange("p (b t) -> p b t", b=GT), ACT.Copy,
                                         scale=coef[:, 3:4]).then_inc(drive_sb, 1)
                    for m in range(FC):
                        n = FC * g + m
                        act.wait_ge(gate_ps, n + 1)
                        if m >= 2:
                            act.wait_ge(hf_sb, n - 1)
                        nc.scalar.activation(act_[m % 2][:], ps[2 + m % 2][:], ACT.Silu).then_inc(act_sb, 1)
                        if m:
                            high_h(g, m - 1)
                        if m == 1 and q + 1 < QB:
                            before_silu(j, q + 1)
                    high_h(g, FC - 1)
                    if q + 1 < QB:
                        before_stores(j, q + 1)
                        turn(j, q + 1)
                    act.wait_ge(gs_out, 16 * g + 16)
                    for u in range(2):
                        act.wait_ge(down_ps, 2 * g + u + 2)
                        nc.scalar.activation(gs[:, 2 * u:2 * u + 2, :].rearrange("p t n -> p (t n)"), ps[6 + u][:],
                                             ACT.Silu).then_inc(gs_sb, 1)
                    act.wait_ge(gs_sb, 2 * g + 4)
                    act.dma_start(at(g_v, j, q), gs[:]).then_inc(gs_out, 16)
            act.wait_ge(gs_out, 16 * ROWS + 16)
            act.wait_ge(xn_out, 16 * ROWS + 16)
            for r in range(2):
                act.wait_ge(x_out[r], 16 * (ROWS // 2) + 16)

        @block.tensor
        def _(pe):
            pe.wait_ge(raw_in, 16 * 7)

            def turn(j, q):
                g = QB * j + q
                pe.wait_ge(normed, g + 2)
                pe.wait_ge(drive_sb, g + 1)
                for k in range(KD):
                    for t in range(GT):
                        last = nc.tensor.transpose(ps[k][:, t * P:(t + 1) * P], xn[:, t, k * P:(k + 1) * P], ident[:])
                last.then_inc(turned, 1)

            def product(out, terms):
                pairs = [(a[i], b[j]) for a, b in terms for i, j in ((0, 0), (1, 0), (0, 1))]
                for n, (lhsT, rhs) in enumerate(pairs):
                    last = nc.tensor.matmul(out, lhsT, rhs, start=(n == 0), stop=(n == len(pairs) - 1))
                return last

            pe.wait_ge(bm_split, 1)
            pe.sem_inc(drive_sb, 1)
            pe.sem_inc(gs_sb, 2)
            with pe.Fori(0, NE) as j:
                turn(j, 0)
                for q in range(QB):
                    g, r = QB * j + q, q % 2
                    pe.wait_ge(xT_sb, g + 2)
                    product(ps[0][:], [([v[:, k, :] for v in bmp], [v[:, k, :] for v in xT[r]]) for k in range(KD)]
                            ).then_inc(drive_ps, 1)
                    if q == 0:
                        pe.wait_ge(up_split, j + 2)
                    for m in range(FC):
                        n = FC * g + m
                        if m >= 2:
                            pe.wait_ge(act_sb, n - 1)
                        for wp, bank, s in ((w1p, 2, gate_ps), (w3p, 4, up_ps)):
                            if bank == 4 and m >= 2:
                                pe.wait_ge(hf_sb, n - 1)
                            product(ps[bank + m % 2][:], [([v[:, k, m * P:(m + 1) * P] for v in wp],
                                                           [v[:, k, :] for v in xT[r]]) for k in range(KD)]
                                    ).then_inc(s, 1)
                    if q + 1 < QB:
                        turn(j, q + 1)
                    if q == 0:
                        pe.wait_ge(down_split, j + 2)
                    pe.wait_ge(h_sb, FC * (g + 1) + 2)
                    for u in range(2):
                        pe.wait_ge(gs_sb, 2 * g + u + 1)
                        for t in (2 * u, 2 * u + 1):
                            last = product(ps[6 + u][:, (t % 2) * D:(t % 2 + 1) * D],
                                           [([v[:, m, t * P:(t + 1) * P] for v in hT], [v[:, m, :] for v in w2p])
                                            for m in range(FC)])
                        last.then_inc(down_ps, 1)


def out_phase(nc, ctx, ps, x1_d, xn1_d, g_d, out, w, Y, coef):
    with ExitStack() as mem:
        def sb(name, shape, dt=F32):
            return mem.enter_context(nc.sbuf_tensor(name, shape, dt))

        sem = phase_semaphores(nc, mem)

        NB = B * NBLK
        DEPTH = 4
        z = sb("o_z", [P, NB])
        t = sb("o_t", [P, NB])
        zc = sb("o_zc", [P, B, NBLK])
        yc = sb("o_yc", [P, B, NBLK])
        t1 = sb("o_t1", [P, B])
        t2 = sb("o_t2", [P, B])
        qz = sb("o_qz", [P, 2])
        qt = sb("o_qt", [P, 2])
        qy = sb("o_qy", [P, BLK + 1, 2])
        q2 = sb("o_q2", [P, 2])
        cm = sb("o_cm", [P, D])
        dv = sb("o_dv", [P, D])
        yg = [sb(f"o_yg{r}", [P, GN]) for r in range(DEPTH)]
        xg = [sb(f"o_x{r}", [P, GT, D]) for r in range(DEPTH)]
        ng = [sb(f"o_n{r}", [P, GT, D]) for r in range(DEPTH)]
        gg = [sb(f"o_g{r}", [P, GT, D]) for r in range(DEPTH)]

        w_in = sem("o_w_in")
        set_up = sem("o_set_up")
        scan_o = sem("o_scan_o")
        scanned = sem("o_scanned")
        x_in = [sem(f"o_x_in{r}") for r in range(DEPTH)]
        skip = sem("o_skip")
        yg_sb = sem("o_yg_sb")
        c_ps = sem("o_c_ps")
        s_sb = sem("o_s_sb")
        sg_sb = sem("o_sg_sb")
        o_sb = sem("o_o_sb")
        o_out = [sem(f"o_o_out{r}") for r in range(DEPTH)]

        block = mem.enter_context(nc.Block())
        tv = [d.rearrange("(g t p) d -> p (g t) d", t=GT, p=P) for d in (x1_d, xn1_d, g_d, out)]
        Yb = Y[:].rearrange("p b (k i) -> p (b k) i", i=BLK)
        Yc = Y[:].rearrange("p b (k i) -> p b k i", i=BLK)
        m11, m12, step = (coef[:, n:n + 1] for n in range(3))

        @block.sync
        def _(sp):
            sp.dma_start(cm[:], w["L1_attn_C_mat"]).then_inc(w_in, 16)
            sp.dma_start(dv[:], w["L1_attn_D_vec"].to_broadcast([P, D])).then_inc(w_in, 16)
            with sp.Fori(0, NG // DEPTH) as i:
                for r in range(DEPTH):
                    sp.wait_ge(o_out[r], 16 * i + 16)
                    for dst, v in zip((xg, ng, gg), tv):
                        sp.dma_start(dst[r][:], v[:, bass.ds(GT * (DEPTH * i + r), GT), :]).then_inc(x_in[r], 16)

        @block.gpsimd
        def _(pool):
            for r in range(DEPTH):
                pool.sem_inc(o_out[r], 16)
            nc.gpsimd.memset(qz[:, 0:1], 1.0).then_inc(set_up, 1)
            nc.gpsimd.memset(qz[:, 1:2], 0.0).then_inc(set_up, 1)
            nc.gpsimd.memset(qy[:, 0, 0:1], 0.0).then_inc(set_up, 1)
            nc.gpsimd.memset(qy[:, 0, 1:2], 1.0).then_inc(set_up, 1)
            nc.gpsimd.memset(zc[:, :, 0:1], 0.0).then_inc(set_up, 1)
            nc.gpsimd.memset(yc[:, :, 0:1], 0.0).then_inc(set_up, 1)
            pool.wait_ge(w_in, 32)
            pool.wait_ge(set_up, 6)
            nc.gpsimd.tensor_scalar(cm[PS:2 * PS, :], cm[PS:2 * PS, :], -1.0, None, ALU.mult).then_inc(set_up, 1)
            pool.wait_ge(set_up, 7)
            with pool.Fori(0, NG // DEPTH) as i:
                for r in range(DEPTH):
                    g = DEPTH * i + r
                    pool.wait_ge(x_in[r], 48 * i + 48)
                    nc.gpsimd.tensor_tensor(ng[r][:], ng[r][:], dv[:].unsqueeze(1).to_broadcast([P, GT, D]), ALU.mult
                                            ).then_inc(skip, 1)
                    pool.wait_ge(s_sb, g + 1 + DEPTH)
                    nc.gpsimd.tensor_tensor(ng[r][:], ng[r][:], gg[r][:], ALU.mult).then_inc(sg_sb, 1)

        @block.vector
        def _(dve):
            stt = nc.vector.scalar_tensor_tensor
            dve.wait_ge(set_up, 6)
            o = Order(dve, scan_o)
            o.link(nc.vector.tensor_copy(z[:], Yb[:, :, 0]))
            o.link(nc.vector.tensor_scalar(Yb[:, :, 0], z[:], step, None, ALU.mult))

            def powers(i):
                a, c = qy[:, bass.ds(i, 1), :], qy[:, bass.ds(i + 1, 1), :]
                a, c = (v.rearrange("p o q -> p (o q)") for v in (a, c))
                return (lambda: nc.vector.tensor_scalar(qt[:], a, m12, None, ALU.mult),
                        lambda: stt(out=qz[:], in0=qz[:], scalar=m11, in1=qt[:], op0=ALU.mult, op1=ALU.add),
                        lambda: stt(out=c, in0=qz[:], scalar=step, in1=a, op0=ALU.mult, op1=ALU.add))

            for op in powers(0):
                o.link(op())
            n0 = o.n
            with dve.Fori(1, BLK) as i:
                oi = Order(dve, scan_o, n0 + 6 * (i - 1))
                was, now = (Yb[:, :, bass.ds(i - 1, 1)].rearrange("p n o -> p (n o)"),
                            Yb[:, :, bass.ds(i, 1)].rearrange("p n o -> p (n o)"))
                power_t, power_z, power_y = powers(i)
                oi.did(stt(out=t[:], in0=was, scalar=m12, in1=now, op0=ALU.mult, op1=ALU.add))
                oi.link(power_t())
                oi.did(stt(out=z[:], in0=z[:], scalar=m11, in1=t[:], op0=ALU.mult, op1=ALU.add))
                oi.link(power_z())
                oi.did(stt(out=now, in0=z[:], scalar=step, in1=was, op0=ALU.mult, op1=ALU.add))
                oi.link(power_y())
            n0 += 6 * (BLK - 1)
            zb = z[:].rearrange("p (b k) -> p b k", k=NBLK)

            def col(v, k):
                return v[:, :, bass.ds(k, 1)].rearrange("p b o -> p (b o)")

            ends = Yc[:, :, :, BLK - 1]
            with dve.Fori(0, NBLK - 1) as k:
                ok = Order(dve, scan_o, n0 + 4 * k)
                ok.did(stt(out=t1[:], in0=col(zc, k), scalar=qz[:, 0:1], in1=col(zb, k), op0=ALU.mult, op1=ALU.add))
                ok.link(stt(out=t2[:], in0=col(zc, k), scalar=qy[:, BLK, 0:1], in1=col(ends, k),
                            op0=ALU.mult, op1=ALU.add))
                ok.did(stt(out=col(zc, k + 1), in0=col(yc, k), scalar=qz[:, 1:2], in1=t1[:],
                           op0=ALU.mult, op1=ALU.add))
                ok.link(stt(out=col(yc, k + 1), in0=col(yc, k), scalar=qy[:, BLK, 1:2], in1=t2[:],
                            op0=ALU.mult, op1=ALU.add))
            n0 += 4 * (NBLK - 1)
            zcf, ycf = (v[:].rearrange("p b k -> p (b k)") for v in (zc, yc))
            with dve.Fori(0, BLK) as i:
                oi = Order(dve, scan_o, n0 + 3 * i)
                now = Yb[:, :, bass.ds(i, 1)].rearrange("p n o -> p (n o)")
                oi.link(nc.vector.tensor_copy(q2[:], qy[:, bass.ds(i + 1, 1), :].rearrange("p o q -> p (o q)")))
                oi.link(stt(out=t[:], in0=zcf, scalar=q2[:, 0:1], in1=now, op0=ALU.mult, op1=ALU.add))
                oi.link(stt(out=now, in0=ycf, scalar=q2[:, 1:2], in1=t[:], op0=ALU.mult, op1=ALU.add))
            dve.sem_inc(scanned, 1)
            with dve.Fori(0, NG // DEPTH) as i:
                for r in range(DEPTH):
                    g = DEPTH * i + r
                    dve.wait_ge(skip, g + 1)
                    dve.wait_ge(c_ps, g + 1 + DEPTH)
                    for u in range(2):
                        last = nc.vector.tensor_tensor(
                            ng[r][:, 2 * u:2 * u + 2, :].rearrange("p t n -> p (t n)"), ps[2 * r + u][:],
                            ng[r][:, 2 * u:2 * u + 2, :].rearrange("p t n -> p (t n)"), ALU.add)
                    last.then_inc(s_sb, 1)
                    dve.wait_ge(sg_sb, g + 1)
                    nc.vector.tensor_tensor(ng[r][:], ng[r][:], xg[r][:], ALU.add).then_inc(o_sb, 1)

        @block.scalar
        def _(act):
            AHEAD = 2

            def copy(g, r):
                act.wait_ge(c_ps, g + 1)
                at = Y[:].rearrange("p b t -> p (b t)")
                nc.scalar.copy(yg[r][:], at[:, GN * g:GN * (g + 1)] if isinstance(g, int)
                               else at[:, bass.ds(GN * g, GN)]).then_inc(yg_sb, 1)

            def groups(i, last=False):
                for r in range(DEPTH):
                    g = DEPTH * i + r
                    if not last or r + AHEAD < DEPTH:
                        copy(g + AHEAD, (r + AHEAD) % DEPTH)
                    act.wait_ge(o_sb, g + 1)
                    act.dma_start(tv[3][:, GT * g:GT * (g + 1), :] if isinstance(g, int)
                                  else tv[3][:, bass.ds(GT * g, GT), :], ng[r][:]).then_inc(o_out[r], 16)

            act.wait_ge(scanned, 1)
            for g in range(AHEAD):
                copy(g, g)
            with act.Fori(0, NG // DEPTH - 1) as i:
                groups(i)
            groups(NG // DEPTH - 1, last=True)
            for r in range(DEPTH):
                act.wait_ge(o_out[r], 16 * (NG // DEPTH) + 16)

        @block.tensor
        def _(pe):
            pe.sem_inc(c_ps, DEPTH)
            pe.sem_inc(s_sb, DEPTH)
            pe.wait_ge(set_up, 7)
            with pe.Fori(0, NG // DEPTH) as i:
                for r in range(DEPTH):
                    g = DEPTH * i + r
                    pe.wait_ge(yg_sb, g + 1)
                    pe.wait_ge(s_sb, g + 1)
                    for q in range(GT):
                        last = nc.tensor.matmul(ps[2 * r + q // 2][:, (q % 2) * D:(q % 2 + 1) * D],
                                                yg[r][:, q * P:(q + 1) * P], cm[:], start=True, stop=True)
                    last.then_inc(c_ps, 1)


def build(nc, a, out):
    def dram(name, shape):
        return nc.dram_tensor(name, shape, F32).ap()

    xn_d = dram("xn_d", (N, D))
    xnT_d = dram("xnT_d", (KD, P, N))
    s0_d = dram("s0_d", (N, D))
    acc_d = dram("acc_d", (N, D))
    left_d = dram("left_d", (2, P))
    x1_d = dram("x1_d", (N, D))
    xn1_d = dram("xn1_d", (N, D))
    g_d = dram("g_d", (N, D))

    with ExitStack() as ctx:
        ps = [ctx.enter_context(nc.psum_tensor(f"ps{i}", [P, 512], F32)) for i in range(8)]
        ident = ctx.enter_context(nc.sbuf_tensor("ident", [P, P], F32))
        with ExitStack() as mem:
            ident_o = ctx.enter_context(nc.semaphore("ident_o"))
            block = mem.enter_context(nc.Block())

            @block.gpsimd
            def _(pool):
                nc.gpsimd.memset(ident[:], 0.0).then_inc(ident_o, 1)
                pool.wait_ge(ident_o, 1)
                nc.gpsimd.affine_select(out=ident[:], in_=ident[:], compare_op=ALU.not_equal, fill=1.0, base=0,
                                        pattern=[[-1, P]], channel_multiplier=1).then_inc(ident_o, 1)
                pool.wait_ge(ident_o, 2)

        with ExitStack() as mem:
            idxT = mem.enter_context(nc.sbuf_tensor("idxT", [P, P, 2], U32))
            gateT = mem.enter_context(nc.sbuf_tensor("gateT", [P, P, 2], F32))
            idxL = mem.enter_context(nc.sbuf_tensor("idxL", [B, NE], U32))
            gateL = mem.enter_context(nc.sbuf_tensor("gateL", [B, NE], F32))
            route_phase(nc, ctx, ps, a["L0_attn_hidden_states"], xn_d, xnT_d, acc_d, left_d,
                        a["L0_ffn_router_w"], ident, idxT, gateT, idxL, gateL)
            experts_phase(nc, ctx, ps, xn_d, acc_d, a["L0_ffn_w1"], a["L0_ffn_b1"], a["L0_ffn_w2"], a["L0_ffn_b2"],
                          ident, idxT, gateT, idxL, gateL)
        recurrence_phase(nc, ctx, ps, xnT_d, s0_d, ident, a)
        with ExitStack() as mem:
            Y = mem.enter_context(nc.sbuf_tensor("Y", [P, B, T], F32))
            coef = mem.enter_context(nc.sbuf_tensor("coef", [P, 4], F32))
            layer1_phase(nc, ctx, ps, a["L0_attn_hidden_states"], s0_d, acc_d, x1_d, xn1_d, g_d, ident, a, Y, coef)
            out_phase(nc, ctx, ps, x1_d, xn1_d, g_d, out, a, Y, coef)


INS = {
    "L0_attn_hidden_states": lambda a: a.reshape(N, D),
    "L0_ffn_router_w": lambda a: a.T.reshape(KD, P, NE).transpose(1, 0, 2),
    "L0_attn_x_proj_mu": lambda a: a.reshape(KD, P).T,
    "L0_attn_xl_w1": lambda a: a.T.reshape(KD, P, RANK).transpose(1, 0, 2),
    "L0_attn_xl_w2": lambda a: a.T,
    "L0_attn_xl_b2": lambda a: a.reshape(NMU * RANK, 1),
    "L0_attn_x_out_w": lambda a: a.T,
    "L0_attn_x_bias": lambda a: a.reshape(NMU, KD, P).transpose(2, 0, 1),
    "L0_attn_r_w": lambda a: a.T.reshape(KD, P, KW).transpose(1, 0, 2),
    "L0_attn_w_w1": lambda a: a.T.reshape(KD, P, GATE).transpose(1, 0, 2),
    "L0_attn_w_w2": lambda a: a.T,
    "L0_attn_w_b": lambda a: a.reshape(KW, 1),
    "L0_attn_k_w": lambda a: a.T.reshape(KD, P, KW).transpose(1, 0, 2),
    "L0_attn_v_w": lambda a: a.T.reshape(KD, P, VW).transpose(1, 0, 2),
    "L0_attn_g_w": lambda a: a.T.reshape(KD, P, VW).transpose(1, 0, 2),
    "L0_attn_bonus": lambda a: a.reshape(KW, 1),
    "L0_attn_gn_weight": lambda a: a.reshape(1, VW),
    "L0_attn_gn_bias": lambda a: a.reshape(1, VW),
    "L0_attn_o_w": lambda a: a.T.reshape(KD, P, D).transpose(1, 0, 2),
    "L0_ffn_w1": lambda a: a.reshape(NE, KD, P, HID).transpose(0, 2, 1, 3),
    "L0_ffn_b1": lambda a: a.reshape(NE, HC, P).transpose(0, 2, 1),
    "L0_ffn_w2": lambda a: a.reshape(NE, HC, P, D).transpose(0, 2, 1, 3),
    "L0_ffn_b2": lambda a: a.reshape(NE, 1, D),
    "L1_attn_steps_raw": lambda a: a.reshape(PS, 1),
    "L1_attn_G_raw": lambda a: a.reshape(PS, 1),
    "L1_attn_A_raw": lambda a: a.reshape(PS, 1),
    "L1_attn_B_mat": lambda a: a.transpose(1, 2, 0).reshape(KD, P, 2 * PS).transpose(1, 0, 2),
    "L1_attn_C_mat": lambda a: a.transpose(2, 1, 0).reshape(2 * PS, D),
    "L1_attn_D_vec": lambda a: a.reshape(1, D),
    "L1_ffn_w1": lambda a: a.reshape(NE, KD, P, FF).transpose(0, 2, 1, 3),
    "L1_ffn_w3": lambda a: a.reshape(NE, KD, P, FF).transpose(0, 2, 1, 3),
    "L1_ffn_w2": lambda a: a,
}


def kernel(**inputs):
    import numpy as np
    import concourse.bacc as bacc
    from concourse.bass_utils import run_bass_kernel_spmd

    nc = bacc.Bacc("TRN2", target_bir_lowering=False, num_devices=1)
    arrays, args = {}, {}
    for name, lay in INS.items():
        a = np.ascontiguousarray(lay(np.asarray(inputs[name])))
        arrays[f"in_{name}"] = a
        args[name] = nc.dram_tensor(f"in_{name}", a.shape, mybir.dt.from_np(a.dtype), kind="ExternalInput").ap()
    out = nc.dram_tensor("out_0", (N, D), F32, kind="ExternalOutput").ap()
    build(nc, args, out)
    r = run_bass_kernel_spmd(nc, [arrays], core_ids=[0])
    return r.results[0]["out_0"].reshape(B, T, D)
```
